# Optimizing a Trainium2 kernel written in Bass

```python
import numpy as np
import jax
import jax.numpy as jnp

def _softmax(x, axis=-1):
    return jax.nn.softmax(x, axis=axis)

def _gelu(x):
    return jax.nn.gelu(x, approximate=True)

def _silu(x):
    return jax.nn.silu(x)

def _sigmoid(x):
    return jax.nn.sigmoid(x)

def _layernorm(x, axis=-1, eps=1e-05):
    m = jnp.mean(x, axis=axis, keepdims=True)
    v = jnp.var(x, axis=axis, keepdims=True)
    return (x - m) / jnp.sqrt(v + eps)

def _scatter_add(tgt, idx, src, axis=0):
    return tgt.at[idx].add(src)

def _segment_sum(src, seg, n):
    return jax.ops.segment_sum(src, seg, n)
kernel_name = 'mk_xattn_seq_d2_seqx_r8_3f70e7'

def setup_inputs(seed: int=0):
    np.random.seed(seed)
    _w = jnp.asarray

    def _rec_inputs():
        import jax
        import jax.numpy as jnp
        _rk = jax.random.key(seed)
        x = -0.000125 + 0.9999 * jax.random.normal(jax.random.fold_in(_rk, 1), (32, 64, 256), jnp.float32)
        _lenS = 64 - jax.random.randint(jax.random.fold_in(_rk, 7), (32,), 0, max(1, 64 // 4) + 1, jnp.int32)
        _lenS2 = 64 - jax.random.randint(jax.random.fold_in(_rk, 8), (32,), 0, max(1, 64 // 4) + 1, jnp.int32)
        _ctx_1024P = jax.random.normal(jax.random.fold_in(_rk, 11), (32, 16, 128), jnp.float32)
        _ctx_1024c = jax.random.dirichlet(jax.random.fold_in(_rk, 511), 0.3 * jnp.ones((16,), jnp.float32), (32, 64))
        _ctx_1024t = jnp.einsum('bsk,bkd->bsd', _ctx_1024c, _ctx_1024P)
        _ctx_1024t = _ctx_1024t * jax.lax.rsqrt(jnp.mean(jnp.square(_ctx_1024t)) + 1e-12) * 0.953939
        ctx_1024 = 4.13588e-05 + 0.999923 * (_ctx_1024t + 0.3 * jax.random.normal(jax.random.fold_in(_rk, 611), (32, 64, 128), jnp.float32))
        pos_1xS = jnp.broadcast_to(jnp.arange(64, dtype=jnp.int32), (1, 64))
        _validS = jnp.arange(64)[None, :] < _lenS[:, None]
        _validS2 = jnp.arange(64)[None, :] < _lenS2[:, None]
        _causal = jnp.tril(jnp.ones((64, 64), dtype=bool))
        mask_BxS_ik0 = jnp.where(jnp.broadcast_to(_validS[:, :], (32, 64)), 0, 1).astype(jnp.int32)
        return (x, ctx_1024, pos_1xS, mask_BxS_ik0)
    x, ctx_1024, pos_1xS, mask_BxS_ik0 = _rec_inputs()

    def _L0_xattn_setup():
        import jax, jax.numpy as jnp
        import numpy as np
        EPS = 1e-06

        def _rmsnorm(x, w):
            var = jnp.mean(jnp.square(x), axis=-1, keepdims=True)
            return x * jax.lax.rsqrt(var + EPS) * w
        key = jax.random.key(seed)
        ks = jax.random.split(key, 6)
        B, N, M = (4, 512, 256)
        d_model, memory_dim = (256, 128)
        hidden_states = jax.random.normal(ks[0], (B, N, d_model), dtype=jnp.float32)
        memory = jax.random.normal(ks[1], (B, M, memory_dim), dtype=jnp.float32)
        W_mem = jax.random.normal(ks[2], (d_model, memory_dim), dtype=jnp.float32) / np.sqrt(memory_dim)
        W_gate = jax.random.normal(ks[3], (d_model, 2 * d_model), dtype=jnp.float32) / np.sqrt(2 * d_model)
        b_gate = jax.random.normal(ks[4], (d_model,), dtype=jnp.float32) * 0.01
        norm_w = jnp.ones((d_model,), dtype=jnp.float32)
        return {'hidden_states': hidden_states, 'memory': memory, 'W_mem': W_mem, 'W_gate': W_gate, 'b_gate': b_gate, 'norm_w': norm_w}
    _L0_xattn_all = _L0_xattn_setup()
    _L0_xattn_in = {k: v for k, v in _L0_xattn_all.items() if k in ('W_mem', 'W_gate', 'b_gate', 'norm_w')}
    del _L0_xattn_all

    def _L1_xattn_setup():
        import jax, jax.numpy as jnp
        import numpy as np
        H = 256
        NH = 16
        HD = H // NH
        CH = 128
        CC = 128
        CHD = CC // NH
        I = 688
        B = 2
        L = 256
        LE = 128
        EPS = 1e-06

        def rms_norm(x, w):
            xf = x.astype(jnp.float32)
            var = jnp.mean(xf * xf, axis=-1, keepdims=True)
            return (w * (xf * jax.lax.rsqrt(var + EPS))).astype(x.dtype)

        def expert_mask(tt):
            vm = jnp.zeros(tt.shape, dtype=bool)
            vm = vm.at[:, :-1].set((tt[:, :-1] == 1) & (tt[:, 1:] == 1))
            return vm

        def rotate_half(x):
            d = x.shape[-1] // 2
            return jnp.concatenate([-x[..., d:], x[..., :d]], axis=-1)

        def apply_rotary(q, k, position_ids, seq_len):
            inv = 1.0 / 10000.0 ** (jnp.arange(0, HD, 2, dtype=jnp.float32) / HD)
            t = jnp.arange(seq_len, dtype=jnp.float32)
            freqs = jnp.outer(t, inv)
            emb = jnp.concatenate([freqs, freqs], axis=-1)
            cos = jnp.cos(emb)[position_ids][:, None].astype(q.dtype)
            sin = jnp.sin(emb)[position_ids][:, None].astype(q.dtype)
            return (q * cos + rotate_half(q) * sin, k * cos + rotate_half(k) * sin)

        def sdpa(q, k, v, causal):
            scale = 1.0 / np.sqrt(q.shape[-1])
            scores = jnp.einsum('bhqd,bhkd->bhqk', q * scale, k)
            if causal:
                mask = jnp.tril(jnp.ones((q.shape[-2], k.shape[-2]), dtype=bool))
                scores = jnp.where(mask, scores, jnp.finfo(jnp.float32).min)
            p = jax.nn.softmax(scores.astype(jnp.float32), axis=-1).astype(q.dtype)
            return jnp.einsum('bhqk,bhkd->bhqd', p, v)

        def heads(x, nh, hd):
            b, l, _ = x.shape
            return x.reshape(b, l, nh, hd).transpose(0, 2, 1, 3)
        key = jax.random.key(seed)
        ks = jax.random.split(key, 20)
        s = 0.02
        f32 = jnp.float32
        return {'hidden_states': jax.random.normal(ks[0], (B, L, H), f32), 'encoder_outputs': jax.random.normal(ks[1], (B, LE, CH), f32), 'token_type_ids': jax.random.randint(ks[2], (B, L), 0, 2, jnp.int32), 'position_ids': jnp.arange(L, dtype=jnp.int32)[None, :], 'ln_in_w': jnp.ones((H,), f32), 'ln_post_attn_w': jnp.ones((H,), f32), 'ln_post_cross_w': jnp.ones((H,), f32), 'v_qkv': jax.random.normal(ks[3], (H, 3 * H), f32) * s, 'l_qkv': jax.random.normal(ks[4], (H, 3 * H), f32) * s, 'v_dense': jax.random.normal(ks[5], (H, H), f32) * s, 'l_dense': jax.random.normal(ks[6], (H, H), f32) * s, 'cq_w': jax.random.normal(ks[7], (H, CC), f32) * s, 'ckv_w': jax.random.normal(ks[8], (CH, 2 * CC), f32) * s, 'cdense_w': jax.random.normal(ks[9], (CC, H), f32) * s, 'v_gate': jax.random.normal(ks[10], (H, I), f32) * s, 'v_up': jax.random.normal(ks[11], (H, I), f32) * s, 'v_down': jax.random.normal(ks[12], (I, H), f32) * s, 'l_gate': jax.random.normal(ks[13], (H, I), f32) * s, 'l_up': jax.random.normal(ks[14], (H, I), f32) * s, 'l_down': jax.random.normal(ks[15], (I, H), f32) * s}
    _L1_xattn_all = _L1_xattn_setup()
    _L1_xattn_in = {k: v for k, v in _L1_xattn_all.items() if k in ('ln_in_w', 'ln_post_attn_w', 'ln_post_cross_w', 'v_qkv', 'l_qkv', 'v_dense', 'l_dense', 'cq_w', 'ckv_w', 'cdense_w', 'v_gate', 'v_up', 'v_down', 'l_gate', 'l_up', 'l_down')}
    del _L1_xattn_all
    return {'x': x, 'ctx_1024': ctx_1024, 'pos_1xS': pos_1xS, 'mask_BxS_ik0': mask_BxS_ik0, 'L0_xattn_W_mem': _L0_xattn_in['W_mem'], 'L0_xattn_W_gate': _L0_xattn_in['W_gate'], 'L0_xattn_b_gate': _L0_xattn_in['b_gate'], 'L0_xattn_norm_w': _L0_xattn_in['norm_w'], 'L1_xattn_ln_in_w': _L1_xattn_in['ln_in_w'], 'L1_xattn_ln_post_attn_w': _L1_xattn_in['ln_post_attn_w'], 'L1_xattn_ln_post_cross_w': _L1_xattn_in['ln_post_cross_w'], 'L1_xattn_v_qkv': _L1_xattn_in['v_qkv'], 'L1_xattn_l_qkv': _L1_xattn_in['l_qkv'], 'L1_xattn_v_dense': _L1_xattn_in['v_dense'], 'L1_xattn_l_dense': _L1_xattn_in['l_dense'], 'L1_xattn_cq_w': _L1_xattn_in['cq_w'], 'L1_xattn_ckv_w': _L1_xattn_in['ckv_w'], 'L1_xattn_cdense_w': _L1_xattn_in['cdense_w'], 'L1_xattn_v_gate': _L1_xattn_in['v_gate'], 'L1_xattn_v_up': _L1_xattn_in['v_up'], 'L1_xattn_v_down': _L1_xattn_in['v_down'], 'L1_xattn_l_gate': _L1_xattn_in['l_gate'], 'L1_xattn_l_up': _L1_xattn_in['l_up'], 'L1_xattn_l_down': _L1_xattn_in['l_down']}

def reference(x, ctx_1024, pos_1xS, mask_BxS_ik0, L0_xattn_W_mem, L0_xattn_W_gate, L0_xattn_b_gate, L0_xattn_norm_w, L1_xattn_ln_in_w, L1_xattn_ln_post_attn_w, L1_xattn_ln_post_cross_w, L1_xattn_v_qkv, L1_xattn_l_qkv, L1_xattn_v_dense, L1_xattn_l_dense, L1_xattn_cq_w, L1_xattn_ckv_w, L1_xattn_cdense_w, L1_xattn_v_gate, L1_xattn_v_up, L1_xattn_v_down, L1_xattn_l_gate, L1_xattn_l_up, L1_xattn_l_down):
    import jax
    import jax.numpy as jnp

    def _L0_xattn_ref(hidden_states, memory, W_mem, W_gate, b_gate, norm_w):
        import jax, jax.numpy as jnp
        import numpy as np
        EPS = 1e-06

        def _rmsnorm(x, w):
            var = jnp.mean(jnp.square(x), axis=-1, keepdims=True)
            return x * jax.lax.rsqrt(var + EPS) * w
        D = hidden_states.shape[-1]
        memory_proj = jnp.einsum('bme,de->bmd', memory, W_mem)
        scores = jnp.einsum('bnd,bmd->bnm', hidden_states, memory_proj) / jnp.sqrt(jnp.float32(D))
        attn = jax.nn.softmax(scores, axis=-1)
        memory_context = jnp.einsum('bnm,bmd->bnd', attn, memory_proj)
        gate_input = jnp.concatenate([hidden_states, memory_context], axis=-1)
        gate = jax.nn.sigmoid(jnp.einsum('bnf,df->bnd', gate_input, W_gate) + b_gate)
        fused = hidden_states + gate * memory_context
        return _rmsnorm(fused, norm_w)

    def _L1_xattn_ref(hidden_states, encoder_outputs, token_type_ids, position_ids, ln_in_w, ln_post_attn_w, ln_post_cross_w, v_qkv, l_qkv, v_dense, l_dense, cq_w, ckv_w, cdense_w, v_gate, v_up, v_down, l_gate, l_up, l_down):
        import jax, jax.numpy as jnp
        import numpy as np
        H = 256
        NH = 16
        HD = H // NH
        CH = 128
        CC = 128
        CHD = CC // NH
        I = 688
        B = 2
        L = 256
        LE = 128
        EPS = 1e-06

        def rms_norm(x, w):
            xf = x.astype(jnp.float32)
            var = jnp.mean(xf * xf, axis=-1, keepdims=True)
            return (w * (xf * jax.lax.rsqrt(var + EPS))).astype(x.dtype)

        def expert_mask(tt):
            vm = jnp.zeros(tt.shape, dtype=bool)
            vm = vm.at[:, :-1].set((tt[:, :-1] == 1) & (tt[:, 1:] == 1))
            return vm

        def rotate_half(x):
            d = x.shape[-1] // 2
            return jnp.concatenate([-x[..., d:], x[..., :d]], axis=-1)

        def apply_rotary(q, k, position_ids, seq_len):
            inv = 1.0 / 10000.0 ** (jnp.arange(0, HD, 2, dtype=jnp.float32) / HD)
            t = jnp.arange(seq_len, dtype=jnp.float32)
            freqs = jnp.outer(t, inv)
            emb = jnp.concatenate([freqs, freqs], axis=-1)
            cos = jnp.cos(emb)[position_ids][:, None].astype(q.dtype)
            sin = jnp.sin(emb)[position_ids][:, None].astype(q.dtype)
            return (q * cos + rotate_half(q) * sin, k * cos + rotate_half(k) * sin)

        def sdpa(q, k, v, causal):
            scale = 1.0 / np.sqrt(q.shape[-1])
            scores = jnp.einsum('bhqd,bhkd->bhqk', q * scale, k)
            if causal:
                mask = jnp.tril(jnp.ones((q.shape[-2], k.shape[-2]), dtype=bool))
                scores = jnp.where(mask, scores, jnp.finfo(jnp.float32).min)
            p = jax.nn.softmax(scores.astype(jnp.float32), axis=-1).astype(q.dtype)
            return jnp.einsum('bhqk,bhkd->bhqd', p, v)

        def heads(x, nh, hd):
            b, l, _ = x.shape
            return x.reshape(b, l, nh, hd).transpose(0, 2, 1, 3)
        b, l, _ = hidden_states.shape
        vm = expert_mask(token_type_ids)[..., None]
        residual = hidden_states
        x = rms_norm(hidden_states, ln_in_w)
        mixed = jnp.where(vm, x @ v_qkv, x @ l_qkv)
        q, k, v = jnp.split(mixed, 3, axis=-1)
        q, k, v = (heads(q, NH, HD), heads(k, NH, HD), heads(v, NH, HD))
        q, k = apply_rotary(q, k, position_ids, l)
        ctx = sdpa(q, k, v, causal=True)
        ctx = ctx.transpose(0, 2, 1, 3).reshape(b, l, H)
        attn_out = jnp.where(vm, ctx @ v_dense, ctx @ l_dense)
        hidden_states = residual + attn_out
        ci = rms_norm(hidden_states, ln_post_cross_w)
        cq = heads(ci @ cq_w, NH, CHD)
        ckv = encoder_outputs @ ckv_w
        ck, cv = jnp.split(ckv, 2, axis=-1)
        ck, cv = (heads(ck, NH, CHD), heads(cv, NH, CHD))
        cctx = sdpa(cq, ck, cv, causal=False)
        cctx = cctx.transpose(0, 2, 1, 3).reshape(b, l, CC)
        hidden_states = hidden_states + cctx @ cdense_w
        mi = rms_norm(hidden_states, ln_post_attn_w)
        v_out = jax.nn.silu(mi @ v_gate) * (mi @ v_up) @ v_down
        l_out = jax.nn.silu(mi @ l_gate) * (mi @ l_up) @ l_down
        hidden_states = hidden_states + jnp.where(vm, v_out, l_out)
        return hidden_states
    x = _L0_xattn_ref(x, ctx_1024, L0_xattn_W_mem, L0_xattn_W_gate, L0_xattn_b_gate, L0_xattn_norm_w)
    x = _L1_xattn_ref(x, ctx_1024, mask_BxS_ik0, pos_1xS, L1_xattn_ln_in_w, L1_xattn_ln_post_attn_w, L1_xattn_ln_post_cross_w, L1_xattn_v_qkv, L1_xattn_l_qkv, L1_xattn_v_dense, L1_xattn_l_dense, L1_xattn_cq_w, L1_xattn_ckv_w, L1_xattn_cdense_w, L1_xattn_v_gate, L1_xattn_v_up, L1_xattn_v_down, L1_xattn_l_gate, L1_xattn_l_up, L1_xattn_l_down)
    return x

_drawn_inputs = setup_inputs


def setup_inputs(seed=0):
    import zlib

    import numpy as np

    out = dict(_drawn_inputs(seed))
    spreads = {'L0_xattn_norm_w': (1.0, 0.2),
     'L1_xattn_ln_in_w': (1.0, 0.6),
     'L1_xattn_ln_post_attn_w': (1.0, 0.6),
     'L1_xattn_ln_post_cross_w': (1.0, 0.6)}
    factors = {'L0_xattn_b_gate': 8.0,
     'L1_xattn_v_qkv': 8.0,
     'L1_xattn_v_dense': 6.429,
     'L1_xattn_cq_w': 64.0,
     'L1_xattn_v_gate': 5.864,
     'L1_xattn_v_up': 5.822,
     'L1_xattn_v_down': 5.832,
     'L1_xattn_l_dense': 4.093,
     'L1_xattn_ckv_w': 7.6,
     'L1_xattn_cdense_w': 7.603,
     'L1_xattn_l_gate': 5.421,
     'L1_xattn_l_up': 5.295,
     'L1_xattn_l_down': 5.321}
    for name, (base, spread) in spreads.items():
        noise = np.random.default_rng([zlib.crc32(name.encode()), seed]).standard_normal(out[name].shape)
        drawn = base * np.exp(spread * noise) if base else spread * noise
        out[name] = jnp.asarray(drawn.astype(out[name].dtype))
    for name, factor in factors.items():
        out[name] = (out[name] * factor).astype(out[name].dtype)
    return out
```

```python
from contextlib import ExitStack

import concourse.bass as bass
from concourse import mybir

F32 = mybir.dt.float32
F32R = mybir.dt.float32r
I32 = mybir.dt.int32
ALU = mybir.AluOpType
ACT = mybir.ActivationFunctionType
AX_X = mybir.AxisListType.X

P = 128
B, S, D, C = 32, 64, 256, 128
TOK = 256
NT = TOK // P
GROUPS = B * S // TOK
KD = D // P
HEADS = 16
HD, CHD = D // HEADS, C // HEADS
PAIRS = HEADS // 2
INNER = 688
FULL = INNER // P
LEFT = INNER - FULL * P
MT = 2 * FULL + 1
EPS = 1e-6
MASKED = -1e30
GU = 4 * INNER
VB = 2 * 2 * HD + 2
CVB = 2 * 2 * CHD + 2
STAGE = MT * TOK

SIZES = [("mem", KD * C), ("gate_x", KD * D), ("mem_t", D), ("gate_m", D), ("ckv", 2 * C), ("cq", KD * C),
         ("qkv", KD * 6 * D), ("dense", KD * 2 * D), ("cdense", D),
         ("gu", KD * GU), ("down", 2 * FULL * D), ("down_left", 2 * D)]
AT, COLS = {}, 0
for _name, _size in SIZES:
    AT[_name] = COLS
    COLS += _size


def build_program(nc, a, out):
    with ExitStack() as ctx:
        def sb(name, shape, dt=F32):
            return ctx.enter_context(nc.sbuf_tensor(name, shape, dt))

        def sem(name):
            return ctx.enter_context(nc.semaphore(name))

        def sems(name, n):
            return [sem(f"{name}{k}") for k in range(n)]

        w_hi, w_lo = sb("w_hi", [P, COLS], F32R), sb("w_lo", [P, COLS], F32R)
        with nc.sbuf_tensor("stage", [P, 2, STAGE], F32) as stage:
            pass
        h_hi, h_lo = sb("h_hi", [P, MT, TOK], F32R), sb("h_lo", [P, MT, TOK], F32R)
        xc = sb("xc", [P, KD + 1, TOK])
        xc_hi, xc_lo = sb("xc_hi", [P, KD + 1, TOK], F32R), sb("xc_lo", [P, KD + 1, TOK], F32R)
        x_tok = sb("x_tok", [P, NT, D])
        ctx_tok = sb("ctx_tok", [P, 2, C])
        mask_in = sb("mask_in", [P, 2, NT], I32)
        mask_is1 = sb("mask_is1", [P, 2, NT])
        pick = sb("pick", [P, 2, NT])
        pick_r = sb("pick_r", [P, 2, NT])
        pick_b = sb("pick_b", [P, 2, NT])
        am_hi, am_lo = sb("am_hi", [P, NT, P], F32R), sb("am_lo", [P, NT, P], F32R)
        res = sb("res", [P, NT, D])
        t_hi, t_lo = sb("t_hi", [P, KD, TOK], F32R), sb("t_lo", [P, KD, TOK], F32R)
        mi_hi, mi_lo = sb("mi_hi", [P, KD, TOK], F32R), sb("mi_lo", [P, KD, TOK], F32R)
        sm = sb("sm", [P, 4, 512])
        qkv = sb("qkv", [P, NT, 3 * D])
        ra, rb = sb("ra", [P, NT, 512]), sb("rb", [P, NT, 512])
        tok = sb("tok", [P, NT, D])
        qblk = sb("qblk", [P, 2, 2 * NT, 2, S])
        ck_t = sb("ck_t", [P, TOK])
        vblk = sb("vblk", [P, NT, PAIRS, VB])
        cvblk = sb("cvblk", [P, NT, PAIRS, CVB])
        with (nc.sbuf_tensor("pos_i", [S, S], I32) as pos_i, nc.sbuf_tensor("pos_f", [S, S], F32) as pos_f,
              nc.sbuf_tensor("pos_neg", [S, S], F32) as pos_neg, nc.sbuf_tensor("onehot", [S, 2, S], F32) as onehot,
              nc.sbuf_tensor("trig_tab", [S, 2 * HD], F32) as trig_tab, nc.sbuf_tensor("b_row", [1, D], F32) as b_row,
              nc.sbuf_tensor("ones_row", [1, P], F32) as ones_row):
            pass
        hb = sb("hb", [P, 2, TOK])
        res_b = sb("res_b", [P, NT, D])
        top = sb("top", [P, 32])
        inv = sb("inv", [P, 16, 2])
        sumsq, var, rms = sb("sumsq", [P, 4, NT]), sb("var", [P, 4, NT]), sb("rms", [P, 4, NT])
        minus_half = sb("minus_half", [P, NT])
        ident = sb("ident", [P, P])
        causal = sb("causal", [P, S])
        consts = sb("consts", [P, 8])
        norm0 = sb("norm0", [P, D])
        ln = sb("ln", [P, 3, KD])
        trig = sb("trig", [P, 2, HD])
        b_hi, b_lo, ones_r = sb("b_hi", [1, D], F32R), sb("b_lo", [1, D], F32R), sb("ones_r", [1, P], F32R)
        ps = ctx.enter_context(nc.psum_tensor("ps", [P, 8, 512], F32))
        M0 = 6

        consts_in, raw_in = sem("consts_in"), sems("raw_in", 8)
        raw_hi, raw_lo = sem("raw_hi"), sem("raw_lo")
        gm_mm, gm_hi, gm_lo = sem("gm_mm"), sem("gm_hi"), sem("gm_lo")
        zeroed, filled, bias_hi, bias_lo = sem("zeroed"), sem("filled"), sem("bias_hi"), sem("bias_lo")
        pos_done, trig_mm, trig_ready = sem("pos_done"), sem("trig_mm"), sem("trig_ready")
        xc_in, xtok_in, ctok_in, mask_dma = sem("xc_in"), sem("xtok_in"), sem("ctok_in"), sem("mask_dma")
        is1, pick_v, picks = sem("is1"), sem("pick_v"), sem("picks")
        xc_hi_r, xc_lo_r = sem("xc_hi_r"), sem("xc_lo_r")
        q0_mm, q0_r, kv_mm, kv_r = sem("q0_mm"), sem("q0_r"), sem("kv_mm"), sem("kv_r")
        sc0_mm, top0, low0, exp0, sum0, inv0, p0 = (sem(n) for n in "sc0_mm top0 low0 exp0 sum0 inv0 p0".split())
        p0t_mm, p0t, am_mm, am_hi_r, am_lo_r = (sem(n) for n in "p0t_mm p0t am_mm am_hi_r am_lo_r".split())
        mcz_mm, tanh0, gated, fused = (sem(n) for n in "mcz_mm tanh0 gated fused".split())
        sq_r, var_r, rms_r = sems("sq_r", 4), sems("var_r", 4), sems("rms_r", 4)
        x1_r, tx1_mm, x1_hi, x1_lo = (sem(n) for n in "x1_r tx1_mm x1_hi x1_lo".split())
        pickr_r, qkv_mm, vpart, qkv_r = sem("pickr_r"), sems("qkv_mm", 2), sems("vpart", 2), sems("qkv_r", 2)
        vb_r, rope_c, rope_s, rope_r = (sem(n) for n in "vb_r rope_c rope_s rope_r".split())
        tq_mm, tk_mm, qb_r, kt_r = (sem(n) for n in "tq_mm tk_mm qb_r kt_r".split())
        s_mm = [sems(f"s_mm{k}_", 2) for k in range(2)]
        masked = sems("masked", 2)
        top_r = [sems(f"top_r{k}_", 2) for k in range(2)]
        low_r = [sems(f"low_r{k}_", 2) for k in range(2)]
        exp_r = [sems(f"exp_r{k}_", 2) for k in range(2)]
        pt_mm = [sems(f"pt_mm{k}_", 2) for k in range(2)]
        pt_r = [sems(f"pt_r{k}_", 2) for k in range(2)]
        pv_mm, inv_r, ctx_r, tctx_mm, ctx_hi, ctx_lo = (
            sems(n, 2) for n in "pv_mm inv_r ctx_r tctx_mm ctx_hi ctx_lo".split())
        dense_mm, res_v, x2_r = sem("dense_mm"), sems("res_v", 2), sem("x2_r")
        ci_r, tci_mm, ci_hi, ci_lo = (sem(n) for n in "ci_r tci_mm ci_hi ci_lo".split())
        cq_mm, cq_s, cqb_r = sem("cq_mm"), sem("cq_s"), sem("cqb_r")
        cd_mm, x3_r, resb_r, pickb_r = (sem(n) for n in "cd_mm x3_r resb_r pickb_r".split())
        mi_r, tmi_mm, mi_hi_r, mi_lo_r = (sem(n) for n in "mi_r tmi_mm mi_hi_r mi_lo_r".split())
        gu_mm, th_r, tg_r, h_r, h_hi_r, h_lo_r = (sem(n) for n in "gu_mm th_r tg_r h_r h_hi_r h_lo_r".split())
        down_mm, y_v, y_r, stored = sems("down_mm", 2), sems("y_v", 2), sem("y_r"), sem("stored")

        def wcols(name, at, n):
            return slice(AT[name] + at, AT[name] + at + n)

        chunks = [
            (a["w_first"], P, 2048, [(0, 1024, AT["mem"], 1.0), (1024, 256, AT["ckv"], 1.0),
                                     (1280, 128, AT["cq"], ln[:, 1, 0:1]),
                                     (1408, 128, AT["cq"] + 128, ln[:, 1, 1:2])]),
            (a["w_qkv"][0], P, 6 * D, [(0, 6 * D, AT["qkv"], ln[:, 0, 0:1])]),
            (a["w_qkv"][1], P, 6 * D, [(0, 6 * D, AT["qkv"] + 6 * D, ln[:, 0, 1:2])]),
            (a["w_dense"], P, 5 * D, [(0, 5 * D, AT["dense"], 1.0)]),
            (a["w_gu"][0], P, GU, [(0, GU, AT["gu"], ln[:, 2, 0:1])]),
            (a["w_gu"][1], P, GU, [(0, GU, AT["gu"] + GU, ln[:, 2, 1:2])]),
            (a["w_down"], P, 2 * FULL * D, [(0, 2 * FULL * D, AT["down"], 0.5)]),
            (a["w_down_left"], 2 * LEFT, 2 * D, [(0, 2 * D, AT["down_left"], 0.5)]),
        ]
        raw_mem, raw_gate_m = stage[:, 0, 0:KD * C], stage[:, 0, 1536:2048]

        def before(eng, s, v):
            if not (isinstance(v, int) and v <= 0):
                eng.wait_ge(s, v)

        def f32(ap):
            return ap.bitcast(F32)

        block = ctx.enter_context(nc.Block())

        @block.sync
        def _(sp):
            def load_chunk(n):
                src, rows, cols, _ = chunks[n]
                if n >= 2:
                    sp.wait_ge(raw_lo, n - 1)
                if n == 2:
                    sp.wait_ge(gm_mm, 1)
                sp.dma_start(stage[0:rows, n % 2, 0:cols], src).then_inc(raw_in[n], 16)

            def load_group(g, prev):
                before(sp, sc0_mm, prev)
                before(sp, xc_lo_r, prev)
                sp.dma_start(xc[:, :, :], a["xc"][g]).then_inc(xc_in, 16)
                before(sp, am_mm, prev)
                sp.dma_start(ctx_tok[:, :, :], a["ctx_tok"][g]).then_inc(ctok_in, 16)
                before(sp, is1, prev)
                sp.dma_start(mask_in[:, :, :], a["mask"][g]).then_inc(mask_dma, 16)
                before(sp, fused, prev)
                sp.dma_start(x_tok[:, :, :], a["x_tok"][g]).then_inc(xtok_in, 16)

            def store_group(g, cur):
                sp.wait_ge(y_r, cur + 1)
                sp.dma_start(out[g], res_b[:, :, :]).then_inc(stored, 16)

            sp.dma_start(ln[:, :, :], a["ln"]).then_inc(consts_in, 16)
            load_chunk(0)
            load_group(0, 0)
            sp.dma_start(ident[:, :], a["ident"]).then_inc(consts_in, 16)
            sp.dma_start(consts[:, :], a["consts"]).then_inc(consts_in, 16)
            sp.dma_start(causal[:, :], a["causal"]).then_inc(consts_in, 16)
            sp.dma_start(trig_tab[:, :], a["trig_tab"]).then_inc(consts_in, 16)
            sp.dma_start(b_row[:, :], a["b_gate"]).then_inc(consts_in, 16)
            sp.dma_start(norm0[:, :], a["norm0"].partition_broadcast(P)).then_inc(consts_in, 16)
            sp.dma_start(pos_i[:, :], a["pos"].partition_broadcast(S)).then_inc(consts_in, 16)
            for n in range(1, len(chunks)):
                load_chunk(n)
            load_group(1, 1)
            with sp.Fori(1, GROUPS - 1) as i:
                load_group(i + 1, i + 1)
                store_group(i - 1, i)
            store_group(GROUPS - 2, GROUPS - 1)
            store_group(GROUPS - 1, GROUPS)
            sp.wait_ge(stored, 16 * GROUPS)

        @block.scalar
        def _(act):
            def split_chunk(n):
                rows = chunks[n][1]
                act.wait_ge(raw_in[n], 16)
                for at, count, to, scale in chunks[n][3]:
                    last = act.activation(w_hi[0:rows, to:to + count], stage[0:rows, n % 2, at:at + count],
                                          ACT.Copy, scale=scale)
                last.then_inc(raw_hi, 1)

            def square_sum(n, cur):
                for t in range(NT):
                    last = act.activation(tok[:, t, :], res[:, t, :], ACT.Square, accum_out=sumsq[:, n, t:t + 1])
                last.then_inc(sq_r[n], 1)

            def probabilities(k, scale, cur):
                for c in range(2):
                    act.wait_ge(low_r[k][c], cur)
                    act.activation(sm[:, 2 * c:2 * c + 2, :], sm[:, 2 * c:2 * c + 2, :], ACT.Exp,
                                   scale=scale).then_inc(exp_r[k][c], 1)

            def layer0(cur, prev):
                act.wait_ge(xc_in, cur * 16)
                act.activation(xc_hi[:, :, :], xc[:, :, :], ACT.Copy).then_inc(xc_hi_r, 1)
                act.wait_ge(q0_mm, cur)
                act.activation(tok[:, 0, :], ps[:, 4, 0:TOK], ACT.Copy, scale=float(D) ** -0.5).then_inc(q0_r, 1)
                act.wait_ge(kv_mm, cur)
                act.activation(ck_t[:, :], ps[:, 5, 0:TOK], ACT.Copy)
                cv = ps[:, 5, TOK:2 * TOK].rearrange("p (t h c) -> p t h c", t=NT, h=PAIRS)
                for b in range(2):
                    r = slice(64 * b, 64 * b + 64)
                    last = act.activation(cvblk[r, :, :, b * 2 * CHD:(b + 1) * 2 * CHD], cv[r], ACT.Copy)
                last.then_inc(kv_r, 1)
                act.wait_ge(low0, cur)
                act.activation(sm[:, 0, 0:P], sm[:, 0, 0:P], ACT.Exp).then_inc(exp0, 1)
                act.wait_ge(p0t_mm, cur)
                act.activation(sm[:, 1, 0:P], ps[:, 1, 0:P], ACT.Copy).then_inc(p0t, 1)
                act.wait_ge(am_mm, cur)
                act.activation(am_hi[:, :, :], ps[:, 2:4, 0:P], ACT.Copy).then_inc(am_hi_r, 1)
                act.wait_ge(mcz_mm, cur)
                act.activation(ra[:, :, 0:D], ps[:, 4:6, D:2 * D], ACT.Tanh, scale=0.5).then_inc(tanh0, 1)
                act.wait_ge(fused, cur)
                square_sum(0, cur)
                act.wait_ge(x1_r, cur)
                square_sum(1, cur)

            def self_attention(cur, prev):
                act.wait_ge(tx1_mm, cur)
                act.activation(t_hi[:, :, :], ps[:, 5, :], ACT.Copy).then_inc(x1_hi, 1)
                act.wait_ge(pickr_r, cur)
                for t in range(NT):
                    act.wait_ge(qkv_mm[t], cur)
                    part = (ra, rb)[t][:, :, :].rearrange("p t c -> p (t c)")[:, 0:3 * D]
                    src = ps[:, 3 * t:3 * t + 3, :].rearrange("p b c -> p (b c)")[:, 0:3 * D]
                    act.activation(part, src, ACT.Copy, scale=pick_r[:, 0, t:t + 1]).then_inc(vpart[t], 1)
                act.wait_ge(qkv_r[1], cur)
                v = qkv[:, :, 2 * D:3 * D].rearrange("p t (h c) -> p t h c", h=PAIRS)
                for b in range(2):
                    r = slice(64 * b, 64 * b + 64)
                    last = act.activation(vblk[r, :, :, b * 2 * HD:(b + 1) * 2 * HD], v[r], ACT.Copy)
                last.then_inc(vb_r, 1)
                act.wait_ge(tk_mm, cur)
                act.activation(tok[:, :, :], ps[:, 1, :], ACT.Copy).then_inc(kt_r, 1)
                probabilities(0, float(HD) ** -0.5, cur)
                act.wait_ge(pt_mm[0][0], cur)
                act.activation(sm[:, 0:2, :], ps[:, 0:2, :], ACT.Copy).then_inc(pt_r[0][0], 1)
                act.wait_ge(tctx_mm[0], cur)
                act.activation(t_hi[:, :, :], ps[:, 4, :], ACT.Copy).then_inc(ctx_hi[0], 1)
                act.wait_ge(x2_r, cur)
                square_sum(2, cur)

            def cross_attention(cur, prev):
                act.wait_ge(tci_mm, cur)
                act.activation(t_hi[:, :, :], ps[:, 4, :], ACT.Copy).then_inc(ci_hi, 1)
                act.wait_ge(cq_mm, cur)
                act.activation(tok[:, 0, :], ps[:, 5, 0:TOK], ACT.Copy).then_inc(cq_s, 1)
                probabilities(1, float(CHD) ** -0.5, cur)
                act.wait_ge(pt_mm[1][0], cur)
                act.activation(sm[:, 0:2, :], ps[:, 0:2, :], ACT.Copy).then_inc(pt_r[1][0], 1)
                act.wait_ge(tctx_mm[1], cur)
                act.activation(t_hi[:, 0, :], ps[:, 0, 0:TOK], ACT.Copy).then_inc(ctx_hi[1], 1)
                act.wait_ge(x3_r, cur)
                square_sum(3, cur)
                before(act, stored, prev * 16)
                act.activation(res_b[:, :, :], res[:, :, :], ACT.Copy).then_inc(resb_r, 1)
                act.wait_ge(tmi_mm, cur)
                act.activation(mi_hi[:, :, :], ps[:, 2, :], ACT.Copy).then_inc(mi_hi_r, 1)

            def mlp(base, lo, hi):
                for n in range(lo, hi + 1):
                    if n < hi:
                        r = slice(0, P if n < 2 * FULL else 2 * LEFT)
                        act.wait_ge(gu_mm, base + (n + 1))
                        if n >= 2:
                            act.wait_ge(h_lo_r, base + (n - 1))
                        act.activation(hb[r, n % 2, :], ps[r, M0 + n % 2, 0:TOK], ACT.Tanh,
                                       scale=0.5).then_inc(th_r, 1)
                    if n > lo:
                        m = n - 1
                        r = slice(0, P if m < 2 * FULL else 2 * LEFT)
                        act.wait_ge(h_r, base + (m + 1))
                        act.activation(h_hi[r, m, :], hb[r, m % 2, :], ACT.Copy).then_inc(h_hi_r, 1)

            act.preload_act_table(ACT.Exp)
            act.wait_ge(consts_in, 16 * 8)
            for n in range(3):
                split_chunk(n)
            act.wait_ge(gm_mm, 1)
            act.activation(w_hi[:, wcols("gate_m", 0, D)], ps[:, 7, 0:D], ACT.Copy).then_inc(gm_hi, 1)
            act.activation(b_hi[:, :], b_row[:, :], ACT.Copy)
            act.wait_ge(filled, 1)
            act.activation(ones_r[:, :], ones_row[:, :], ACT.Copy).then_inc(bias_hi, 1)
            act.wait_ge(trig_mm, 1)
            act.activation(trig[:, :, :], ps[:, 6, 0:2 * HD], ACT.Copy).then_inc(trig_ready, 1)
            layer0(1, 0)
            split_chunk(3)
            self_attention(1, 0)
            for n in range(4, len(chunks)):
                split_chunk(n)
            cross_attention(1, 0)
            with act.Fori(1, GROUPS) as i:
                base = act.snap((i - 1) * MT)
                layer0(i + 1, i)
                mlp(base, 0, MT)
                self_attention(i + 1, i)
                cross_attention(i + 1, i)
            mlp((GROUPS - 1) * MT, 0, MT)

        @block.vector
        def _(dve):
            def split_chunk(n):
                rows = chunks[n][1]
                dve.wait_ge(raw_in[n], 16)
                dve.wait_ge(raw_hi, n + 1)
                for at, count, to, scale in chunks[n][3]:
                    last = dve.scalar_tensor_tensor(
                        out=w_lo[0:rows, to:to + count], in0=stage[0:rows, n % 2, at:at + count], scalar=scale,
                        in1=f32(w_hi[0:rows, to:to + count]), op0=ALU.mult, op1=ALU.subtract)
                last.then_inc(raw_lo, 1)

            def lo_part(out_, full, hi_part):
                return dve.tensor_tensor(out_, full, f32(hi_part), ALU.subtract)

            def variance(n, cur):
                dve.wait_ge(sq_r[n], cur)
                dve.tensor_scalar(var[:, n, :], sumsq[:, n, :], 1.0 / D, EPS, ALU.mult, ALU.add).then_inc(var_r[n], 1)

            def softmax(k, cur):
                if k == 0:
                    for c in range(2):
                        dve.wait_ge(s_mm[0][c], cur)
                        dve.tensor_tensor(sm[:, 2 * c:2 * c + 2, :].rearrange("p a (g s) -> p (a g) s", s=S),
                                          ps[:, 2 * c:2 * c + 2, :].rearrange("p a (g s) -> p (a g) s", s=S),
                                          causal[:, :].unsqueeze(1).to_broadcast([P, 16, S]),
                                          ALU.add).then_inc(masked[c], 1)
                for c in range(2):
                    dve.wait_ge(masked[c] if k == 0 else s_mm[1][c], cur)
                    src = (sm if k == 0 else ps)[:, 2 * c:2 * c + 2, :]
                    dve.tensor_reduce(top[:, 16 * c:16 * c + 16], src.rearrange("p a (g s) -> p (a g) s", s=S),
                                      AX_X, ALU.max).then_inc(top_r[k][c], 1)
                for c in range(2):
                    dve.wait_ge(top_r[k][c], cur)
                    src = (sm if k == 0 else ps)[:, 2 * c:2 * c + 2, :]
                    dve.tensor_tensor(sm[:, 2 * c:2 * c + 2, :].rearrange("p a (g s) -> p (a g) s", s=S),
                                      src.rearrange("p a (g s) -> p (a g) s", s=S),
                                      top[:, 16 * c:16 * c + 16].unsqueeze(2).to_broadcast([P, 16, S]),
                                      ALU.subtract).then_inc(low_r[k][c], 1)

            def layer0(cur, prev):
                dve.wait_ge(mask_dma, cur * 16)
                dve.tensor_scalar(mask_is1[:, :, :], mask_in[:, :, :], 1.0, None, ALU.is_equal).then_inc(is1, 1)
                dve.wait_ge(is1, cur)
                dve.scalar_tensor_tensor(out=pick[:, 0, :], in0=mask_is1[:, 0, :], scalar=consts[:, 6:7],
                                         in1=mask_is1[:, 1, :], op0=ALU.mult, op1=ALU.mult).then_inc(pick_v, 1)
                dve.wait_ge(xc_in, cur * 16)
                dve.wait_ge(xc_hi_r, cur)
                lo_part(xc_lo[:, :, :], xc[:, :, :], xc_hi[:, :, :]).then_inc(xc_lo_r, 1)
                dve.wait_ge(pick_v, cur)
                dve.tensor_scalar(pick[:, 1, :], pick[:, 0, :], -1.0, 1.0, ALU.mult, ALU.add).then_inc(picks, 1)
                sc, g0 = ps[:, 0, 0:P].rearrange("p (t s) -> p t s", s=S), sm[:, 0, 0:P].rearrange("p (t s) -> p t s", s=S)
                dve.wait_ge(sc0_mm, cur)
                dve.tensor_reduce(top[:, 0:NT], sc, AX_X, ALU.max).then_inc(top0, 1)
                dve.wait_ge(top0, cur)
                dve.tensor_tensor(g0, sc, top[:, 0:NT].unsqueeze(2).to_broadcast([P, NT, S]),
                                  ALU.subtract).then_inc(low0, 1)
                dve.wait_ge(exp0, cur)
                dve.tensor_reduce(inv[:, 0:NT, 0], g0, AX_X, ALU.add).then_inc(sum0, 1)
                dve.wait_ge(sum0, cur)
                dve.reciprocal(inv[:, 0:NT, 1], inv[:, 0:NT, 0]).then_inc(inv0, 1)
                dve.wait_ge(inv0, cur)
                dve.tensor_tensor(g0, g0, inv[:, 0:NT, 1:2].to_broadcast([P, NT, S]), ALU.mult).then_inc(p0, 1)
                dve.wait_ge(am_hi_r, cur)
                lo_part(am_lo[:, :, :], ps[:, 2:4, 0:P], am_hi[:, :, :]).then_inc(am_lo_r, 1)
                dve.wait_ge(tanh0, cur)
                dve.scalar_tensor_tensor(out=ra[:, :, 0:D], in0=ra[:, :, 0:D], scalar=1.0, in1=ps[:, 4:6, 0:D],
                                         op0=ALU.add, op1=ALU.mult).then_inc(gated, 1)
                dve.wait_ge(gated, cur)
                dve.wait_ge(xtok_in, cur * 16)
                before(dve, resb_r, prev)
                dve.scalar_tensor_tensor(out=res[:, :, :], in0=ra[:, :, 0:D], scalar=0.5, in1=x_tok[:, :, :],
                                         op0=ALU.mult, op1=ALU.add).then_inc(fused, 1)
                variance(0, cur)
                dve.wait_ge(rms_r[0], cur)
                for t in range(NT):
                    last = dve.scalar_tensor_tensor(out=res[:, t, :], in0=res[:, t, :], scalar=rms[:, 0, t:t + 1],
                                                    in1=norm0[:, :], op0=ALU.mult, op1=ALU.mult)
                last.then_inc(x1_r, 1)
                variance(1, cur)

            def self_attention(cur, prev):
                dve.wait_ge(x1_hi, cur)
                lo_part(t_lo[:, :, :], ps[:, 5, :], t_hi[:, :, :]).then_inc(x1_lo, 1)
                dve.wait_ge(rms_r[1], cur)
                dve.wait_ge(picks, cur)
                dve.tensor_tensor(pick_r[:, :, :], pick[:, :, :],
                                  rms[:, 1, :].unsqueeze(1).to_broadcast([P, 2, NT]), ALU.mult).then_inc(pickr_r, 1)
                dve.wait_ge(pickr_r, cur)
                for t in range(NT):
                    part = (ra, rb)[t][:, :, :].rearrange("p t c -> p (t c)")[:, 0:3 * D]
                    src = ps[:, 3 * t:3 * t + 3, :].rearrange("p b c -> p (b c)")[:, 3 * D:6 * D]
                    dve.wait_ge(vpart[t], cur)
                    dve.scalar_tensor_tensor(out=qkv[:, t, :], in0=src, scalar=pick_r[:, 1, t:t + 1], in1=part,
                                             op0=ALU.mult, op1=ALU.add).then_inc(qkv_r[t], 1)
                dve.wait_ge(qkv_r[1], cur)
                dve.tensor_tensor(ra[:, :, :].rearrange("p t (h c) -> p t h c", c=HD),
                                  qkv[:, :, 0:2 * D].rearrange("p t (h c) -> p t h c", c=HD),
                                  trig[:, 0, :].unsqueeze(1).unsqueeze(1).to_broadcast([P, NT, 2 * HEADS, HD]),
                                  ALU.mult).then_inc(rope_c, 1)
                dve.wait_ge(rope_c, cur)
                dve.wait_ge(rope_s, cur)
                dve.tensor_tensor(ra[:, :, :], ra[:, :, :], rb[:, :, :], ALU.add).then_inc(rope_r, 1)
                dve.wait_ge(tq_mm, cur)
                for e in range(2):
                    last = dve.tensor_scalar(qblk[:, :, :, e, :],
                                             ps[:, 0, :].rearrange("p (k r s) -> p k r s", k=2, s=S),
                                             consts[:, e:e + 1], None, ALU.mult)
                last.then_inc(qb_r, 1)
                softmax(0, cur)
                dve.wait_ge(pt_mm[0][1], cur)
                dve.tensor_copy(sm[:, 2:4, :], ps[:, 2:4, :]).then_inc(pt_r[0][1], 1)
                dve.wait_ge(pv_mm[0], cur)
                pv = ps[:, 0:4, 0:4 * VB].rearrange("p a (j c) -> p a j c", c=VB)
                iv = inv[:, :, :].rearrange("p (a j) b -> p a j b", j=4)
                dve.reciprocal(iv, pv[:, :, :, VB - 2:VB]).then_inc(inv_r[0], 1)
                dve.wait_ge(inv_r[0], cur)
                to = tok[:, :, :].rearrange("p t (k j e c) -> p (t k) j e c", k=2, j=4, e=2)
                for e in range(2):
                    for b in range(2):
                        r, w = slice(64 * e, 64 * e + 64), slice(64 * b, 64 * b + 64)
                        at = b * 2 * HD + e * HD
                        last = dve.tensor_tensor(to[w, :, :, e, :], pv[r, :, :, at:at + HD],
                                                 iv[r, :, :, b:b + 1].to_broadcast([64, 4, 4, HD]), ALU.mult)
                last.then_inc(ctx_r[0], 1)
                dve.wait_ge(ctx_hi[0], cur)
                lo_part(t_lo[:, :, :], ps[:, 4, :], t_hi[:, :, :]).then_inc(ctx_lo[0], 1)
                dve.wait_ge(dense_mm, cur)
                for t in range(NT):
                    dve.scalar_tensor_tensor(out=res[:, t, :], in0=ps[:, t, 0:D], scalar=pick[:, 0, t:t + 1],
                                             in1=res[:, t, :], op0=ALU.mult, op1=ALU.add).then_inc(res_v[t], 1)
                for t in range(NT):
                    dve.wait_ge(res_v[t], cur)
                    last = dve.scalar_tensor_tensor(out=res[:, t, :], in0=ps[:, t, D:2 * D], scalar=pick[:, 1, t:t + 1],
                                                    in1=res[:, t, :], op0=ALU.mult, op1=ALU.add)
                last.then_inc(x2_r, 1)
                variance(2, cur)

            def cross_attention(cur, prev):
                dve.wait_ge(ci_hi, cur)
                lo_part(t_lo[:, :, :], ps[:, 4, :], t_hi[:, :, :]).then_inc(ci_lo, 1)
                dve.wait_ge(cq_s, cur)
                for m in range(4):
                    last = dve.tensor_scalar(qblk[:, m // 2, :, m % 2, :],
                                             tok[:, 0, :].rearrange("p (r s) -> p r s", s=S),
                                             consts[:, 2 + m:3 + m], None, ALU.mult)
                last.then_inc(cqb_r, 1)
                softmax(1, cur)
                dve.wait_ge(pt_mm[1][1], cur)
                dve.tensor_copy(sm[:, 2:4, :], ps[:, 2:4, :]).then_inc(pt_r[1][1], 1)
                dve.wait_ge(pv_mm[1], cur)
                pv = ps[:, 4:6, 0:PAIRS * CVB].rearrange("p t (h c) -> p t h c", c=CVB)
                iv = inv[:, :, :].rearrange("p (t h) b -> p t h b", t=NT)
                dve.reciprocal(iv, pv[:, :, :, CVB - 2:CVB]).then_inc(inv_r[1], 1)
                dve.wait_ge(inv_r[1], cur)
                to = tok[:, :, 0:C].rearrange("p t (h e c) -> p t h e c", h=PAIRS, e=2)
                for e in range(2):
                    for b in range(2):
                        r, w = slice(64 * e, 64 * e + 64), slice(64 * b, 64 * b + 64)
                        at = b * 2 * CHD + e * CHD
                        last = dve.tensor_tensor(to[w, :, :, e, :], pv[r, :, :, at:at + CHD],
                                                 iv[r, :, :, b:b + 1].to_broadcast([64, NT, PAIRS, CHD]), ALU.mult)
                last.then_inc(ctx_r[1], 1)
                dve.wait_ge(ctx_hi[1], cur)
                lo_part(t_lo[:, 0, :], ps[:, 0, 0:TOK], t_hi[:, 0, :]).then_inc(ctx_lo[1], 1)
                dve.wait_ge(cd_mm, cur)
                dve.tensor_tensor(res[:, :, :], ps[:, 1, :], res[:, :, :].rearrange("p t c -> p (t c)"),
                                  ALU.add).then_inc(x3_r, 1)
                variance(3, cur)
                dve.wait_ge(y_r, prev + 1)
                dve.tensor_copy(pick_b[:, :, :], pick[:, :, :]).then_inc(pickb_r, 1)
                dve.wait_ge(mi_hi_r, cur)
                lo_part(mi_lo[:, :, :], ps[:, 2, :], mi_hi[:, :, :]).then_inc(mi_lo_r, 1)

            def mlp(base, lo, hi):
                for n in range(lo, hi):
                    r = slice(0, P if n < 2 * FULL else 2 * LEFT)
                    bank = ps[r, M0 + n % 2, :]
                    dve.wait_ge(th_r, base + (n + 1))
                    dve.scalar_tensor_tensor(out=hb[r, n % 2, :], in0=hb[r, n % 2, :], scalar=1.0, in1=bank[:, 0:TOK],
                                             op0=ALU.add, op1=ALU.mult).then_inc(tg_r, 1)
                    dve.wait_ge(tg_r, base + (n + 1))
                    dve.tensor_tensor(hb[r, n % 2, :], hb[r, n % 2, :], bank[:, TOK:2 * TOK], ALU.mult).then_inc(h_r, 1)

            def result(cur):
                for t in range(NT):
                    dve.wait_ge(down_mm[t], cur)
                    dve.wait_ge(resb_r, cur)
                    dve.scalar_tensor_tensor(out=res_b[:, t, :], in0=ps[:, M0 + t, 0:D], scalar=pick_b[:, 0, t:t + 1],
                                             in1=res_b[:, t, :], op0=ALU.mult, op1=ALU.add).then_inc(y_v[t], 1)
                    dve.wait_ge(y_v[t], cur)
                    last = dve.scalar_tensor_tensor(out=res_b[:, t, :], in0=ps[:, M0 + t, D:2 * D],
                                                    scalar=pick_b[:, 1, t:t + 1], in1=res_b[:, t, :],
                                                    op0=ALU.mult, op1=ALU.add)
                last.then_inc(y_r, 1)

            dve.memset(vblk[:, :, :, :], 0.0)
            dve.memset(cvblk[:, :, :, :], 0.0)
            dve.memset(ones_row[:, :], 1.0)
            dve.memset(minus_half[:, :], -0.5).then_inc(zeroed, 1)
            dve.wait_ge(zeroed, 1)
            for b in range(2):
                dve.memset(vblk[64 * b:64 * b + 64, :, :, VB - 2 + b:VB - 1 + b], 1.0)
                last = dve.memset(cvblk[64 * b:64 * b + 64, :, :, CVB - 2 + b:CVB - 1 + b], 1.0)
            last.then_inc(filled, 1)
            dve.memset(pick_b[:, :, :], 0.0).then_inc(y_r, 1)
            dve.wait_ge(consts_in, 16 * 8)
            dve.tensor_copy(pos_f[:, :], pos_i[:, :]).then_inc(pos_done, 1)
            dve.wait_ge(pos_done, 1)
            dve.tensor_scalar(pos_neg[:, :], pos_f[:, :], 0.0, float(S), ALU.is_lt, ALU.mult).then_inc(pos_done, 1)
            dve.wait_ge(pos_done, 2)
            dve.tensor_tensor(pos_f[:, :], pos_f[:, :], pos_neg[:, :], ALU.add).then_inc(pos_done, 1)
            dve.wait_ge(pos_done, 3)
            dve.tensor_scalar(pos_f[:, :], pos_f[:, :], 0.0, float(S - 1), ALU.max, ALU.min).then_inc(pos_done, 1)
            dve.wait_ge(pos_done, 4)
            dve.tensor_scalar(onehot[:, :, :], pos_f[:, :].unsqueeze(1).to_broadcast([S, 2, S]),
                              consts[0:S, 7:8], None, ALU.is_equal).then_inc(pos_done, 1)
            for n in range(3):
                split_chunk(n)
            dve.wait_ge(gm_hi, 1)
            lo_part(w_lo[:, wcols("gate_m", 0, D)], ps[:, 7, 0:D], w_hi[:, wcols("gate_m", 0, D)]).then_inc(gm_lo, 1)
            dve.wait_ge(bias_hi, 1)
            lo_part(b_lo[:, :], b_row[:, :], b_hi[:, :]).then_inc(bias_lo, 1)
            layer0(1, 0)
            split_chunk(3)
            dve.wait_ge(trig_ready, 1)
            self_attention(1, 0)
            for n in range(4, len(chunks)):
                split_chunk(n)
            cross_attention(1, 0)
            with dve.Fori(1, GROUPS) as i:
                base = dve.snap((i - 1) * MT)
                layer0(i + 1, i)
                mlp(base, 0, MT)
                result(i)
                self_attention(i + 1, i)
                cross_attention(i + 1, i)
            mlp((GROUPS - 1) * MT, 0, MT)
            result(GROUPS)

        @block.gpsimd
        def _(pool):
            def root(n, cur):
                pool.wait_ge(var_r[n], cur)
                pool.tensor_tensor(rms[:, n, :], var[:, n, :], minus_half[:, :], ALU.pow).then_inc(rms_r[n], 1)

            def layer0(cur, prev):
                root(0, cur)
                root(1, cur)

            def attention(cur, prev):
                q = qkv[:, :, 0:2 * D].rearrange("p t (h e c) -> p t h e c", h=2 * HEADS, e=2)
                r = rb[:, :, :].rearrange("p t (h e c) -> p t h e c", h=2 * HEADS, e=2)
                pool.wait_ge(qkv_r[1], cur)
                for e in range(2):
                    sin = trig[:, 1, e * HD // 2:(e + 1) * HD // 2]
                    last = pool.tensor_tensor(
                        r[:, :, :, e, :], q[:, :, :, 1 - e, :],
                        sin.unsqueeze(1).unsqueeze(1).to_broadcast([P, NT, 2 * HEADS, HD // 2]), ALU.mult)
                last.then_inc(rope_s, 1)
                root(2, cur)
                pool.wait_ge(rms_r[2], cur)
                pool.tensor_tensor(tok[:, :, :], res[:, :, :], rms[:, 2, :].unsqueeze(2).to_broadcast([P, NT, D]),
                                   ALU.mult).then_inc(ci_r, 1)
                root(3, cur)
                pool.wait_ge(rms_r[3], cur)
                pool.tensor_tensor(tok[:, :, :], res[:, :, :], rms[:, 3, :].unsqueeze(2).to_broadcast([P, NT, D]),
                                   ALU.mult).then_inc(mi_r, 1)

            def mlp(base, lo, hi):
                for n in range(lo, hi):
                    r = slice(0, P if n < 2 * FULL else 2 * LEFT)
                    pool.wait_ge(h_hi_r, base + (n + 1))
                    pool.tensor_tensor(h_lo[r, n, :], hb[r, n % 2, :], f32(h_hi[r, n, :]),
                                       ALU.subtract).then_inc(h_lo_r, 1)

            pool.wait_ge(trig_ready, 1)
            layer0(1, 0)
            attention(1, 0)
            with pool.Fori(1, GROUPS) as i:
                base = pool.snap((i - 1) * MT)
                layer0(i + 1, i)
                mlp(base, 0, MT)
                attention(i + 1, i)
            mlp((GROUPS - 1) * MT, 0, MT)

        @block.tensor
        def _(pe):
            def product(o, lh, ll, rh, rl, start=False, stop=False):
                pe.matmul(o, lh, rh, start=start, stop=False, skip_group_check=True)
                pe.matmul(o, lh, rl, start=False, stop=False, skip_group_check=True)
                return pe.matmul(o, ll, rh, start=False, stop=stop, skip_group_check=True)

            def transposes(bank, src):
                for t in range(NT):
                    for k in range(src.shape[2] // P):
                        last = pe.transpose(ps[:, bank, k * TOK + t * P:k * TOK + (t + 1) * P],
                                            src[:, t, k * P:(k + 1) * P], ident[:, :])
                return last

            def layer0(cur, prev):
                pe.wait_ge(xc_hi_r, cur)
                pe.wait_ge(xc_lo_r, cur)
                for k in range(KD):
                    w = wcols("mem", k * C, C)
                    last = product(ps[:, 4, 0:TOK], w_hi[:, w], w_lo[:, w], xc_hi[:, k, :], xc_lo[:, k, :],
                                   k == 0, k == KD - 1)
                last.then_inc(q0_mm, 1)
                w = wcols("ckv", 0, C)
                product(ps[:, 5, 0:TOK], w_hi[:, w], w_lo[:, w], xc_hi[:, KD, :], xc_lo[:, KD, :], True, True)
                w = wcols("ckv", C, C)
                for t in range(NT):
                    c = slice(t * P, (t + 1) * P)
                    last = product(ps[:, 5, TOK + t * P:TOK + (t + 1) * P], xc_hi[:, KD, c], xc_lo[:, KD, c],
                                   w_hi[:, w], w_lo[:, w], True, True)
                last.then_inc(kv_mm, 1)
                pe.wait_ge(q0_r, cur)
                for t in range(NT):
                    for b in range(2):
                        c = slice(t * P + b * S, t * P + (b + 1) * S)
                        last = pe.matmul(ps[64 * b:64 * b + 64, 0, t * S:(t + 1) * S], tok[:, 0, c], xc[:, KD, c],
                                         start=True, stop=True, skip_group_check=True)
                last.then_inc(sc0_mm, 1)
                pe.wait_ge(p0, cur)
                pe.transpose(ps[:, 1, 0:P], sm[:, 0, 0:P], ident[:, :]).then_inc(p0t_mm, 1)
                pe.wait_ge(p0t, cur)
                pe.wait_ge(ctok_in, cur * 16)
                before(pe, mi_lo_r, prev)
                for t in range(NT):
                    r = slice(64 * t, 64 * t + 64)
                    for b in range(2):
                        last = pe.matmul(ps[:, 2 + t, b * S:(b + 1) * S], ctx_tok[r, b, :],
                                         sm[r, 1, b * S:(b + 1) * S], start=True, stop=True, skip_group_check=True)
                last.then_inc(am_mm, 1)
                pe.wait_ge(kv_r, cur)
                pe.wait_ge(am_hi_r, cur)
                pe.wait_ge(am_lo_r, cur)
                for t in range(NT):
                    w = wcols("mem_t", 0, 2 * D)
                    product(ps[:, 4 + t, :], am_hi[:, t, :], am_lo[:, t, :], w_hi[:, w], w_lo[:, w], True, False)
                    z, c = ps[:, 4 + t, D:2 * D], slice(t * P, (t + 1) * P)
                    for k in range(KD):
                        w = wcols("gate_x", k * D, D)
                        product(z, xc_hi[:, k, c], xc_lo[:, k, c], w_hi[:, w], w_lo[:, w])
                    pe.matmul(z, ones_r[:, :], b_hi[:, :], start=False, stop=False, skip_group_check=True)
                    last = pe.matmul(z, ones_r[:, :], b_lo[:, :], start=False, stop=True, skip_group_check=True)
                last.then_inc(mcz_mm, 1)

            def scores(k, k_of, cur):
                for c in range(2):
                    for m in range(2):
                        for t in range(NT):
                            for b in range(2):
                                tk = slice(t * P + b * S, t * P + (b + 1) * S)
                                at = m * 256 + t * P + b * S
                                for j in (2 * c, 2 * c + 1):
                                    r = slice(32 * j, 32 * j + 32)
                                    last = pe.matmul(ps[:, j, at:at + S],
                                                     qblk[r, m, 2 * t + b, :, :].rearrange("p e s -> p (e s)"),
                                                     k_of(r, m, tk),
                                                     start=True, stop=True, skip_group_check=True)
                    last.then_inc(s_mm[k][c], 1)

            def transposed_probs(k, cur):
                for c in range(2):
                    pe.wait_ge(exp_r[k][c], cur)
                    for j in (2 * c, 2 * c + 1):
                        for m in range(4):
                            last = pe.transpose(ps[:, j, m * P:(m + 1) * P], sm[:, j, m * P:(m + 1) * P], ident[:, :])
                    last.then_inc(pt_mm[k][c], 1)

            def self_attention(cur, prev):
                pe.wait_ge(x1_r, cur)
                transposes(5, res).then_inc(tx1_mm, 1)
                pe.wait_ge(x1_hi, cur)
                pe.wait_ge(x1_lo, cur)
                for t in range(NT):
                    c = slice(t * P, (t + 1) * P)
                    for n in range(3):
                        for k in range(KD):
                            w = wcols("qkv", k * 6 * D + n * 512, 512)
                            last = product(ps[:, 3 * t + n, :], t_hi[:, k, c], t_lo[:, k, c], w_hi[:, w], w_lo[:, w],
                                           k == 0, k == KD - 1)
                    last.then_inc(qkv_mm[t], 1)
                pe.wait_ge(rope_r, cur)
                transposes(0, ra[:, :, 0:D]).then_inc(tq_mm, 1)
                transposes(1, ra[:, :, D:2 * D]).then_inc(tk_mm, 1)
                pe.wait_ge(qb_r, cur)
                pe.wait_ge(kt_r, cur)
                scores(0, lambda r, m, tk: tok[r, m, tk], cur)
                transposed_probs(0, cur)
                pe.wait_ge(vb_r, cur)
                pe.wait_ge(pt_r[0][0], cur)
                pe.wait_ge(pt_r[0][1], cur)
                for t in range(NT):
                    for m in range(2):
                        for j in range(4):
                            last = pe.matmul(ps[:, 2 * t + m, j * VB:(j + 1) * VB],
                                             sm[:, j, m * 256 + t * P:m * 256 + (t + 1) * P],
                                             vblk[:, t, 4 * m + j, :], start=True, stop=True, skip_group_check=True)
                last.then_inc(pv_mm[0], 1)
                pe.wait_ge(ctx_r[0], cur)
                transposes(4, tok).then_inc(tctx_mm[0], 1)
                pe.wait_ge(ctx_hi[0], cur)
                pe.wait_ge(ctx_lo[0], cur)
                for t in range(NT):
                    c = slice(t * P, (t + 1) * P)
                    for k in range(KD):
                        w = wcols("dense", k * 2 * D, 2 * D)
                        last = product(ps[:, t, :], t_hi[:, k, c], t_lo[:, k, c], w_hi[:, w], w_lo[:, w],
                                       k == 0, k == KD - 1)
                last.then_inc(dense_mm, 1)

            def cross_attention(cur, prev):
                pe.wait_ge(ci_r, cur)
                transposes(4, tok).then_inc(tci_mm, 1)
                pe.wait_ge(ci_hi, cur)
                pe.wait_ge(ci_lo, cur)
                for k in range(KD):
                    w = wcols("cq", k * C, C)
                    last = product(ps[:, 5, 0:TOK], w_hi[:, w], w_lo[:, w], t_hi[:, k, :], t_lo[:, k, :],
                                   k == 0, k == KD - 1)
                last.then_inc(cq_mm, 1)
                pe.wait_ge(cqb_r, cur)
                scores(1, lambda r, m, tk: ck_t[r, tk], cur)
                transposed_probs(1, cur)
                pe.wait_ge(pt_r[1][0], cur)
                pe.wait_ge(pt_r[1][1], cur)
                for t in range(NT):
                    for h in range(PAIRS):
                        j, m = h // 2, h % 2
                        last = pe.matmul(ps[:, 4 + t, h * CVB:(h + 1) * CVB],
                                         sm[:, j, m * 256 + t * P:m * 256 + (t + 1) * P],
                                         cvblk[:, t, h, :], start=True, stop=True, skip_group_check=True)
                last.then_inc(pv_mm[1], 1)
                pe.wait_ge(ctx_r[1], cur)
                transposes(0, tok[:, :, 0:C]).then_inc(tctx_mm[1], 1)
                pe.wait_ge(ctx_hi[1], cur)
                pe.wait_ge(ctx_lo[1], cur)
                w = wcols("cdense", 0, D)
                for t in range(NT):
                    c = slice(t * P, (t + 1) * P)
                    last = product(ps[:, 1, t * D:(t + 1) * D], t_hi[:, 0, c], t_lo[:, 0, c], w_hi[:, w], w_lo[:, w],
                                   True, True)
                last.then_inc(cd_mm, 1)
                pe.wait_ge(mi_r, cur)
                transposes(2, tok).then_inc(tmi_mm, 1)

            def gate_up(base, cur, prev, lo, hi):
                if lo == 0:
                    pe.wait_ge(mi_hi_r, cur)
                    pe.wait_ge(mi_lo_r, cur)
                for n in range(lo, hi):
                    width = P if n < 2 * FULL else 2 * LEFT
                    if n < 2:
                        pe.wait_ge(y_r, prev + 1)
                    else:
                        pe.wait_ge(h_r, base + (n - 1))
                    for u in range(2):
                        for k in range(KD):
                            w = wcols("gu", k * GU + n * 2 * P + u * width, width)
                            last = product(ps[0:width, M0 + n % 2, u * TOK:(u + 1) * TOK], w_hi[:, w], w_lo[:, w],
                                           mi_hi[:, k, :], mi_lo[:, k, :], k == 0, k == KD - 1)
                    last.then_inc(gu_mm, 1)

            def down(base):
                pe.wait_ge(h_hi_r, base + MT)
                pe.wait_ge(h_lo_r, base + MT)
                pe.wait_ge(h_r, base + MT)
                for t in range(NT):
                    c, r = slice(t * P, (t + 1) * P), slice(0, 2 * LEFT)
                    w = wcols("down_left", 0, 2 * D)
                    product(ps[:, M0 + t, :], h_hi[r, MT - 1, c], h_lo[r, MT - 1, c], w_hi[r, w], w_lo[r, w], True)
                    for n in range(2 * FULL):
                        w, e = wcols("down", n * D, D), n // FULL
                        last = product(ps[:, M0 + t, e * D:(e + 1) * D], h_hi[:, n, c], h_lo[:, n, c],
                                       w_hi[:, w], w_lo[:, w], False, n == 2 * FULL - 1)
                    last.then_inc(down_mm[t], 1)

            pe.wait_ge(consts_in, 16 * 8)
            pe.wait_ge(pos_done, 5)
            pe.matmul(ps[:, 6, 0:2 * HD], onehot[:, :, :], trig_tab[:, :], start=True, stop=True).then_inc(trig_mm, 1)
            pe.wait_ge(raw_in[0], 16)
            for k in range(KD):
                last = pe.matmul(ps[:, 7, 0:D], raw_mem[:, k * C:(k + 1) * C], raw_gate_m[:, k * D:(k + 1) * D],
                                 start=(k == 0), stop=(k == KD - 1))
            last.then_inc(gm_mm, 1)
            pe.wait_ge(raw_lo, 3)
            pe.wait_ge(gm_lo, 1)
            pe.wait_ge(bias_lo, 1)
            layer0(1, 0)
            pe.wait_ge(raw_lo, 4)
            self_attention(1, 0)
            cross_attention(1, 0)
            pe.wait_ge(raw_lo, len(chunks))
            with pe.Fori(1, GROUPS) as i:
                base = pe.snap((i - 1) * MT)
                layer0(i + 1, i)
                gate_up(base, i, i - 1, 0, MT)
                down(base)
                self_attention(i + 1, i)
                cross_attention(i + 1, i)
            last_base = (GROUPS - 1) * MT
            gate_up(last_base, GROUPS, GROUPS - 1, 0, MT)
            down(last_base)


def kernel(**inputs):
    import numpy as np
    import concourse.bacc as bacc
    from concourse.bass_utils import run_bass_kernel_spmd as run

    v = {n: np.ascontiguousarray(x) for n, x in inputs.items()}

    def by_k(w):
        return w.reshape(-1, P, w.shape[1]).transpose(1, 0, 2).reshape(P, -1)

    x, cx = v["x"].reshape(GROUPS, TOK, D), v["ctx_1024"].reshape(GROUPS, TOK, C)
    x_t = x.transpose(0, 2, 1).reshape(GROUPS, KD, P, TOK).transpose(0, 2, 1, 3)
    xc = np.concatenate([x_t, cx.transpose(0, 2, 1)[:, :, None, :]], axis=2)
    x_tok = x.reshape(GROUPS, NT, P, D).transpose(0, 2, 1, 3)
    ctx_tok = cx.reshape(GROUPS, NT, 2, S, C).transpose(0, 1, 3, 2, 4).reshape(GROUPS, P, 2, C)
    types = v["mask_BxS_ik0"].reshape(-1)
    mask = np.stack([types, np.roll(types, -1)]).reshape(2, GROUPS, NT, P).transpose(1, 3, 0, 2)
    wm, wg = v["L0_xattn_W_mem"], v["L0_xattn_W_gate"].T
    w_first = np.concatenate([by_k(wm), by_k(wg[:D]), wm.T, v["L1_xattn_ckv_w"], by_k(v["L1_xattn_cq_w"]),
                              by_k(wg[D:])], axis=1)
    w_qkv = np.concatenate([v["L1_xattn_v_qkv"], v["L1_xattn_l_qkv"]], axis=1).reshape(KD, P, 6 * D)
    w_dense = np.concatenate([by_k(np.concatenate([v["L1_xattn_v_dense"], v["L1_xattn_l_dense"]], axis=1)),
                              v["L1_xattn_cdense_w"]], axis=1)
    gates, ups = ([v[f"L1_xattn_{e}_{n}"] for e in "vl"] for n in ("gate", "up"))
    cols, cut = [], FULL * P
    for e in range(2):
        for n in range(FULL):
            cols += [w[e][:, n * P:(n + 1) * P] for w in (gates, ups)]
    cols += [w[e][:, cut:] for w in (gates, ups) for e in range(2)]
    w_gu = np.concatenate(cols, axis=1).reshape(KD, P, GU)
    downs = [v["L1_xattn_v_down"], v["L1_xattn_l_down"]]
    w_down = by_k(np.concatenate([w[:cut] for w in downs], axis=0))
    w_down_left = np.zeros((2 * LEFT, 2 * D), np.float32)
    for e in range(2):
        w_down_left[e * LEFT:(e + 1) * LEFT, e * D:(e + 1) * D] = downs[e][cut:]
    ln = np.stack([v[f"L1_xattn_ln_{n}_w"].reshape(KD, P).T for n in ("in", "post_cross", "post_attn")], axis=1)
    p = np.arange(P)
    consts = np.zeros((P, 8), np.float32)
    for e in range(2):
        consts[:, e] = p // HD % 2 == e
    for m in range(4):
        consts[:, 2 + m] = p // CHD % 4 == m
    consts[:, 6] = p % S != S - 1
    consts[:, 7] = p
    causal = np.where(np.arange(S)[None, :] <= (p % S)[:, None], 0.0, MASKED).astype(np.float32)
    inv_freq = (1.0 / np.float32(10000.0) ** (np.arange(0, HD, 2, dtype=np.float32) / np.float32(HD))).astype(np.float32)
    angle = np.outer(np.arange(S, dtype=np.float32), inv_freq).astype(np.float32)
    cos, sin = np.cos(angle), np.sin(angle)
    trig_tab = np.concatenate([cos, cos, -sin, sin], axis=1).astype(np.float32)

    arrays = {
        "xc": xc, "x_tok": x_tok, "ctx_tok": ctx_tok, "mask": mask, "w_first": w_first, "w_qkv": w_qkv,
        "w_dense": w_dense, "w_gu": w_gu, "w_down": w_down, "w_down_left": w_down_left, "ln": ln,
        "ident": np.eye(P, dtype=np.float32), "consts": consts, "causal": causal, "trig_tab": trig_tab,
        "b_gate": v["L0_xattn_b_gate"].reshape(1, D), "norm0": v["L0_xattn_norm_w"], "pos": v["pos_1xS"].reshape(S),
    }
    arrays = {n: np.ascontiguousarray(x) for n, x in arrays.items()}
    nc = bacc.Bacc("TRN2", target_bir_lowering=False, num_devices=1)
    a = {n: nc.dram_tensor(f"in_{n}", x.shape, mybir.dt.from_np(x.dtype), kind="ExternalInput").ap()
         for n, x in arrays.items()}
    out = nc.dram_tensor("out_y", (GROUPS, P, NT, D), F32, kind="ExternalOutput").ap()
    build_program(nc, a, out)
    r = run(nc, [{f"in_{n}": x for n, x in arrays.items()}], core_ids=[0])
    y = r.results[0]["out_y"]
    return y.transpose(0, 2, 1, 3).reshape(B, S, D)
```

```python
from contextlib import ExitStack

import concourse.bass as bass
from concourse import mybir

F32 = mybir.dt.float32
F32R = mybir.dt.float32r
I32 = mybir.dt.int32
ALU = mybir.AluOpType
ACT = mybir.ActivationFunctionType
AX_X = mybir.AxisListType.X

P = 128
B, S, D, C = 32, 64, 256, 128
TOK = 256
NT = TOK // P
GROUPS = B * S // TOK
KD = D // P
HEADS = 16
HD, CHD = D // HEADS, C // HEADS
PAIRS = HEADS // 2
INNER = 688
FULL = INNER // P
LEFT = INNER - FULL * P
MT = 2 * FULL + 1
EPS = 1e-6
MASKED = -1e30
UNITS = 3 * NT
GU = 4 * INNER
VB = 2 * HD + 2
CVB = 2 * CHD + 2
STAGE = MT * TOK

SIZES = [("mem", KD * C), ("gate_x", KD * D), ("mem_t", D), ("gate_m", D), ("ckv", 2 * C), ("cq", KD * C),
         ("qkv", KD * 6 * D), ("dense", KD * 2 * D), ("cdense", D),
         ("gu", KD * GU), ("down", 2 * FULL * D), ("down_left", 2 * D)]
AT, COLS = {}, 0
for _name, _size in SIZES:
    AT[_name] = COLS
    COLS += _size


def build_program(nc, a, out):
    with ExitStack() as ctx:
        def sb(name, shape, dt=F32):
            return ctx.enter_context(nc.sbuf_tensor(name, shape, dt))

        def sem(name):
            return ctx.enter_context(nc.semaphore(name))

        def sems(name, n):
            return [sem(f"{name}{k}") for k in range(n)]

        w_hi, w_lo = sb("w_hi", [P, COLS], F32R), sb("w_lo", [P, COLS], F32R)
        with nc.sbuf_tensor("stage", [P, 2, STAGE], F32) as stage:
            pass
        h_hi, h_lo = sb("h_hi", [P, MT, TOK], F32R), sb("h_lo", [P, MT, TOK], F32R)
        xc = sb("xc", [P, KD + 1, TOK])
        xc_hi, xc_lo = sb("xc_hi", [P, KD + 1, TOK], F32R), sb("xc_lo", [P, KD + 1, TOK], F32R)
        x_res = sb("x_res", [P, NT, D])
        ctx_tok = sb("ctx_tok", [P, 2, C])
        mask_in = sb("mask_in", [P, 2, NT], I32)
        mask_is1 = sb("mask_is1", [P, 2, NT])
        pick = sb("pick", [P, 2, NT])
        pick_r = sb("pick_r", [P, 2, NT])
        am_hi, am_lo = sb("am_hi", [P, NT, P], F32R), sb("am_lo", [P, NT, P], F32R)
        qkv = sb("qkv", [P, NT, 3 * D])
        ra, rb = sb("ra", [P, 512]), sb("rb", [P, 512])
        q0, p0, p0_t = rb[:, 0:TOK], rb[:, TOK:TOK + P], rb[:, TOK + P:512]
        ta_hi, ta_lo = sb("ta_hi", [P, KD, TOK], F32R), sb("ta_lo", [P, KD, TOK], F32R)
        q_t = sb("q_t", [P, 2, TOK])
        kblk = sb("kblk", [P, 4, TOK])
        ck_t = sb("ck_t", [P, TOK])
        vblk = sb("vblk", [P, NT, 2, PAIRS, VB])
        cvblk = sb("cvblk", [P, NT, 2, PAIRS, CVB])
        sm = sb("sm", [P, 4, 512])
        tok = sb("tok", [P, NT, D])
        res = sb("res", [P, NT, D])
        pick_y = sb("pick_y", [P, 2, NT])
        tb_hi, tb_lo = sb("tb_hi", [P, KD, TOK], F32R), sb("tb_lo", [P, KD, TOK], F32R)
        with (nc.sbuf_tensor("pos_i", [S, S], I32) as pos_i, nc.sbuf_tensor("pos_f", [S, S], F32) as pos_f,
              nc.sbuf_tensor("pos_neg", [S, S], F32) as pos_neg, nc.sbuf_tensor("onehot", [S, 2, S], F32) as onehot,
              nc.sbuf_tensor("trig_tab", [S, 2 * HD], F32) as trig_tab, nc.sbuf_tensor("b_row", [1, D], F32) as b_row,
              nc.sbuf_tensor("ones_row", [1, P], F32) as ones_row):
            pass
        HB = 3
        hb = sb("hb", [P, HB, TOK])
        res_b = sb("res_b", [P, NT, D])
        pick_b = sb("pick_b", [P, 2, NT])
        top0 = sb("top0", [P, NT])
        sum0 = sb("sum0", [P, 2, NT])
        top = sb("top", [P, 32])
        inv = sb("inv", [P, NT, PAIRS, 2])
        sumsq, var, rms = sb("sumsq", [P, 4, NT]), sb("var", [P, 4, NT]), sb("rms", [P, 4, NT])
        minus_half = sb("minus_half", [P, NT])
        ident = sb("ident", [P, P])
        causal = sb("causal", [P, S])
        consts = sb("consts", [P, 8])
        norm0 = sb("norm0", [P, D])
        ln = sb("ln", [P, 3, KD])
        trig = sb("trig", [P, 2, HD])
        b_hi, b_lo, ones_r = sb("b_hi", [1, D], F32R), sb("b_lo", [1, D], F32R), sb("ones_r", [1, P], F32R)
        ps = ctx.enter_context(nc.psum_tensor("ps", [P, 8, 512], F32))
        X0, X1, M0 = 4, 5, 6

        consts_in, raw_in = sem("consts_in"), sems("raw_in", 2)
        raw_hi, raw_lo = sem("raw_hi"), sem("raw_lo")
        gm_mm, gm_hi, gm_lo = sem("gm_mm"), sem("gm_hi"), sem("gm_lo")
        zeroed, filled, bias_hi, bias_lo = sem("zeroed"), sem("filled"), sem("bias_hi"), sem("bias_lo")
        pos_done, trig_mm, trig_ready = sem("pos_done"), sem("trig_mm"), sem("trig_ready")
        xc_in, xres_in, ctok_in, mask_dma = sem("xc_in"), sem("xres_in"), sem("ctok_in"), sem("mask_dma")
        is1, pick_v, picks = sem("is1"), sem("pick_v"), sem("picks")
        xc_hi_r, xc_lo_r, q0_mm, q0_r = sem("xc_hi_r"), sem("xc_lo_r"), sem("q0_mm"), sem("q0_r")
        sc0_mm, top0_r, low0_r, exp0_r, sum0_r, inv0_r, p0_r = (
            sem(n) for n in "sc0_mm top0_r low0_r exp0_r sum0_r inv0_r p0_r".split())
        p0t_mm, p0t_r, am_mm, am_hi_r, am_lo_r = (sem(n) for n in "p0t_mm p0t_r am_mm am_hi_r am_lo_r".split())
        mcz_mm, tanh_r, gated, fused = (sem(n) for n in "mcz_mm tanh_r gated fused".split())
        sq_r, var_r, rms_r = sems("sq_r", 4), sems("var_r", 4), sems("rms_r", 4)
        x1_r, tx1_mm, x1_hi, x1_lo = (sem(n) for n in "x1_r tx1_mm x1_hi x1_lo".split())
        pickr_r = sem("pickr_r")
        unit_mm, vpart, qkv_r = sem("unit_mm"), sem("vpart"), sem("qkv_r")
        rope_c, rope_s, rope_r = sem("rope_c"), sem("rope_s"), sem("rope_r")
        vb_r, tq_mm, tk_mm, qt_r, kb_r = (sem(n) for n in "vb_r tq_mm tk_mm qt_r kb_r".split())
        kv_mm, kv_r = sem("kv_mm"), sem("kv_r")
        picky_r = sem("picky_r")
        s_mm = [sems(f"s_mm{k}_", 2) for k in range(2)]
        masked = sems("masked", 2)
        top_r = [sems(f"top_r{k}_", 2) for k in range(2)]
        low_r = [sems(f"low_r{k}_", 2) for k in range(2)]
        exp_r = [sems(f"exp_r{k}_", 2) for k in range(2)]
        pt_mm = [sems(f"pt_mm{k}_", 2) for k in range(2)]
        pt_r = [sems(f"pt_r{k}_", 2) for k in range(2)]
        pv_mm, inv_r, ctx_r, tctx_mm, ctx_hi, ctx_lo = (
            sems(n, 2) for n in "pv_mm inv_r ctx_r tctx_mm ctx_hi ctx_lo".split())
        dense_mm, res_v, x2_r = sem("dense_mm"), sem("res_v"), sem("x2_r")
        ci_r, tci_mm, ci_hi, ci_lo = (sem(n) for n in "ci_r tci_mm ci_hi ci_lo".split())
        ckb_r, cq_mm, cq_r = sem("ckb_r"), sem("cq_mm"), sem("cq_r")
        cd_mm, x3_r, resb_r, pickb_r = (sem(n) for n in "cd_mm x3_r resb_r pickb_r".split())
        mi_r, tmi_mm, mi_hi, mi_lo = (sem(n) for n in "mi_r tmi_mm mi_hi mi_lo".split())
        gu_mm, th_r, tg_r, h_r, h_hi_r, h_lo_r = (sem(n) for n in "gu_mm th_r tg_r h_r h_hi_r h_lo_r".split())
        down_mm, y_v, y_r, stored = sem("down_mm"), sem("y_v"), sem("y_r"), sem("stored")

        def wcols(name, at, n):
            return slice(AT[name] + at, AT[name] + at + n)

        chunks = [
            (a["w_first"], P, 2048, [(0, 1024, AT["mem"], 1.0), (1024, 256, AT["ckv"], 1.0),
                                     (1280, 128, AT["cq"], ln[:, 1, 0:1]),
                                     (1408, 128, AT["cq"] + 128, ln[:, 1, 1:2])]),
            (a["w_qkv"][0], P, 6 * D, [(0, 6 * D, AT["qkv"], ln[:, 0, 0:1])]),
            (a["w_qkv"][1], P, 6 * D, [(0, 6 * D, AT["qkv"] + 6 * D, ln[:, 0, 1:2])]),
            (a["w_dense"], P, 5 * D, [(0, 5 * D, AT["dense"], 1.0)]),
            (a["w_gu"][0], P, GU, [(0, GU, AT["gu"], ln[:, 2, 0:1])]),
            (a["w_gu"][1], P, GU, [(0, GU, AT["gu"] + GU, ln[:, 2, 1:2])]),
            (a["w_down"], P, 2 * FULL * D, [(0, 2 * FULL * D, AT["down"], 0.5)]),
            (a["w_down_left"], 2 * LEFT, 2 * D, [(0, 2 * D, AT["down_left"], 0.5)]),
        ]
        raw_mem, raw_gate_m = stage[:, 0, 0:KD * C], stage[:, 0, 1536:2048]

        def before(eng, s, v):
            if not (isinstance(v, int) and v <= 0):
                eng.wait_ge(s, v)

        def f32(ap):
            return ap.bitcast(F32)

        def of_tile(ap, t):
            return ap[:, t * P:(t + 1) * P]

        def inner(n):
            return slice(0, P if n < 2 * FULL else 2 * LEFT)

        def groups(ap, c):
            return ap[:, 2 * c:2 * c + 2, :].rearrange("p a (g s) -> p (a g) s", s=S)

        def counts(g):
            return g + 1, g

        def unit_count(x, n):
            return x[1] * UNITS + n

        def tile_count(g, t):
            return g[1] * NT + (t + 1)

        block = ctx.enter_context(nc.Block())

        @block.sync
        def _(sp):
            def load_chunk(n):
                src, rows, cols, _ = chunks[n]
                if n >= 2:
                    sp.wait_ge(raw_lo, n - 1)
                if n == 2:
                    sp.wait_ge(gm_mm, 1)
                sp.dma_start(stage[0:rows, n % 2, 0:cols], src).then_inc(raw_in[n % 2], 16)

            def load_xc(g, prev):
                before(sp, sc0_mm, prev)
                before(sp, xc_lo_r, prev)
                sp.dma_start(xc[:, :, :], a["xc"][g]).then_inc(xc_in, 16)
                before(sp, is1, prev)
                sp.dma_start(mask_in[:, :, :], a["mask"][g]).then_inc(mask_dma, 16)
                before(sp, am_mm, prev)
                sp.dma_start(ctx_tok[:, :, :], a["ctx_tok"][g]).then_inc(ctok_in, 16)

            def load_x(g, prev):
                before(sp, x2_r, prev)
                sp.dma_start(x_res[:, :, :], a["x_tok"][g]).then_inc(xres_in, 16)

            def store(g, cur):
                sp.wait_ge(y_r, cur + 1)
                sp.dma_start(out[g], res_b[:, :, :]).then_inc(stored, 16)

            sp.dma_start(ln[:, :, :], a["ln"]).then_inc(consts_in, 16)
            load_chunk(0)
            load_xc(0, 0)
            load_x(0, 0)
            sp.dma_start(ident[:, :], a["ident"]).then_inc(consts_in, 16)
            sp.dma_start(consts[:, :], a["consts"]).then_inc(consts_in, 16)
            sp.dma_start(causal[:, :], a["causal"]).then_inc(consts_in, 16)
            sp.dma_start(trig_tab[:, :], a["trig_tab"]).then_inc(consts_in, 16)
            sp.dma_start(b_row[:, :], a["b_gate"]).then_inc(consts_in, 16)
            sp.dma_start(norm0[:, :], a["norm0"].partition_broadcast(P)).then_inc(consts_in, 16)
            sp.dma_start(pos_i[:, :], a["pos"].partition_broadcast(S)).then_inc(consts_in, 16)
            for n in range(1, 4):
                load_chunk(n)
            load_xc(1, 1)
            for n in range(4, len(chunks)):
                load_chunk(n)
            load_xc(2, 2)
            load_x(1, 1)
            with sp.Fori(1, GROUPS - 2) as i:
                load_xc(i + 2, i + 2)
                load_x(i + 1, i + 1)
                store(i - 1, i)
            load_x(GROUPS - 1, GROUPS - 1)
            for g in range(GROUPS - 3, GROUPS):
                store(g, g + 1)
            sp.wait_ge(stored, 16 * GROUPS)

        @block.scalar
        def _(act):
            def split_chunk(n):
                rows = chunks[n][1]
                act.wait_ge(raw_in[n % 2], 16 * (n // 2 + 1))
                for at, count, to, scale in chunks[n][3]:
                    last = act.activation(w_hi[0:rows, to:to + count], stage[0:rows, n % 2, at:at + count],
                                          ACT.Copy, scale=scale)
                last.then_inc(raw_hi, 1)

            def copy(out_, in_, scale=1.0):
                return act.activation(out_, in_, ACT.Copy, scale=scale)

            def square_sum(n, x, junk):
                for t in range(NT):
                    last = act.activation(junk[:, t, :], x[:, t, :], ACT.Square, accum_out=sumsq[:, n, t:t + 1])
                last.then_inc(sq_r[n], 1)

            def split_xc(x):
                act.wait_ge(xc_in, x[0] * 16)
                before(act, kv_mm, x[1])
                copy(xc_hi[:, :, :], xc[:, :, :]).then_inc(xc_hi_r, 1)

            def q0_out(x):
                act.wait_ge(q0_mm, x[0])
                copy(q0, ps[:, X0, 0:TOK], float(D) ** -0.5).then_inc(q0_r, 1)

            def exp0(x):
                act.wait_ge(low0_r, x[0])
                act.activation(p0, p0, ACT.Exp).then_inc(exp0_r, 1)

            def p0t_out(x):
                act.wait_ge(p0t_mm, x[0])
                copy(p0_t, ps[:, X0, 0:P]).then_inc(p0t_r, 1)

            def am_out(x):
                act.wait_ge(am_mm, x[0])
                copy(am_hi[:, :, :], ps[:, X0:X0 + 2, 0:P]).then_inc(am_hi_r, 1)

            def gate(x):
                act.wait_ge(mcz_mm, x[0])
                act.activation(ra[:, :].rearrange("p (t c) -> p t c", t=NT), ps[:, X0:X0 + 2, D:2 * D], ACT.Tanh,
                               scale=0.5).then_inc(tanh_r, 1)

            def squares_fused(x):
                act.wait_ge(fused, x[0])
                square_sum(0, x_res, rb.rearrange("p (t c) -> p t c", t=NT))

            def squares_x1(x):
                act.wait_ge(x1_r, x[0])
                square_sum(1, x_res, rb.rearrange("p (t c) -> p t c", t=NT))

            def split_x1(x):
                act.wait_ge(tx1_mm, x[0])
                copy(ta_hi[:, :, :], ps[:, X0, :]).then_inc(x1_hi, 1)

            def unit_v(x, u):
                if u == 0:
                    act.wait_ge(pickr_r, x[0])
                if u >= 2:
                    act.wait_ge(qkv_r, unit_count(x, u - 1))
                act.wait_ge(unit_mm, unit_count(x, u + 1))
                copy(ra[:, u % 2 * D:(u % 2 + 1) * D], ps[:, (X1, X0)[u % 2], 0:D],
                     pick_r[:, 0, u // 3:u // 3 + 1]).then_inc(vpart, 1)

            def fill_vblk(x):
                act.wait_ge(qkv_r, unit_count(x, UNITS))
                before(act, pv_mm[0], x[1])
                v = qkv[:, :, 2 * D:3 * D].rearrange("p t (h e c) -> p t h e c", h=PAIRS, e=2)
                for b in range(2):
                    for e in range(2):
                        last = copy(vblk[64 * e:64 * e + 64, :, b, :, e * HD:(e + 1) * HD],
                                    v[64 * b:64 * b + 64, :, :, e, :])
                last.then_inc(vb_r, 1)

            def q_out(x):
                act.wait_ge(tq_mm, x[0])
                before(act, s_mm[0][1], x[1])
                copy(q_t[:, :, :], ps[:, X0, :]).then_inc(qt_r, 1)

            def kv_out(x):
                act.wait_ge(kv_mm, x[0])
                before(act, ckb_r, x[1])
                copy(ck_t[:, :], ps[:, X0, 0:TOK])
                before(act, pv_mm[1], x[1])
                cv = ps[:, X0, TOK:2 * TOK].rearrange("p (t h e c) -> p t h e c", t=NT, h=PAIRS, e=2)
                for b in range(2):
                    for e in range(2):
                        last = copy(cvblk[64 * e:64 * e + 64, :, b, :, e * CHD:(e + 1) * CHD],
                                    cv[64 * b:64 * b + 64, :, :, e, :])
                last.then_inc(kv_r, 1)

            def probs(y, k, c):
                act.wait_ge(low_r[k][c], y[0])
                act.activation(sm[:, 2 * c:2 * c + 2, :], sm[:, 2 * c:2 * c + 2, :], ACT.Exp,
                               scale=float((HD, CHD)[k]) ** -0.5).then_inc(exp_r[k][c], 1)

            def probs_t_out(y, k):
                act.wait_ge(pt_mm[k][0], y[0])
                copy(sm[:, 0:2, :], ps[:, 0:2, :]).then_inc(pt_r[k][0], 1)

            def split_ctx(y):
                act.wait_ge(tctx_mm[0], y[0])
                copy(ta_hi[:, :, :], ps[:, 3, :]).then_inc(ctx_hi[0], 1)

            def squares_x2(y):
                act.wait_ge(x2_r, y[0])
                square_sum(2, res, tok)

            def split_ci(y):
                act.wait_ge(tci_mm, y[0])
                copy(tb_hi[:, :, :], ps[:, 2, :]).then_inc(ci_hi, 1)

            def cq_out(y):
                act.wait_ge(cq_mm, y[0])
                copy(tok[:, 0, :], ps[:, 3, 0:TOK]).then_inc(cq_r, 1)

            def split_cctx(y):
                act.wait_ge(tctx_mm[1], y[0])
                copy(tb_hi[:, 0, :], ps[:, 2, 0:TOK]).then_inc(ctx_hi[1], 1)

            def squares_x3(y):
                act.wait_ge(x3_r, y[0])
                square_sum(3, res, tok)

            def copy_res(y):
                before(act, stored, y[1] * 16)
                copy(res_b[:, :, :], res[:, :, :]).then_inc(resb_r, 1)

            def split_mi(y):
                act.wait_ge(tmi_mm, y[0])
                copy(tb_hi[:, :, :], ps[:, 0, :]).then_inc(mi_hi, 1)

            def tanh_gate(m, n):
                act.wait_ge(gu_mm, m[2] + (n + 1))
                if n >= HB:
                    act.wait_ge(h_lo_r, m[2] + (n + 1 - HB))
                r = inner(n)
                act.activation(hb[r, n % HB, :], ps[r, M0 + n % 2, 0:TOK], ACT.Tanh, scale=0.5).then_inc(th_r, 1)

            def split_h(m, n):
                act.wait_ge(h_r, m[2] + (n + 1))
                r = inner(n)
                copy(h_hi[r, n, :], hb[r, n % HB, :]).then_inc(h_hi_r, 1)

            def mlp(m, lo, hi):
                if m is None:
                    return
                for n in range(lo, hi):
                    if n < MT:
                        tanh_gate(m, n)
                    if n > 0:
                        split_h(m, n - 1)

            def turn(x, y, m, prepare=lambda lo, hi: None):
                if x is not None:
                    split_xc(x)
                    q0_out(x)
                mlp(m, 0, 2)
                if y is not None:
                    probs(y, 0, 0)
                    probs(y, 0, 1)
                if x is not None:
                    exp0(x)
                mlp(m, 2, 4)
                if y is not None:
                    probs_t_out(y, 0)
                if x is not None:
                    p0t_out(x)
                mlp(m, 4, 5)
                if x is not None:
                    am_out(x)
                mlp(m, 5, 6)
                if y is not None:
                    split_ctx(y)
                mlp(m, 6, 8)
                if y is not None:
                    squares_x2(y)
                prepare(4, 8)
                if x is not None:
                    gate(x)
                    squares_fused(x)
                mlp(m, 8, MT + 1)
                if x is not None:
                    squares_x1(x)
                if y is not None:
                    split_ci(y)
                if x is not None:
                    split_x1(x)
                if y is not None:
                    cq_out(y)
                if x is not None:
                    unit_v(x, 0)
                    unit_v(x, 1)
                if y is not None:
                    probs(y, 1, 0)
                if x is not None:
                    unit_v(x, 2)
                if y is not None:
                    probs(y, 1, 1)
                if x is not None:
                    unit_v(x, 3)
                if y is not None:
                    probs_t_out(y, 1)
                if x is not None:
                    unit_v(x, 4)
                    unit_v(x, 5)
                    fill_vblk(x)
                if y is not None:
                    split_cctx(y)
                    squares_x3(y)
                if x is not None:
                    q_out(x)
                if y is not None:
                    split_mi(y)
                    copy_res(y)
                if x is not None:
                    kv_out(x)

            act.preload_act_table(ACT.Exp)
            act.wait_ge(consts_in, 16 * 8)
            for n in range(3):
                split_chunk(n)
            act.wait_ge(gm_mm, 1)
            copy(w_hi[:, wcols("gate_m", 0, D)], ps[:, 7, 0:D]).then_inc(gm_hi, 1)
            copy(b_hi[:, :], b_row[:, :])
            act.wait_ge(filled, 1)
            copy(ones_r[:, :], ones_row[:, :]).then_inc(bias_hi, 1)
            act.wait_ge(trig_mm, 1)
            copy(trig[:, :, :], ps[:, 6, 0:2 * HD]).then_inc(trig_ready, 1)
            turn(counts(0), None, None)
            split_chunk(3)
            turn(counts(1), counts(0), None, lambda lo, hi: [split_chunk(n) for n in range(lo, hi)])
            with act.Fori(1, GROUPS - 1) as i:
                base = act.snap((i - 1) * MT)
                turn((i + 2, i + 1), (i + 1, i), (i, i - 1, base))
            turn(None, counts(GROUPS - 1), (*counts(GROUPS - 2), (GROUPS - 2) * MT))
            turn(None, None, (*counts(GROUPS - 1), (GROUPS - 1) * MT))

        @block.vector
        def _(dve):
            def split_chunk(n):
                rows = chunks[n][1]
                dve.wait_ge(raw_in[n % 2], 16 * (n // 2 + 1))
                dve.wait_ge(raw_hi, n + 1)
                for at, count, to, scale in chunks[n][3]:
                    last = dve.scalar_tensor_tensor(
                        out=w_lo[0:rows, to:to + count], in0=stage[0:rows, n % 2, at:at + count], scalar=scale,
                        in1=f32(w_hi[0:rows, to:to + count]), op0=ALU.mult, op1=ALU.subtract)
                last.then_inc(raw_lo, 1)

            def lo_part(out_, full, hi_part):
                return dve.tensor_tensor(out_, full, f32(hi_part), ALU.subtract)

            def weighted_sum(out_, in0, factor, in1, op=ALU.add):
                return dve.scalar_tensor_tensor(out=out_, in0=in0, scalar=factor, in1=in1, op0=ALU.mult, op1=op)

            def variance(n, cur):
                dve.wait_ge(sq_r[n], cur)
                dve.tensor_scalar(var[:, n, :], sumsq[:, n, :], 1.0 / D, EPS, ALU.mult, ALU.add).then_inc(var_r[n], 1)

            def picking(x):
                dve.wait_ge(mask_dma, x[0] * 16)
                dve.tensor_scalar(mask_is1[:, :, :], mask_in[:, :, :], 1.0, None, ALU.is_equal).then_inc(is1, 1)
                dve.wait_ge(is1, x[0])
                dve.scalar_tensor_tensor(out=pick[:, 0, :], in0=mask_is1[:, 0, :], scalar=consts[:, 6:7],
                                         in1=mask_is1[:, 1, :], op0=ALU.mult, op1=ALU.mult).then_inc(pick_v, 1)
                dve.wait_ge(pick_v, x[0])
                dve.tensor_scalar(pick[:, 1, :], pick[:, 0, :], -1.0, 1.0, ALU.mult, ALU.add).then_inc(picks, 1)

            def split_xc(x):
                dve.wait_ge(xc_in, x[0] * 16)
                before(dve, kv_mm, x[1])
                dve.wait_ge(xc_hi_r, x[0])
                lo_part(xc_lo[:, :, :], xc[:, :, :], xc_hi[:, :, :]).then_inc(xc_lo_r, 1)

            sc0 = ps[:, X1, 0:P].rearrange("p (t s) -> p t s", s=S)
            p0v = p0.rearrange("p (t s) -> p t s", s=S)

            def softmax0_a(x):
                dve.wait_ge(sc0_mm, x[0])
                dve.tensor_reduce(top0[:, :], sc0, AX_X, ALU.max).then_inc(top0_r, 1)
                dve.wait_ge(top0_r, x[0])
                dve.tensor_tensor(p0v, sc0, top0[:, :].unsqueeze(2).to_broadcast([P, NT, S]),
                                  ALU.subtract).then_inc(low0_r, 1)

            def softmax0_b(x):
                dve.wait_ge(exp0_r, x[0])
                dve.tensor_reduce(sum0[:, 0, :], p0v, AX_X, ALU.add).then_inc(sum0_r, 1)
                dve.wait_ge(sum0_r, x[0])
                dve.reciprocal(sum0[:, 1, :], sum0[:, 0, :]).then_inc(inv0_r, 1)
                dve.wait_ge(inv0_r, x[0])
                dve.tensor_tensor(p0v, p0v, sum0[:, 1, :].unsqueeze(2).to_broadcast([P, NT, S]),
                                  ALU.mult).then_inc(p0_r, 1)

            def am_out(x):
                dve.wait_ge(am_hi_r, x[0])
                lo_part(am_lo[:, :, :], ps[:, X0:X0 + 2, 0:P], am_hi[:, :, :]).then_inc(am_lo_r, 1)

            def fuse(x):
                g = ra[:, :].rearrange("p (t c) -> p t c", t=NT)
                dve.wait_ge(tanh_r, x[0])
                dve.scalar_tensor_tensor(out=g, in0=g, scalar=1.0, in1=ps[:, X0:X0 + 2, 0:D],
                                         op0=ALU.add, op1=ALU.mult).then_inc(gated, 1)
                dve.wait_ge(gated, x[0])
                dve.wait_ge(xres_in, x[0] * 16)
                weighted_sum(x_res[:, :, :], g, 0.5, x_res[:, :, :]).then_inc(fused, 1)

            def norm_fused(x):
                dve.wait_ge(rms_r[0], x[0])
                for t in range(NT):
                    last = dve.scalar_tensor_tensor(out=x_res[:, t, :], in0=x_res[:, t, :], scalar=rms[:, 0, t:t + 1],
                                                    in1=norm0[:, :], op0=ALU.mult, op1=ALU.mult)
                last.then_inc(x1_r, 1)

            def split_x1(x):
                dve.wait_ge(x1_hi, x[0])
                lo_part(ta_lo[:, :, :], ps[:, X0, :], ta_hi[:, :, :]).then_inc(x1_lo, 1)

            def factors(x):
                dve.wait_ge(rms_r[1], x[0])
                dve.wait_ge(picks, x[0])
                dve.tensor_tensor(pick_r[:, :, :], pick[:, :, :],
                                  rms[:, 1, :].unsqueeze(1).to_broadcast([P, 2, NT]), ALU.mult).then_inc(pickr_r, 1)

            def unit_l(x, u):
                t, n = divmod(u, 3)
                dve.wait_ge(pickr_r, x[0])
                dve.wait_ge(vpart, unit_count(x, u + 1))
                weighted_sum(qkv[:, t, n * D:(n + 1) * D], ps[:, (X1, X0)[u % 2], D:2 * D], pick_r[:, 1, t:t + 1],
                             ra[:, u % 2 * D:(u % 2 + 1) * D]).then_inc(qkv_r, 1)

            def rotary(x, t):
                if t == 0:
                    dve.wait_ge(qkv_r, unit_count(x, UNITS))
                else:
                    dve.wait_ge(rope_r, tile_count(x, t - 1))
                qk = qkv[:, t, 0:2 * D]
                dve.tensor_tensor(ra[:, :].rearrange("p (h c) -> p h c", c=HD), qk.rearrange("p (h c) -> p h c", c=HD),
                                  trig[:, 0, :].unsqueeze(1).to_broadcast([P, 2 * HEADS, HD]),
                                  ALU.mult).then_inc(rope_c, 1)
                dve.wait_ge(rope_c, tile_count(x, t))
                dve.wait_ge(rope_s, tile_count(x, t))
                dve.tensor_tensor(qk, ra[:, :], rb[:, :], ALU.add).then_inc(rope_r, 1)

            def k_out(x):
                dve.wait_ge(tk_mm, x[0])
                before(dve, s_mm[1][1], x[1])
                kb = kblk[:, :, :].rearrange("p (m e) c -> p m e c", e=2)
                for e in range(2):
                    last = dve.tensor_scalar(kb[:, :, e, :], ps[:, X1, :].rearrange("p (m c) -> p m c", m=2),
                                             consts[:, e:e + 1], None, ALU.mult)
                last.then_inc(kb_r, 1)

            def own_picks(y):
                dve.wait_ge(picks, y[0])
                before(dve, pickb_r, y[1])
                dve.tensor_copy(pick_y[:, :, :], pick[:, :, :]).then_inc(picky_r, 1)

            def mask_scores(y, c):
                dve.wait_ge(s_mm[0][c], y[0])
                dve.tensor_tensor(groups(sm, c), groups(ps, c), causal[:, :].unsqueeze(1).to_broadcast([P, 16, S]),
                                  ALU.add).then_inc(masked[c], 1)

            def less_top(y, k, c):
                src = groups(ps if k else sm, c)
                dve.wait_ge(s_mm[1][c] if k else masked[c], y[0])
                dve.tensor_reduce(top[:, 16 * c:16 * c + 16], src, AX_X, ALU.max).then_inc(top_r[k][c], 1)
                dve.wait_ge(top_r[k][c], y[0])
                dve.tensor_tensor(groups(sm, c), src, top[:, 16 * c:16 * c + 16].unsqueeze(2).to_broadcast([P, 16, S]),
                                  ALU.subtract).then_inc(low_r[k][c], 1)

            def probs_t_out(y, k):
                dve.wait_ge(pt_mm[k][1], y[0])
                dve.tensor_copy(sm[:, 2:4, :], ps[:, 2:4, :]).then_inc(pt_r[k][1], 1)

            def context(y, k):
                width, block_ = (HD, CHD)[k], (VB, CVB)[k]
                dve.wait_ge(pv_mm[k], y[0])
                pv = ps[:, 0:NT, 0:PAIRS * block_].rearrange("p t (h c) -> p t h c", c=block_)
                dve.reciprocal(inv[:, :, :, :], pv[:, :, :, 2 * width:block_]).then_inc(inv_r[k], 1)
                dve.wait_ge(inv_r[k], y[0])
                to = tok[:, :, 0:HEADS * width].rearrange("p t (h e c) -> p t h e c", h=PAIRS, e=2)
                for e in range(2):
                    last = dve.tensor_tensor(to[:, :, :, e, :], pv[:, :, :, e * width:(e + 1) * width],
                                             inv[:, :, :, e:e + 1].to_broadcast([P, NT, PAIRS, width]), ALU.mult)
                last.then_inc(ctx_r[k], 1)

            def split_ctx(y):
                dve.wait_ge(ctx_hi[0], y[0])
                lo_part(ta_lo[:, :, :], ps[:, 3, :], ta_hi[:, :, :]).then_inc(ctx_lo[0], 1)

            def add_dense(y):
                dve.wait_ge(picky_r, y[0])
                for t in range(NT):
                    dve.wait_ge(dense_mm, tile_count(y, t))
                    weighted_sum(res[:, t, :], ps[:, t, 0:D], pick_y[:, 0, t:t + 1], x_res[:, t, :]).then_inc(res_v, 1)
                    dve.wait_ge(res_v, tile_count(y, t))
                    last = weighted_sum(res[:, t, :], ps[:, t, D:2 * D], pick_y[:, 1, t:t + 1], res[:, t, :])
                last.then_inc(x2_r, 1)

            def split_ci(y):
                dve.wait_ge(ci_hi, y[0])
                lo_part(tb_lo[:, :, :], ps[:, 2, :], tb_hi[:, :, :]).then_inc(ci_lo, 1)

            def ck_blocks(y):
                dve.wait_ge(kv_r, y[0])
                dve.wait_ge(s_mm[0][1], y[0])
                for m in range(4):
                    last = dve.tensor_scalar(kblk[:, m, :], ck_t[:, :], consts[:, 2 + m:3 + m], None, ALU.mult)
                last.then_inc(ckb_r, 1)

            def split_cctx(y):
                dve.wait_ge(ctx_hi[1], y[0])
                lo_part(tb_lo[:, 0, :], ps[:, 2, 0:TOK], tb_hi[:, 0, :]).then_inc(ctx_lo[1], 1)

            def add_cross(y):
                dve.wait_ge(cd_mm, y[0])
                dve.tensor_tensor(res[:, :, :], ps[:, 3, :], res[:, :, :].rearrange("p t c -> p (t c)"),
                                  ALU.add).then_inc(x3_r, 1)

            def split_mi(y):
                dve.wait_ge(mi_hi, y[0])
                lo_part(tb_lo[:, :, :], ps[:, 0, :], tb_hi[:, :, :]).then_inc(mi_lo, 1)

            def mlp_picks(y):
                dve.wait_ge(y_r, y[1] + 1)
                dve.tensor_copy(pick_b[:, :, :], pick_y[:, :, :]).then_inc(pickb_r, 1)

            def mlp(m, lo, hi):
                if m is None:
                    return
                for n in range(lo, hi):
                    r = inner(n)
                    bank, h = ps[r, M0 + n % 2, :], hb[r, n % HB, :]
                    dve.wait_ge(th_r, m[2] + (n + 1))
                    dve.scalar_tensor_tensor(out=h, in0=h, scalar=1.0, in1=bank[:, 0:TOK],
                                             op0=ALU.add, op1=ALU.mult).then_inc(tg_r, 1)
                    dve.wait_ge(tg_r, m[2] + (n + 1))
                    dve.tensor_tensor(h, h, bank[:, TOK:2 * TOK], ALU.mult).then_inc(h_r, 1)

            def result(m):
                dve.wait_ge(resb_r, m[0])
                dve.wait_ge(pickb_r, m[0])
                for t in range(NT):
                    dve.wait_ge(down_mm, tile_count(m, t))
                    weighted_sum(res_b[:, t, :], ps[:, M0 + t, 0:D], pick_b[:, 0, t:t + 1],
                                 res_b[:, t, :]).then_inc(y_v, 1)
                    dve.wait_ge(y_v, tile_count(m, t))
                    last = weighted_sum(res_b[:, t, :], ps[:, M0 + t, D:2 * D], pick_b[:, 1, t:t + 1], res_b[:, t, :])
                last.then_inc(y_r, 1)

            def turn(x, y, m, prepare=lambda lo, hi: None):
                if y is not None:
                    own_picks(y)
                if x is not None:
                    split_xc(x)
                    picking(x)
                if y is not None:
                    mask_scores(y, 0)
                    less_top(y, 0, 0)
                    mask_scores(y, 1)
                    less_top(y, 0, 1)
                mlp(m, 0, 2)
                if x is not None:
                    softmax0_a(x)
                    softmax0_b(x)
                mlp(m, 2, 4)
                if y is not None:
                    probs_t_out(y, 0)
                mlp(m, 4, 5)
                if y is not None:
                    context(y, 0)
                if x is not None:
                    am_out(x)
                mlp(m, 5, 6)
                if y is not None:
                    split_ctx(y)
                mlp(m, 6, 8)
                if y is not None:
                    add_dense(y)
                    variance(2, y[0])
                prepare(4, 8)
                if x is not None:
                    fuse(x)
                    variance(0, x[0])
                mlp(m, 8, MT)
                if x is not None:
                    norm_fused(x)
                    variance(1, x[0])
                if y is not None:
                    split_ci(y)
                    ck_blocks(y)
                if x is not None:
                    split_x1(x)
                    factors(x)
                    unit_l(x, 0)
                if y is not None:
                    less_top(y, 1, 0)
                if x is not None:
                    unit_l(x, 1)
                    unit_l(x, 2)
                if y is not None:
                    less_top(y, 1, 1)
                if x is not None:
                    unit_l(x, 3)
                if y is not None:
                    probs_t_out(y, 1)
                if x is not None:
                    unit_l(x, 4)
                    unit_l(x, 5)
                if y is not None:
                    context(y, 1)
                if x is not None:
                    rotary(x, 0)
                if y is not None:
                    split_cctx(y)
                    add_cross(y)
                    variance(3, y[0])
                if x is not None:
                    rotary(x, 1)
                if m is not None:
                    result(m)
                if x is not None:
                    k_out(x)
                if y is not None:
                    mlp_picks(y)
                    split_mi(y)

            dve.memset(vblk[:, :, :, :, :], 0.0)
            dve.memset(cvblk[:, :, :, :, :], 0.0)
            dve.memset(ones_row[:, :], 1.0)
            dve.memset(minus_half[:, :], -0.5).then_inc(zeroed, 1)
            dve.wait_ge(zeroed, 1)
            for e in range(2):
                dve.memset(vblk[64 * e:64 * e + 64, :, :, :, 2 * HD + e:2 * HD + e + 1], 1.0)
                last = dve.memset(cvblk[64 * e:64 * e + 64, :, :, :, 2 * CHD + e:2 * CHD + e + 1], 1.0)
            last.then_inc(filled, 1)
            dve.memset(pick_b[:, :, :], 0.0).then_inc(y_r, 1)
            dve.wait_ge(consts_in, 16 * 8)
            dve.tensor_copy(pos_f[:, :], pos_i[:, :]).then_inc(pos_done, 1)
            dve.wait_ge(pos_done, 1)
            dve.tensor_scalar(pos_neg[:, :], pos_f[:, :], 0.0, float(S), ALU.is_lt, ALU.mult).then_inc(pos_done, 1)
            dve.wait_ge(pos_done, 2)
            dve.tensor_tensor(pos_f[:, :], pos_f[:, :], pos_neg[:, :], ALU.add).then_inc(pos_done, 1)
            dve.wait_ge(pos_done, 3)
            dve.tensor_scalar(pos_f[:, :], pos_f[:, :], 0.0, float(S - 1), ALU.max, ALU.min).then_inc(pos_done, 1)
            dve.wait_ge(pos_done, 4)
            dve.tensor_scalar(onehot[:, :, :], pos_f[:, :].unsqueeze(1).to_broadcast([S, 2, S]),
                              consts[0:S, 7:8], None, ALU.is_equal).then_inc(pos_done, 1)
            for n in range(3):
                split_chunk(n)
            dve.wait_ge(gm_hi, 1)
            lo_part(w_lo[:, wcols("gate_m", 0, D)], ps[:, 7, 0:D], w_hi[:, wcols("gate_m", 0, D)]).then_inc(gm_lo, 1)
            dve.wait_ge(bias_hi, 1)
            lo_part(b_lo[:, :], b_row[:, :], b_hi[:, :]).then_inc(bias_lo, 1)
            dve.wait_ge(trig_ready, 1)
            turn(counts(0), None, None)
            split_chunk(3)
            turn(counts(1), counts(0), None, lambda lo, hi: [split_chunk(n) for n in range(lo, hi)])
            with dve.Fori(1, GROUPS - 1) as i:
                base = dve.snap((i - 1) * MT)
                turn((i + 2, i + 1), (i + 1, i), (i, i - 1, base))
            turn(None, counts(GROUPS - 1), (*counts(GROUPS - 2), (GROUPS - 2) * MT))
            turn(None, None, (*counts(GROUPS - 1), (GROUPS - 1) * MT))

        @block.gpsimd
        def _(pool):
            def root(n, cur):
                pool.wait_ge(var_r[n], cur)
                pool.tensor_tensor(rms[:, n, :], var[:, n, :], minus_half[:, :], ALU.pow).then_inc(rms_r[n], 1)

            def rotary(x, t):
                q = qkv[:, t, 0:2 * D].rearrange("p (h e c) -> p h e c", h=2 * HEADS, e=2)
                r = rb[:, :].rearrange("p (h e c) -> p h e c", h=2 * HEADS, e=2)
                if t == 0:
                    pool.wait_ge(qkv_r, unit_count(x, 2))
                else:
                    pool.wait_ge(qkv_r, unit_count(x, 5))
                    pool.wait_ge(rope_r, tile_count(x, t - 1))
                for e in range(2):
                    sin = trig[:, 1, e * HD // 2:(e + 1) * HD // 2]
                    last = pool.tensor_tensor(r[:, :, e, :], q[:, :, 1 - e, :],
                                              sin.unsqueeze(1).to_broadcast([P, 2 * HEADS, HD // 2]), ALU.mult)
                last.then_inc(rope_s, 1)

            def normed(y, n, done):
                pool.wait_ge(rms_r[n], y[0])
                pool.tensor_tensor(tok[:, :, :], res[:, :, :], rms[:, n, :].unsqueeze(2).to_broadcast([P, NT, D]),
                                   ALU.mult).then_inc(done, 1)

            def mlp(m, lo, hi):
                if m is None:
                    return
                for n in range(lo, hi):
                    r = inner(n)
                    pool.wait_ge(h_hi_r, m[2] + (n + 1))
                    pool.tensor_tensor(h_lo[r, n, :], hb[r, n % HB, :], f32(h_hi[r, n, :]),
                                       ALU.subtract).then_inc(h_lo_r, 1)

            def turn(x, y, m):
                mlp(m, 0, 6)
                if y is not None:
                    root(2, y[0])
                    normed(y, 2, ci_r)
                if x is not None:
                    root(0, x[0])
                mlp(m, 6, MT)
                if x is not None:
                    root(1, x[0])
                    rotary(x, 0)
                if y is not None:
                    root(3, y[0])
                    normed(y, 3, mi_r)
                if x is not None:
                    rotary(x, 1)

            pool.wait_ge(trig_ready, 1)
            turn(counts(0), None, None)
            turn(counts(1), counts(0), None)
            with pool.Fori(1, GROUPS - 1) as i:
                base = pool.snap((i - 1) * MT)
                turn((i + 2, i + 1), (i + 1, i), (i, i - 1, base))
            turn(None, counts(GROUPS - 1), (*counts(GROUPS - 2), (GROUPS - 2) * MT))
            turn(None, None, (*counts(GROUPS - 1), (GROUPS - 1) * MT))

        @block.tensor
        def _(pe):
            def product(o, lh, ll, rh, rl, start=False, stop=False):
                pe.matmul(o, lh, rh, start=start, stop=False, skip_group_check=True)
                pe.matmul(o, lh, rl, start=False, stop=False, skip_group_check=True)
                return pe.matmul(o, ll, rh, start=False, stop=stop, skip_group_check=True)

            def single(o, lhs, rhs):
                return pe.matmul(o, lhs, rhs, start=True, stop=True, skip_group_check=True)

            def transposes(bank, src):
                for t in range(NT):
                    for k in range(src.shape[2] // P):
                        last = pe.transpose(ps[:, bank, k * TOK + t * P:k * TOK + (t + 1) * P],
                                            src[:, t, k * P:(k + 1) * P], ident[:, :])
                return last

            def q0_product(x):
                pe.wait_ge(xc_hi_r, x[0])
                pe.wait_ge(xc_lo_r, x[0])
                before(pe, kv_r, x[1])
                for k in range(KD):
                    w = wcols("mem", k * C, C)
                    last = product(ps[:, X0, 0:TOK], w_hi[:, w], w_lo[:, w], xc_hi[:, k, :], xc_lo[:, k, :],
                                   k == 0, k == KD - 1)
                last.then_inc(q0_mm, 1)

            def scores0(x):
                pe.wait_ge(q0_r, x[0])
                before(pe, kb_r, x[1])
                for t in range(NT):
                    for b in range(2):
                        c = slice(t * P + b * S, t * P + (b + 1) * S)
                        last = single(ps[64 * b:64 * b + 64, X1, t * S:(t + 1) * S], q0[:, c], xc[:, KD, c])
                last.then_inc(sc0_mm, 1)

            def probs0_t(x):
                pe.wait_ge(p0_r, x[0])
                pe.transpose(ps[:, X0, 0:P], p0, ident[:, :]).then_inc(p0t_mm, 1)

            def attend0(x):
                pe.wait_ge(p0t_r, x[0])
                pe.wait_ge(ctok_in, x[0] * 16)
                for t in range(NT):
                    r = slice(64 * t, 64 * t + 64)
                    for b in range(2):
                        last = single(ps[:, X0 + t, b * S:(b + 1) * S], ctx_tok[r, b, :], p0_t[r, b * S:(b + 1) * S])
                last.then_inc(am_mm, 1)

            def context_gate(x):
                pe.wait_ge(am_hi_r, x[0])
                pe.wait_ge(am_lo_r, x[0])
                for t in range(NT):
                    w = wcols("mem_t", 0, 2 * D)
                    product(ps[:, X0 + t, :], am_hi[:, t, :], am_lo[:, t, :], w_hi[:, w], w_lo[:, w], True, False)
                    z = ps[:, X0 + t, D:2 * D]
                    for k in range(KD):
                        w = wcols("gate_x", k * D, D)
                        product(z, of_tile(xc_hi[:, k, :], t), of_tile(xc_lo[:, k, :], t), w_hi[:, w], w_lo[:, w])
                    pe.matmul(z, ones_r[:, :], b_hi[:, :], start=False, stop=False, skip_group_check=True)
                    last = pe.matmul(z, ones_r[:, :], b_lo[:, :], start=False, stop=True, skip_group_check=True)
                last.then_inc(mcz_mm, 1)

            def x1_t(x):
                pe.wait_ge(x1_r, x[0])
                transposes(X0, x_res).then_inc(tx1_mm, 1)

            def unit(x, u):
                t, n = divmod(u, 3)
                if u == 0:
                    pe.wait_ge(x1_hi, x[0])
                    pe.wait_ge(x1_lo, x[0])
                if u >= 2:
                    pe.wait_ge(qkv_r, unit_count(x, u - 1))
                for k in range(KD):
                    w = wcols("qkv", k * 6 * D + n * 2 * D, 2 * D)
                    last = product(ps[:, (X1, X0)[u % 2], :], of_tile(ta_hi[:, k, :], t), of_tile(ta_lo[:, k, :], t),
                                   w_hi[:, w], w_lo[:, w], k == 0, k == KD - 1)
                last.then_inc(unit_mm, 1)

            def qk_t(x):
                pe.wait_ge(rope_r, tile_count(x, NT - 1))
                transposes(X0, qkv[:, :, 0:D]).then_inc(tq_mm, 1)
                transposes(X1, qkv[:, :, D:2 * D]).then_inc(tk_mm, 1)

            def ctx_kv(x):
                pe.wait_ge(qt_r, x[0])
                w = wcols("ckv", 0, C)
                product(ps[:, X0, 0:TOK], w_hi[:, w], w_lo[:, w], xc_hi[:, KD, :], xc_lo[:, KD, :], True, True)
                w = wcols("ckv", C, C)
                for t in range(NT):
                    last = product(ps[:, X0, TOK + t * P:TOK + (t + 1) * P], of_tile(xc_hi[:, KD, :], t),
                                   of_tile(xc_lo[:, KD, :], t), w_hi[:, w], w_lo[:, w], True, True)
                last.then_inc(kv_mm, 1)

            def scores(y, c):
                if c == 0:
                    pe.wait_ge(qt_r, y[0])
                    pe.wait_ge(kb_r, y[0])
                    before(pe, mi_lo, y[1])
                kb = kblk[:, :, :].rearrange("p (m e) c -> p m e c", e=2)
                for m in range(2):
                    for t in range(NT):
                        for j in (2 * c, 2 * c + 1):
                            for b in range(2):
                                r, tk = slice(32 * j, 32 * j + 32), slice(t * P + b * S, t * P + (b + 1) * S)
                                last = single(ps[64 * b:64 * b + 64, j, (2 * m + t) * P:(2 * m + t + 1) * P],
                                              q_t[r, m, tk], kb[r, m, :, tk])
                last.then_inc(s_mm[0][c], 1)

            def cross_scores(y, c):
                if c == 0:
                    pe.wait_ge(cq_r, y[0])
                    pe.wait_ge(ckb_r, y[0])
                for t in range(NT):
                    for j in (2 * c, 2 * c + 1):
                        for b in range(2):
                            r, tk = slice(32 * j, 32 * j + 32), slice(t * P + b * S, t * P + (b + 1) * S)
                            last = single(ps[64 * b:64 * b + 64, j, t * 2 * P:(t + 1) * 2 * P],
                                          tok[r, 0, tk], kblk[r, :, tk])
                last.then_inc(s_mm[1][c], 1)

            def probs_t(y, k, c):
                pe.wait_ge(exp_r[k][c], y[0])
                for j in (2 * c, 2 * c + 1):
                    for n in range(4):
                        last = pe.transpose(ps[:, j, n * P:(n + 1) * P], sm[:, j, n * P:(n + 1) * P], ident[:, :])
                last.then_inc(pt_mm[k][c], 1)

            def values(y, k):
                pe.wait_ge(vb_r if k == 0 else kv_r, y[0])
                pe.wait_ge(pt_r[k][0], y[0])
                pe.wait_ge(pt_r[k][1], y[0])
                blocks, width = ((vblk, VB), (cvblk, CVB))[k]
                for t in range(NT):
                    for h in range(PAIRS):
                        j, n = (h % 4, 2 * (h // 4) + t) if k == 0 else (h // 2, 2 * t + h % 2)
                        for b in range(2):
                            last = single(ps[64 * b:64 * b + 64, t, h * width:(h + 1) * width],
                                          sm[:, j, n * P + b * S:n * P + (b + 1) * S], blocks[:, t, b, h, :])
                last.then_inc(pv_mm[k], 1)

            def context_t(y):
                pe.wait_ge(ctx_r[0], y[0])
                transposes(3, tok).then_inc(tctx_mm[0], 1)

            def dense(y, t):
                pe.wait_ge(ctx_hi[0], y[0])
                pe.wait_ge(ctx_lo[0], y[0])
                for k in range(KD):
                    w = wcols("dense", k * 2 * D, 2 * D)
                    last = product(ps[:, t, :], of_tile(ta_hi[:, k, :], t), of_tile(ta_lo[:, k, :], t),
                                   w_hi[:, w], w_lo[:, w], k == 0, k == KD - 1)
                last.then_inc(dense_mm, 1)

            def cross_input_t(y):
                pe.wait_ge(ci_r, y[0])
                transposes(2, tok).then_inc(tci_mm, 1)

            def cross_q(y):
                pe.wait_ge(ci_hi, y[0])
                pe.wait_ge(ci_lo, y[0])
                for k in range(KD):
                    w = wcols("cq", k * C, C)
                    last = product(ps[:, 3, 0:TOK], w_hi[:, w], w_lo[:, w], tb_hi[:, k, :], tb_lo[:, k, :],
                                   k == 0, k == KD - 1)
                last.then_inc(cq_mm, 1)

            def cross_context_t(y):
                pe.wait_ge(ctx_r[1], y[0])
                transposes(2, tok[:, :, 0:C]).then_inc(tctx_mm[1], 1)

            def cross_dense(y):
                pe.wait_ge(ctx_hi[1], y[0])
                pe.wait_ge(ctx_lo[1], y[0])
                w = wcols("cdense", 0, D)
                for t in range(NT):
                    last = product(ps[:, 3, t * D:(t + 1) * D], of_tile(tb_hi[:, 0, :], t), of_tile(tb_lo[:, 0, :], t),
                                   w_hi[:, w], w_lo[:, w], True, True)
                last.then_inc(cd_mm, 1)

            def mlp_input_t(y):
                pe.wait_ge(mi_r, y[0])
                transposes(0, tok).then_inc(tmi_mm, 1)

            def gate_up(m, lo, hi):
                if m is None:
                    return
                if lo == 0:
                    pe.wait_ge(mi_hi, m[0])
                    pe.wait_ge(mi_lo, m[0])
                for n in range(lo, hi):
                    width = P if n < 2 * FULL else 2 * LEFT
                    if n < 2:
                        pe.wait_ge(y_r, m[1] + 1)
                    else:
                        pe.wait_ge(h_r, m[2] + (n - 1))
                    for u in range(2):
                        for k in range(KD):
                            w = wcols("gu", k * GU + n * 2 * P + u * width, width)
                            last = product(ps[0:width, M0 + n % 2, u * TOK:(u + 1) * TOK], w_hi[:, w], w_lo[:, w],
                                           tb_hi[:, k, :], tb_lo[:, k, :], k == 0, k == KD - 1)
                    last.then_inc(gu_mm, 1)

            def down(m, t):
                if m is None:
                    return
                if t == 0:
                    pe.wait_ge(h_r, m[2] + MT)
                    pe.wait_ge(h_hi_r, m[2] + MT)
                    pe.wait_ge(h_lo_r, m[2] + MT)
                r = slice(0, 2 * LEFT)
                w = wcols("down_left", 0, 2 * D)
                product(ps[:, M0 + t, :], of_tile(h_hi[r, MT - 1, :], t), of_tile(h_lo[r, MT - 1, :], t),
                        w_hi[r, w], w_lo[r, w], True)
                for n in range(2 * FULL):
                    w, e = wcols("down", n * D, D), n // FULL
                    last = product(ps[:, M0 + t, e * D:(e + 1) * D], of_tile(h_hi[:, n, :], t), of_tile(h_lo[:, n, :], t),
                                   w_hi[:, w], w_lo[:, w], False, n == 2 * FULL - 1)
                last.then_inc(down_mm, 1)

            def turn(x, y, m):
                if y is not None:
                    scores(y, 0)
                if x is not None:
                    q0_product(x)
                if y is not None:
                    scores(y, 1)
                gate_up(m, 0, 2)
                if x is not None:
                    scores0(x)
                gate_up(m, 2, 4)
                if y is not None:
                    probs_t(y, 0, 0)
                if x is not None:
                    probs0_t(x)
                if y is not None:
                    probs_t(y, 0, 1)
                gate_up(m, 4, 5)
                if y is not None:
                    values(y, 0)
                if x is not None:
                    attend0(x)
                gate_up(m, 5, 6)
                if y is not None:
                    context_t(y)
                gate_up(m, 6, 8)
                if y is not None:
                    dense(y, 0)
                    dense(y, 1)
                if x is not None:
                    context_gate(x)
                gate_up(m, 8, MT)
                if y is not None:
                    cross_input_t(y)
                if x is not None:
                    x1_t(x)
                if y is not None:
                    cross_q(y)
                if x is not None:
                    unit(x, 0)
                if y is not None:
                    cross_scores(y, 0)
                    cross_scores(y, 1)
                if x is not None:
                    unit(x, 1)
                    unit(x, 2)
                    unit(x, 3)
                if y is not None:
                    probs_t(y, 1, 0)
                    probs_t(y, 1, 1)
                if x is not None:
                    unit(x, 4)
                if y is not None:
                    values(y, 1)
                if x is not None:
                    unit(x, 5)
                if y is not None:
                    cross_context_t(y)
                down(m, 0)
                if y is not None:
                    cross_dense(y)
                down(m, 1)
                if x is not None:
                    qk_t(x)
                if y is not None:
                    mlp_input_t(y)
                if x is not None:
                    ctx_kv(x)

            pe.wait_ge(consts_in, 16 * 8)
            pe.wait_ge(pos_done, 5)
            pe.matmul(ps[:, 6, 0:2 * HD], onehot[:, :, :], trig_tab[:, :], start=True, stop=True).then_inc(trig_mm, 1)
            pe.wait_ge(raw_in[0], 16)
            for k in range(KD):
                last = pe.matmul(ps[:, 7, 0:D], raw_mem[:, k * C:(k + 1) * C], raw_gate_m[:, k * D:(k + 1) * D],
                                 start=(k == 0), stop=(k == KD - 1))
            last.then_inc(gm_mm, 1)
            pe.wait_ge(raw_lo, 3)
            pe.wait_ge(gm_lo, 1)
            pe.wait_ge(bias_lo, 1)
            turn(counts(0), None, None)
            pe.wait_ge(raw_lo, 4)
            turn(counts(1), counts(0), None)
            pe.wait_ge(raw_lo, len(chunks))
            with pe.Fori(1, GROUPS - 1) as i:
                base = pe.snap((i - 1) * MT)
                turn((i + 2, i + 1), (i + 1, i), (i, i - 1, base))
            turn(None, counts(GROUPS - 1), (*counts(GROUPS - 2), (GROUPS - 2) * MT))
            turn(None, None, (*counts(GROUPS - 1), (GROUPS - 1) * MT))


def kernel(**inputs):
    import numpy as np
    import concourse.bacc as bacc
    from concourse.bass_utils import run_bass_kernel_spmd as run

    v = {n: np.ascontiguousarray(x) for n, x in inputs.items()}

    def by_k(w):
        return w.reshape(-1, P, w.shape[1]).transpose(1, 0, 2).reshape(P, -1)

    x, cx = v["x"].reshape(GROUPS, TOK, D), v["ctx_1024"].reshape(GROUPS, TOK, C)
    x_t = x.transpose(0, 2, 1).reshape(GROUPS, KD, P, TOK).transpose(0, 2, 1, 3)
    xc = np.concatenate([x_t, cx.transpose(0, 2, 1)[:, :, None, :]], axis=2)
    x_tok = x.reshape(GROUPS, NT, P, D).transpose(0, 2, 1, 3)
    ctx_tok = cx.reshape(GROUPS, NT, 2, S, C).transpose(0, 1, 3, 2, 4).reshape(GROUPS, P, 2, C)
    types = v["mask_BxS_ik0"].reshape(-1)
    mask = np.stack([types, np.roll(types, -1)]).reshape(2, GROUPS, NT, P).transpose(1, 3, 0, 2)
    wm, wg = v["L0_xattn_W_mem"], v["L0_xattn_W_gate"].T
    w_first = np.concatenate([by_k(wm), by_k(wg[:D]), wm.T, v["L1_xattn_ckv_w"], by_k(v["L1_xattn_cq_w"]),
                              by_k(wg[D:])], axis=1)
    w_qkv = np.concatenate([v[f"L1_xattn_{e}_qkv"][:, n * D:(n + 1) * D] for n in range(3) for e in "vl"],
                           axis=1).reshape(KD, P, 6 * D)
    w_dense = np.concatenate([by_k(np.concatenate([v["L1_xattn_v_dense"], v["L1_xattn_l_dense"]], axis=1)),
                              v["L1_xattn_cdense_w"]], axis=1)
    gates, ups = ([v[f"L1_xattn_{e}_{n}"] for e in "vl"] for n in ("gate", "up"))
    cols, cut = [], FULL * P
    for e in range(2):
        for n in range(FULL):
            cols += [w[e][:, n * P:(n + 1) * P] for w in (gates, ups)]
    cols += [w[e][:, cut:] for w in (gates, ups) for e in range(2)]
    w_gu = np.concatenate(cols, axis=1).reshape(KD, P, GU)
    downs = [v["L1_xattn_v_down"], v["L1_xattn_l_down"]]
    w_down = by_k(np.concatenate([w[:cut] for w in downs], axis=0))
    w_down_left = np.zeros((2 * LEFT, 2 * D), np.float32)
    for e in range(2):
        w_down_left[e * LEFT:(e + 1) * LEFT, e * D:(e + 1) * D] = downs[e][cut:]
    ln = np.stack([v[f"L1_xattn_ln_{n}_w"].reshape(KD, P).T for n in ("in", "post_cross", "post_attn")], axis=1)
    p = np.arange(P)
    consts = np.zeros((P, 8), np.float32)
    for e in range(2):
        consts[:, e] = p // HD % 2 == e
    for m in range(4):
        consts[:, 2 + m] = p // CHD % 4 == m
    consts[:, 6] = p % S != S - 1
    consts[:, 7] = p
    causal = np.where(np.arange(S)[None, :] <= (p % S)[:, None], 0.0, MASKED).astype(np.float32)
    inv_freq = (1.0 / np.float32(10000.0) ** (np.arange(0, HD, 2, dtype=np.float32) / np.float32(HD))).astype(np.float32)
    angle = np.outer(np.arange(S, dtype=np.float32), inv_freq).astype(np.float32)
    cos, sin = np.cos(angle), np.sin(angle)
    trig_tab = np.concatenate([cos, cos, -sin, sin], axis=1).astype(np.float32)

    arrays = {
        "xc": xc, "x_tok": x_tok, "ctx_tok": ctx_tok, "mask": mask, "w_first": w_first, "w_qkv": w_qkv,
        "w_dense": w_dense, "w_gu": w_gu, "w_down": w_down, "w_down_left": w_down_left, "ln": ln,
        "ident": np.eye(P, dtype=np.float32), "consts": consts, "causal": causal, "trig_tab": trig_tab,
        "b_gate": v["L0_xattn_b_gate"].reshape(1, D), "norm0": v["L0_xattn_norm_w"], "pos": v["pos_1xS"].reshape(S),
    }
    arrays = {n: np.ascontiguousarray(x) for n, x in arrays.items()}
    nc = bacc.Bacc("TRN2", target_bir_lowering=False, num_devices=1)
    a = {n: nc.dram_tensor(f"in_{n}", x.shape, mybir.dt.from_np(x.dtype), kind="ExternalInput").ap()
         for n, x in arrays.items()}
    out = nc.dram_tensor("out_y", (GROUPS, P, NT, D), F32, kind="ExternalOutput").ap()
    build_program(nc, a, out)
    r = run(nc, [{f"in_{n}": x for n, x in arrays.items()}], core_ids=[0])
    y = r.results[0]["out_y"]
    return y.transpose(0, 2, 1, 3).reshape(B, S, D)
```

```python
from contextlib import ExitStack

import concourse.bass as bass
from concourse import mybir

F32 = mybir.dt.float32
F32R = mybir.dt.float32r
I32 = mybir.dt.int32
ALU = mybir.AluOpType
ACT = mybir.ActivationFunctionType
AX_X = mybir.AxisListType.X

P = 128
B, S, D, C = 32, 64, 256, 128
TOK = 256
NT = TOK // P
GROUPS = B * S // TOK
KD = D // P
HEADS = 16
HD, CHD = D // HEADS, C // HEADS
PAIRS = HEADS // 2
INNER = 688
FULL = INNER // P
LEFT = INNER - FULL * P
MT = 2 * FULL + 1
EPS = 1e-6
MASKED = -1e30
UNITS = [(0, 0), (0, 1), (1, 0), (1, 1), (0, 2), (1, 2)]
BIAS = 2 * LEFT
GU = 4 * INNER
VB = 2 * HD + 2
CVB = 2 * CHD + 2
STAGE = MT * TOK

SIZES = [("mem", KD * C), ("gate_x", KD * D), ("mem_t", D), ("gate_m", D), ("ckv", 2 * C), ("cq", KD * C),
         ("qkv", KD * 6 * D), ("dense", KD * 2 * D), ("cdense", D),
         ("gu", KD * GU), ("down", 2 * FULL * D), ("down_left", 2 * D)]
AT, COLS = {}, 0
for _name, _size in SIZES:
    AT[_name] = COLS
    COLS += _size


def build_program(nc, a, out):
    with ExitStack() as ctx:
        def sb(name, shape, dt=F32):
            return ctx.enter_context(nc.sbuf_tensor(name, shape, dt))

        def sem(name):
            return ctx.enter_context(nc.semaphore(name))

        def sems(name, n):
            return [sem(f"{name}{k}") for k in range(n)]

        w_hi, w_lo = sb("w_hi", [P, COLS], F32R), sb("w_lo", [P, COLS], F32R)
        with nc.sbuf_tensor("stage", [P, 2, STAGE], F32) as stage:
            pass
        h_hi, h_lo = sb("h_hi", [P, MT, TOK], F32R), sb("h_lo", [P, MT, TOK], F32R)
        xc = sb("xc", [P, KD + 1, TOK])
        xc_hi, xc_lo = sb("xc_hi", [P, KD + 1, TOK], F32R), sb("xc_lo", [P, KD + 1, TOK], F32R)
        x_res = sb("x_res", [P, NT, D])
        ctx_tok = sb("ctx_tok", [P, 2, C])
        mask_in = sb("mask_in", [P, 2, NT], I32)
        mask_is1 = sb("mask_is1", [P, 2, NT])
        pick = sb("pick", [P, 2, NT])
        pick_r = sb("pick_r", [P, 2, NT])
        am_hi, am_lo = sb("am_hi", [P, NT, P], F32R), sb("am_lo", [P, NT, P], F32R)
        qkv = sb("qkv", [P, NT, 3 * D])
        ra, rb = sb("ra", [P, 512]), sb("rb", [P, 512])
        q0, p0, p0_t = rb[:, 0:TOK], rb[:, TOK:TOK + P], rb[:, TOK + P:512]
        ta_hi, ta_lo = sb("ta_hi", [P, KD, TOK], F32R), sb("ta_lo", [P, KD, TOK], F32R)
        q_t = sb("q_t", [P, 2, TOK])
        kblk = sb("kblk", [P, 4, TOK])
        ck_t = sb("ck_t", [P, TOK])
        vblk = sb("vblk", [P, NT, 2, PAIRS, VB])
        cvblk = sb("cvblk", [P, NT, 2, PAIRS, CVB])
        sm = sb("sm", [P, 4, 512])
        tok = sb("tok", [P, NT, D])
        res = sb("res", [P, NT, D])
        pick_y = sb("pick_y", [P, 2, NT])
        tb_hi, tb_lo = sb("tb_hi", [P, KD, TOK], F32R), sb("tb_lo", [P, KD, TOK], F32R)
        tc_hi, tc_lo = sb("tc_hi", [P, KD, TOK], F32R), sb("tc_lo", [P, KD, TOK], F32R)
        with (nc.sbuf_tensor("pos_i", [S, S], I32) as pos_i, nc.sbuf_tensor("pos_f", [S, S], F32) as pos_f,
              nc.sbuf_tensor("pos_neg", [S, S], F32) as pos_neg, nc.sbuf_tensor("onehot", [S, 2, S], F32) as onehot,
              nc.sbuf_tensor("trig_tab", [S, 2 * HD], F32) as trig_tab,
              nc.sbuf_tensor("bias_raw", [BIAS + 1, D], F32) as bias_raw,
              nc.sbuf_tensor("ones_row", [BIAS + 1, P], F32) as ones_row):
            pass
        HB = 3
        hb = sb("hb", [P, HB, TOK])
        res_b = sb("res_b", [P, NT, D])
        pick_b = sb("pick_b", [P, 2, NT])
        top0 = sb("top0", [P, NT])
        sum0 = sb("sum0", [P, 2, NT])
        top = sb("top", [P, 32])
        inv = sb("inv", [P, NT, PAIRS, 2])
        sumsq, var, rms = sb("sumsq", [P, 4, NT]), sb("var", [P, 4, NT]), sb("rms", [P, 4, NT])
        minus_half = sb("minus_half", [P, NT])
        ident = sb("ident", [P, P])
        causal = sb("causal", [P, S])
        consts = sb("consts", [P, 8])
        norm0 = sb("norm0", [P, D])
        ln = sb("ln", [P, 3, KD])
        trig = sb("trig", [P, 2, HD])
        ident_r, causal_r = sb("ident_r", [P, P], F32R), sb("causal_r", [P, S], F32R)
        one = slice(BIAS, BIAS + 1)
        ones_r = sb("ones_r", [BIAS + 1, P], F32R)
        b_hi, b_lo = (w[one, AT["down_left"]:AT["down_left"] + D] for w in (w_hi, w_lo))
        b_row = bias_raw[one, :]
        ps = ctx.enter_context(nc.psum_tensor("ps", [P, 8, 512], F32))
        X0, X1, M0 = 4, 5, 6

        consts_in, raw_in = sem("consts_in"), sems("raw_in", 2)
        raw_hi, raw_lo = sem("raw_hi"), sem("raw_lo")
        gm_mm, gm_hi, gm_lo = sem("gm_mm"), sem("gm_hi"), sem("gm_lo")
        zeroed, filled, bias_hi, bias_lo, mask_set = (
            sem(n) for n in "zeroed filled bias_hi bias_lo mask_set".split())
        pos_done, trig_mm, trig_ready = sem("pos_done"), sem("trig_mm"), sem("trig_ready")
        xc_in, xres_in, ctok_in, mask_dma = sem("xc_in"), sem("xres_in"), sem("ctok_in"), sem("mask_dma")
        is1, pick_v, picks = sem("is1"), sem("pick_v"), sem("picks")
        xc_hi_r, xc_lo_r, q0_mm, q0_r = sem("xc_hi_r"), sem("xc_lo_r"), sem("q0_mm"), sem("q0_r")
        sc0_mm, top0_r, low0_r, exp0_r, sum0_r, inv0_r, p0_r = (
            sem(n) for n in "sc0_mm top0_r low0_r exp0_r sum0_r inv0_r p0_r".split())
        p0t_mm, p0t_r, am_mm, am_hi_r, am_lo_r = (sem(n) for n in "p0t_mm p0t_r am_mm am_hi_r am_lo_r".split())
        mcz_mm, tanh_r, gated, fused = (sem(n) for n in "mcz_mm tanh_r gated fused".split())
        sq_r, var_r, rms_r = sems("sq_r", 4), sems("var_r", 4), sems("rms_r", 4)
        x1_r, tx1_mm, x1_hi, x1_lo = (sem(n) for n in "x1_r tx1_mm x1_hi x1_lo".split())
        pickr_r = sem("pickr_r")
        unit_mm, vpart, qkv_r = sem("unit_mm"), sem("vpart"), sem("qkv_r")
        rope_c, rope_s, rope_r = sem("rope_c"), sem("rope_s"), sem("rope_r")
        vb_r, tq_mm, tk_mm, qt_r, kb_r = (sem(n) for n in "vb_r tq_mm tk_mm qt_r kb_r".split())
        kv_mm, kv_r = sem("kv_mm"), sem("kv_r")
        picky_r = sem("picky_r")
        s_mm = [sems(f"s_mm{k}_", 2) for k in range(2)]
        top_r, low_r, exp_r, pt_mm, pt_r = (sems(n, 2) for n in "top_r low_r exp_r pt_mm pt_r".split())
        pv_mm, inv_r, ctx_r = sems("pv_mm", 2), sems("inv_r", 2), sems("ctx_r", 2)
        tctx_mm, ctx_hi, ctx_lo = sems("tctx_mm", 2), sems("ctx_hi", 2), sems("ctx_lo", 2)
        dense_mm, res_v = sem("dense_mm"), sem("res_v")
        taken, x2_r = sem("taken"), sem("x2_r")
        tci_mm, ci_hi, ci_lo = (sem(n) for n in "tci_mm ci_hi ci_lo".split())
        ckb_r, cq_mm, cq_r = sem("ckb_r"), sem("cq_mm"), sem("cq_r")
        cd_mm, x3_r, resb_r, pickb_r = (sem(n) for n in "cd_mm x3_r resb_r pickb_r".split())
        mi_r, tmi_mm, mi_hi, mi_lo = (sem(n) for n in "mi_r tmi_mm mi_hi mi_lo".split())
        gu_mm, th_r, tg_r, h_r, h_hi_r, h_lo_r = (sem(n) for n in "gu_mm th_r tg_r h_r h_hi_r h_lo_r".split())
        down_mm, y_v = sem("down_mm"), sem("y_v")
        y_r, stored = sem("y_r"), sem("stored")

        def wcols(name, at, n):
            return slice(AT[name] + at, AT[name] + at + n)

        chunks = [
            (a["w_first"], P, 2048, [(0, 1024, AT["mem"], 1.0), (1024, 256, AT["ckv"], 1.0),
                                     (1280, 128, AT["cq"], ln[:, 1, 0:1]),
                                     (1408, 128, AT["cq"] + 128, ln[:, 1, 1:2])]),
            (a["w_qkv"][0], P, 6 * D, [(0, 6 * D, AT["qkv"], ln[:, 0, 0:1])]),
            (a["w_qkv"][1], P, 6 * D, [(0, 6 * D, AT["qkv"] + 6 * D, ln[:, 0, 1:2])]),
            (a["w_dense"], P, 5 * D, [(0, 5 * D, AT["dense"], 1.0)]),
            (a["w_gu"][0], P, GU, [(0, GU, AT["gu"], ln[:, 2, 0:1])]),
            (a["w_gu"][1], P, GU, [(0, GU, AT["gu"] + GU, ln[:, 2, 1:2])]),
            (a["w_down"], P, 2 * FULL * D, [(0, 2 * FULL * D, AT["down"], 0.5)]),
            (a["w_down_left"], 2 * LEFT, 2 * D, [(0, 2 * D, AT["down_left"], 0.5)]),
        ]
        raw_mem, raw_gate_m = stage[:, 0, 0:KD * C], stage[:, 0, 1536:2048]

        def before(eng, s, v):
            if not (isinstance(v, int) and v <= 0):
                eng.wait_ge(s, v)

        def f32(ap):
            return ap.bitcast(F32)

        def of_tile(ap, t):
            return ap[:, t * P:(t + 1) * P]

        def inner(n):
            return slice(0, P if n < 2 * FULL else 2 * LEFT)

        def counts(g):
            return g + 1, g

        def unit_count(x, n):
            return x[1] * len(UNITS) + n

        def bank_count(y, j):
            return y[1] * 4 + (j + 1)

        def tile_count(g, t):
            return g[1] * NT + (t + 1)

        block = ctx.enter_context(nc.Block())

        @block.sync
        def _(sp):
            def load_chunk(n):
                src, rows, cols, _ = chunks[n]
                if n >= 2:
                    sp.wait_ge(raw_lo, n - 1)
                if n == 2:
                    sp.wait_ge(gm_mm, 1)
                sp.dma_start(stage[0:rows, n % 2, 0:cols], src).then_inc(raw_in[n % 2], 16)

            def load_xc(g, prev):
                before(sp, sc0_mm, prev)
                before(sp, xc_lo_r, prev)
                sp.dma_start(xc[:, :, :], a["xc"][g]).then_inc(xc_in, 16)
                before(sp, is1, prev)
                sp.dma_start(mask_in[:, :, :], a["mask"][g]).then_inc(mask_dma, 16)
                before(sp, am_mm, prev)
                sp.dma_start(ctx_tok[:, :, :], a["ctx_tok"][g]).then_inc(ctok_in, 16)

            def load_x(g, prev):
                before(sp, taken, prev)
                sp.dma_start(x_res[:, :, :], a["x_tok"][g]).then_inc(xres_in, 16)

            def store(g, cur):
                sp.wait_ge(y_r, cur + 1)
                sp.dma_start(out[g], res_b[:, :, :]).then_inc(stored, 16)

            sp.dma_start(ln[:, :, :], a["ln"]).then_inc(consts_in, 16)
            sp.dma_start(ident[:, :], a["ident"]).then_inc(consts_in, 16)
            sp.dma_start(consts[:, :], a["consts"]).then_inc(consts_in, 16)
            sp.dma_start(causal[:, :], a["causal"]).then_inc(consts_in, 16)
            sp.dma_start(trig_tab[:, :], a["trig_tab"]).then_inc(consts_in, 16)
            sp.dma_start(b_row, a["b_gate"]).then_inc(consts_in, 16)
            sp.dma_start(norm0[:, :], a["norm0"].partition_broadcast(P)).then_inc(consts_in, 16)
            sp.dma_start(pos_i[:, :], a["pos"].partition_broadcast(S)).then_inc(consts_in, 16)
            load_chunk(0)
            load_xc(0, 0)
            load_x(0, 0)
            for n in range(1, 4):
                load_chunk(n)
            load_xc(1, 1)
            load_chunk(4)
            load_chunk(5)
            load_x(1, 1)
            load_chunk(6)
            load_xc(2, 2)
            load_chunk(7)
            with sp.Fori(1, GROUPS - 2) as i:
                load_xc(i + 2, i + 2)
                load_x(i + 1, i + 1)
                store(i - 1, i)
            load_x(GROUPS - 1, GROUPS - 1)
            for g in range(GROUPS - 3, GROUPS):
                store(g, g + 1)
            sp.wait_ge(stored, 16 * GROUPS)

        @block.scalar
        def _(act):
            def split_chunk(n):
                rows = chunks[n][1]
                act.wait_ge(raw_in[n % 2], 16 * (n // 2 + 1))
                for at, count, to, scale in chunks[n][3]:
                    last = act.activation(w_hi[0:rows, to:to + count], stage[0:rows, n % 2, at:at + count],
                                          ACT.Copy, scale=scale)
                last.then_inc(raw_hi, 1)

            def copy(out_, in_, scale=1.0):
                return act.activation(out_, in_, ACT.Copy, scale=scale)

            def square_sum(n, x, junk):
                for t in range(NT):
                    last = act.activation(junk[:, t, :], x[:, t, :], ACT.Square, accum_out=sumsq[:, n, t:t + 1])
                last.then_inc(sq_r[n], 1)

            def setup(n):
                if n in (1, 2, 3):
                    split_chunk(n)
                elif n == 0:
                    act.wait_ge(gm_mm, 1)
                    copy(w_hi[:, wcols("gate_m", 0, D)], ps[:, 7, 0:D]).then_inc(gm_hi, 1)
                    copy(b_hi, b_row)
                    act.wait_ge(filled, 1)
                    copy(ones_r[one, :], ones_row[one, :]).then_inc(bias_hi, 1)
                    copy(ident_r[:, :], ident[:, :])
                    copy(causal_r[:, :], causal[:, :]).then_inc(mask_set, 1)
                    act.wait_ge(trig_mm, 1)
                    copy(trig[:, :, :], ps[:, 6, 0:2 * HD]).then_inc(trig_ready, 1)

            def split_xc(x):
                act.wait_ge(xc_in, x[0] * 16)
                before(act, kv_mm, x[1])
                copy(xc_hi[:, :, :], xc[:, :, :]).then_inc(xc_hi_r, 1)

            def q0_out(x):
                act.wait_ge(q0_mm, x[0])
                copy(q0, ps[:, X0, 0:TOK], float(D) ** -0.5).then_inc(q0_r, 1)

            def exp0(x):
                act.wait_ge(low0_r, x[0])
                act.activation(p0, p0, ACT.Exp).then_inc(exp0_r, 1)

            def p0t_out(x):
                act.wait_ge(p0t_mm, x[0])
                copy(p0_t, ps[:, X0, 0:P]).then_inc(p0t_r, 1)

            def am_out(x):
                act.wait_ge(am_mm, x[0])
                copy(am_hi[:, :, :], ps[:, X0:X0 + 2, 0:P]).then_inc(am_hi_r, 1)

            def gate(x):
                act.wait_ge(mcz_mm, x[0])
                act.activation(ra[:, :].rearrange("p (t c) -> p t c", t=NT), ps[:, X0:X0 + 2, D:2 * D], ACT.Tanh,
                               scale=0.5).then_inc(tanh_r, 1)

            def squares_fused(x):
                act.wait_ge(fused, x[0])
                square_sum(0, x_res, rb.rearrange("p (t c) -> p t c", t=NT))

            def squares_x1(x):
                act.wait_ge(x1_r, x[0])
                square_sum(1, x_res, rb.rearrange("p (t c) -> p t c", t=NT))

            def split_x1(x):
                act.wait_ge(tx1_mm, x[0])
                copy(ta_hi[:, :, :], ps[:, X0, :]).then_inc(x1_hi, 1)

            def unit_v(x, u):
                if u == 0:
                    act.wait_ge(pickr_r, x[0])
                act.wait_ge(unit_mm, unit_count(x, u + 1))
                t, n = UNITS[u]
                copy(qkv[:, t, n * D:(n + 1) * D], ps[:, (X1, X0)[u % 2], 0:D],
                     pick_r[:, 0, t:t + 1]).then_inc(vpart, 1)

            def fill_vblk(x):
                act.wait_ge(qkv_r, unit_count(x, len(UNITS)))
                before(act, pv_mm[0], x[1] * NT)
                v = qkv[:, :, 2 * D:3 * D].rearrange("p t (h e c) -> p t h e c", h=PAIRS, e=2)
                for b in range(2):
                    for e in range(2):
                        last = copy(vblk[64 * e:64 * e + 64, :, b, :, e * HD:(e + 1) * HD],
                                    v[64 * b:64 * b + 64, :, :, e, :])
                last.then_inc(vb_r, 1)

            def q_out(x):
                act.wait_ge(tq_mm, x[0])
                before(act, s_mm[0][1], x[1])
                copy(q_t[:, :, :], ps[:, X0, :]).then_inc(qt_r, 1)

            def kv_out(x):
                act.wait_ge(kv_mm, x[0])
                before(act, ckb_r, x[1])
                copy(ck_t[:, :], ps[:, X0, 0:TOK])
                before(act, pv_mm[1], x[1] * NT)
                cv = ps[:, X0, TOK:2 * TOK].rearrange("p (t h e c) -> p t h e c", t=NT, h=PAIRS, e=2)
                for b in range(2):
                    for e in range(2):
                        last = copy(cvblk[64 * e:64 * e + 64, :, b, :, e * CHD:(e + 1) * CHD],
                                    cv[64 * b:64 * b + 64, :, :, e, :])
                last.then_inc(kv_r, 1)

            def take_residual(y):
                act.wait_ge(x1_r, y[0])
                before(act, mi_r, y[1])
                before(act, resb_r, y[1])
                copy(res[:, :, :], x_res[:, :, :]).then_inc(taken, 1)

            def probs(y, j):
                act.wait_ge(low_r[0], bank_count(y, j))
                act.activation(sm[:, j, :], sm[:, j, :], ACT.Exp, scale=float(HD) ** -0.5).then_inc(exp_r[0], 1)

            def cross_probs(y, j):
                act.wait_ge(low_r[1], bank_count(y, j))
                if j == 0:
                    act.wait_ge(rms_r[2], y[0])
                for t in range(NT):
                    s_ = sm[:, j, t * 2 * P:(t + 1) * 2 * P]
                    last = act.activation(s_, s_, ACT.Exp, scale=rms[:, 2, t:t + 1])
                last.then_inc(exp_r[1], 1)

            def probs_t_out(y, k, j):
                act.wait_ge(pt_mm[k], bank_count(y, j))
                copy(sm[:, j, :], ps[:, j, :]).then_inc(pt_r[k], 1)

            def split_ctx(y):
                act.wait_ge(tctx_mm[0], y[0])
                copy(ta_hi[:, :, :], ps[:, 3, :]).then_inc(ctx_hi[0], 1)

            def squares_x2(y):
                act.wait_ge(x2_r, y[0])
                square_sum(2, res, tok)

            def split_ci(y):
                act.wait_ge(tci_mm, y[0])
                copy(tb_hi[:, :, :], ps[:, 2, :]).then_inc(ci_hi, 1)

            def cq_out(y):
                act.wait_ge(cq_mm, y[0])
                copy(tok[:, 0, :], ps[:, 3, 0:TOK], float(CHD) ** -0.5).then_inc(cq_r, 1)

            def split_cctx(y):
                act.wait_ge(tctx_mm[1], y[0])
                copy(tb_hi[:, 0, :], ps[:, 2, 0:TOK]).then_inc(ctx_hi[1], 1)

            def squares_x3(y):
                act.wait_ge(x3_r, y[0])
                square_sum(3, res, tok)

            def copy_res(y):
                before(act, stored, y[1] * 16)
                copy(res_b[:, :, :], res[:, :, :]).then_inc(resb_r, 1)

            def split_mi(y):
                act.wait_ge(tmi_mm, y[0])
                copy(tc_hi[:, :, :], ps[:, 2, :]).then_inc(mi_hi, 1)

            def tanh_gate(m, n):
                act.wait_ge(gu_mm, m[2] + (n + 1))
                if n >= HB:
                    act.wait_ge(h_lo_r, m[2] + (n + 1 - HB))
                r = inner(n)
                act.activation(hb[r, n % HB, :], ps[r, M0 + n % 2, 0:TOK], ACT.Tanh, scale=0.5).then_inc(th_r, 1)

            def split_h(m, n):
                act.wait_ge(h_r, m[2] + (n + 1))
                r = inner(n)
                copy(h_hi[r, n, :], hb[r, n % HB, :]).then_inc(h_hi_r, 1)

            def mlp(m, lo, hi):
                for n in range(lo, hi):
                    if n < MT:
                        tanh_gate(m, n)
                    if n > 0:
                        split_h(m, n - 1)

            def turn(x, y, m, prepare=lambda n: None):
                if m is not None:
                    mlp(m, 0, 1)
                if x is not None:
                    split_xc(x)
                if m is not None:
                    mlp(m, 1, 2)
                prepare(4)
                prepare(0)
                prepare(1)
                if y is not None:
                    take_residual(y)
                    probs(y, 2)
                if x is not None:
                    q0_out(x)
                if y is not None:
                    probs(y, 3)
                    probs_t_out(y, 0, 0)
                    probs_t_out(y, 0, 1)
                    probs_t_out(y, 0, 2)
                    probs_t_out(y, 0, 3)
                if x is not None:
                    exp0(x)
                if m is not None:
                    mlp(m, 2, 4)
                if x is not None:
                    p0t_out(x)
                if y is not None:
                    split_ctx(y)
                prepare(2)
                if m is not None:
                    mlp(m, 4, 5)
                if x is not None:
                    am_out(x)
                if m is not None:
                    mlp(m, 5, 6)
                prepare(3)
                prepare(5)
                if y is not None:
                    squares_x2(y)
                    split_ci(y)
                if m is not None:
                    mlp(m, 6, 8)
                if x is not None:
                    gate(x)
                if y is not None:
                    cq_out(y)
                if x is not None:
                    squares_fused(x)
                prepare(6)
                if m is not None:
                    mlp(m, 8, 10)
                prepare(7)
                if m is not None:
                    mlp(m, 10, MT + 1)
                if y is not None:
                    cross_probs(y, 0)
                if x is not None:
                    squares_x1(x)
                if y is not None:
                    cross_probs(y, 1)
                    cross_probs(y, 2)
                if x is not None:
                    split_x1(x)
                if y is not None:
                    cross_probs(y, 3)
                    probs_t_out(y, 1, 0)
                    probs_t_out(y, 1, 1)
                    probs_t_out(y, 1, 2)
                    probs_t_out(y, 1, 3)
                if x is not None:
                    unit_v(x, 0)
                    unit_v(x, 1)
                if y is not None:
                    split_cctx(y)
                if x is not None:
                    unit_v(x, 2)
                    unit_v(x, 3)
                if y is not None:
                    squares_x3(y)
                if x is not None:
                    unit_v(x, 4)
                    unit_v(x, 5)
                    q_out(x)
                    fill_vblk(x)
                if y is not None:
                    split_mi(y)
                if x is not None:
                    kv_out(x)
                    probs(x, 0)
                    probs(x, 1)
                if y is not None:
                    copy_res(y)

            act.preload_act_table(ACT.Exp)
            act.wait_ge(consts_in, 16 * 8)
            split_chunk(0)
            turn(counts(0), None, None, setup)
            turn(counts(1), counts(0), None, lambda n: split_chunk(n) if n >= 4 else None)
            with act.Fori(1, GROUPS - 1) as i:
                base = act.snap((i - 1) * MT)
                turn((i + 2, i + 1), (i + 1, i), (i, i - 1, base))
            turn(None, counts(GROUPS - 1), (*counts(GROUPS - 2), (GROUPS - 2) * MT))
            turn(None, None, (*counts(GROUPS - 1), (GROUPS - 1) * MT))

        @block.vector
        def _(dve):
            def split_chunk(n):
                rows = chunks[n][1]
                dve.wait_ge(raw_in[n % 2], 16 * (n // 2 + 1))
                dve.wait_ge(raw_hi, n + 1)
                for at, count, to, scale in chunks[n][3]:
                    last = dve.scalar_tensor_tensor(
                        out=w_lo[0:rows, to:to + count], in0=stage[0:rows, n % 2, at:at + count], scalar=scale,
                        in1=f32(w_hi[0:rows, to:to + count]), op0=ALU.mult, op1=ALU.subtract)
                last.then_inc(raw_lo, 1)

            def lo_part(out_, full, hi_part):
                return dve.tensor_tensor(out_, full, f32(hi_part), ALU.subtract)

            def setup(n):
                if n in (1, 2, 3):
                    split_chunk(n)
                elif n == 0:
                    dve.wait_ge(gm_hi, 1)
                    w = wcols("gate_m", 0, D)
                    lo_part(w_lo[:, w], ps[:, 7, 0:D], w_hi[:, w]).then_inc(gm_lo, 1)
                    dve.wait_ge(bias_hi, 1)
                    lo_part(b_lo, b_row, b_hi).then_inc(bias_lo, 1)

            def weighted_sum(out_, in0, factor, in1, op=ALU.add):
                return dve.scalar_tensor_tensor(out=out_, in0=in0, scalar=factor, in1=in1, op0=ALU.mult, op1=op)

            def variance(n, cur):
                dve.wait_ge(sq_r[n], cur)
                dve.tensor_scalar(var[:, n, :], sumsq[:, n, :], 1.0 / D, EPS, ALU.mult, ALU.add).then_inc(var_r[n], 1)

            def picking(x):
                dve.wait_ge(mask_dma, x[0] * 16)
                dve.tensor_scalar(mask_is1[:, :, :], mask_in[:, :, :], 1.0, None, ALU.is_equal).then_inc(is1, 1)
                dve.wait_ge(is1, x[0])
                dve.scalar_tensor_tensor(out=pick[:, 0, :], in0=mask_is1[:, 0, :], scalar=consts[:, 6:7],
                                         in1=mask_is1[:, 1, :], op0=ALU.mult, op1=ALU.mult).then_inc(pick_v, 1)
                dve.wait_ge(pick_v, x[0])
                dve.tensor_scalar(pick[:, 1, :], pick[:, 0, :], -1.0, 1.0, ALU.mult, ALU.add).then_inc(picks, 1)

            sc0 = ps[:, X1, 0:P].rearrange("p (t s) -> p t s", s=S)
            p0v = p0.rearrange("p (t s) -> p t s", s=S)

            def softmax0_a(x):
                dve.wait_ge(sc0_mm, x[0])
                dve.tensor_reduce(top0[:, :], sc0, AX_X, ALU.max).then_inc(top0_r, 1)
                dve.wait_ge(top0_r, x[0])
                dve.tensor_tensor(p0v, sc0, top0[:, :].unsqueeze(2).to_broadcast([P, NT, S]),
                                  ALU.subtract).then_inc(low0_r, 1)

            def softmax0_b(x):
                dve.wait_ge(exp0_r, x[0])
                dve.tensor_reduce(sum0[:, 0, :], p0v, AX_X, ALU.add).then_inc(sum0_r, 1)
                dve.wait_ge(sum0_r, x[0])
                dve.reciprocal(sum0[:, 1, :], sum0[:, 0, :]).then_inc(inv0_r, 1)
                dve.wait_ge(inv0_r, x[0])
                dve.tensor_tensor(p0v, p0v, sum0[:, 1, :].unsqueeze(2).to_broadcast([P, NT, S]),
                                  ALU.mult).then_inc(p0_r, 1)

            def am_out(x):
                dve.wait_ge(am_hi_r, x[0])
                lo_part(am_lo[:, :, :], ps[:, X0:X0 + 2, 0:P], am_hi[:, :, :]).then_inc(am_lo_r, 1)

            def fuse(x):
                g = ra[:, :].rearrange("p (t c) -> p t c", t=NT)
                dve.wait_ge(tanh_r, x[0])
                dve.scalar_tensor_tensor(out=g, in0=g, scalar=1.0, in1=ps[:, X0:X0 + 2, 0:D],
                                         op0=ALU.add, op1=ALU.mult).then_inc(gated, 1)
                dve.wait_ge(gated, x[0])
                dve.wait_ge(xres_in, x[0] * 16)
                weighted_sum(x_res[:, :, :], g, 0.5, x_res[:, :, :]).then_inc(fused, 1)

            def norm_fused(x):
                dve.wait_ge(rms_r[0], x[0])
                for t in range(NT):
                    last = dve.scalar_tensor_tensor(out=x_res[:, t, :], in0=x_res[:, t, :], scalar=rms[:, 0, t:t + 1],
                                                    in1=norm0[:, :], op0=ALU.mult, op1=ALU.mult)
                last.then_inc(x1_r, 1)

            def split_x1(x):
                dve.wait_ge(x1_hi, x[0])
                lo_part(ta_lo[:, :, :], ps[:, X0, :], ta_hi[:, :, :]).then_inc(x1_lo, 1)

            def factors(x):
                dve.wait_ge(rms_r[1], x[0])
                dve.wait_ge(picks, x[0])
                dve.tensor_tensor(pick_r[:, :, :], pick[:, :, :],
                                  rms[:, 1, :].unsqueeze(1).to_broadcast([P, 2, NT]), ALU.mult).then_inc(pickr_r, 1)

            def unit_l(x, u):
                t, n = UNITS[u]
                to = qkv[:, t, n * D:(n + 1) * D]
                dve.wait_ge(pickr_r, x[0])
                dve.wait_ge(vpart, unit_count(x, u + 1))
                weighted_sum(to, ps[:, (X1, X0)[u % 2], D:2 * D], pick_r[:, 1, t:t + 1], to).then_inc(qkv_r, 1)

            def rotary_cos(x, t):
                dve.wait_ge(qkv_r, unit_count(x, 2 * t + 2))
                if t == 0:
                    dve.wait_ge(trig_ready, 1)
                else:
                    dve.wait_ge(rope_r, tile_count(x, t - 1))
                dve.tensor_tensor(ra[:, :].rearrange("p (h c) -> p h c", c=HD),
                                  qkv[:, t, 0:2 * D].rearrange("p (h c) -> p h c", c=HD),
                                  trig[:, 0, :].unsqueeze(1).to_broadcast([P, 2 * HEADS, HD]),
                                  ALU.mult).then_inc(rope_c, 1)

            def rotary_sum(x, t):
                dve.wait_ge(rope_c, tile_count(x, t))
                dve.wait_ge(rope_s, tile_count(x, t))
                dve.tensor_tensor(qkv[:, t, 0:2 * D], ra[:, :], rb[:, :], ALU.add).then_inc(rope_r, 1)

            def k_out(x):
                dve.wait_ge(tk_mm, x[0])
                before(dve, s_mm[1][1], x[1])
                kb = kblk[:, :, :].rearrange("p (m e) c -> p m e c", e=2)
                for e in range(2):
                    last = dve.tensor_scalar(kb[:, :, e, :], ps[:, X1, :].rearrange("p (m c) -> p m c", m=2),
                                             consts[:, e:e + 1], None, ALU.mult)
                last.then_inc(kb_r, 1)

            def own_picks(y):
                dve.wait_ge(picks, y[0])
                before(dve, pickb_r, y[1])
                dve.tensor_copy(pick_y[:, :, :], pick[:, :, :]).then_inc(picky_r, 1)

            def less_top(y, k, j):
                src, to = (u[:, j, :].rearrange("p (g s) -> p g s", s=S) for u in (ps, sm))
                highest = top[:, 8 * j:8 * j + 8]
                dve.wait_ge(s_mm[k][j // 2], y[0])
                dve.tensor_reduce(highest, src, AX_X, ALU.max).then_inc(top_r[k], 1)
                dve.wait_ge(top_r[k], bank_count(y, j))
                dve.tensor_tensor(to, src, highest.unsqueeze(2).to_broadcast([P, 8, S]),
                                  ALU.subtract).then_inc(low_r[k], 1)

            def context(y, k, t):
                width, block_ = (HD, CHD)[k], (VB, CVB)[k]
                dve.wait_ge(pv_mm[k], tile_count(y, t))
                pv = ps[:, t, 0:PAIRS * block_].rearrange("p (h c) -> p h c", c=block_)
                dve.reciprocal(inv[:, t, :, :], pv[:, :, 2 * width:block_]).then_inc(inv_r[k], 1)
                dve.wait_ge(inv_r[k], tile_count(y, t))
                to = tok[:, t, 0:HEADS * width].rearrange("p (h e c) -> p h e c", h=PAIRS, e=2)
                for e in range(2):
                    last = dve.tensor_tensor(to[:, :, e, :], pv[:, :, e * width:(e + 1) * width],
                                             inv[:, t, :, e:e + 1].to_broadcast([P, PAIRS, width]), ALU.mult)
                last.then_inc(ctx_r[k], 1)

            def split_ctx(y):
                dve.wait_ge(ctx_hi[0], y[0])
                lo_part(ta_lo[:, :, :], ps[:, 3, :], ta_hi[:, :, :]).then_inc(ctx_lo[0], 1)

            def add_dense(y):
                dve.wait_ge(taken, y[0])
                dve.wait_ge(picky_r, y[0])
                for t in range(NT):
                    dve.wait_ge(dense_mm, tile_count(y, t))
                    weighted_sum(res[:, t, :], ps[:, t, 0:D], pick_y[:, 0, t:t + 1], res[:, t, :]).then_inc(res_v, 1)
                    dve.wait_ge(res_v, tile_count(y, t))
                    last = weighted_sum(res[:, t, :], ps[:, t, D:2 * D], pick_y[:, 1, t:t + 1], res[:, t, :])
                last.then_inc(x2_r, 1)

            def split_ci(y):
                dve.wait_ge(ci_hi, y[0])
                lo_part(tb_lo[:, :, :], ps[:, 2, :], tb_hi[:, :, :]).then_inc(ci_lo, 1)

            def split_cctx(y):
                dve.wait_ge(ctx_hi[1], y[0])
                lo_part(tb_lo[:, 0, :], ps[:, 2, 0:TOK], tb_hi[:, 0, :]).then_inc(ctx_lo[1], 1)

            def add_cross(y):
                dve.wait_ge(cd_mm, y[0])
                dve.tensor_tensor(res[:, :, :], ps[:, 3, :], res[:, :, :].rearrange("p t c -> p (t c)"),
                                  ALU.add).then_inc(x3_r, 1)

            def split_mi(y):
                dve.wait_ge(mi_hi, y[0])
                lo_part(tc_lo[:, :, :], ps[:, 2, :], tc_hi[:, :, :]).then_inc(mi_lo, 1)

            def mlp_picks(y):
                dve.wait_ge(y_r, y[1] + 1)
                dve.tensor_copy(pick_b[:, :, :], pick_y[:, :, :]).then_inc(pickb_r, 1)

            def mlp(m, lo, hi):
                for n in range(lo, hi):
                    r = inner(n)
                    bank, h = ps[r, M0 + n % 2, :], hb[r, n % HB, :]
                    dve.wait_ge(th_r, m[2] + (n + 1))
                    dve.scalar_tensor_tensor(out=h, in0=h, scalar=1.0, in1=bank[:, 0:TOK],
                                             op0=ALU.add, op1=ALU.mult).then_inc(tg_r, 1)
                    dve.wait_ge(tg_r, m[2] + (n + 1))
                    dve.tensor_tensor(h, h, bank[:, TOK:2 * TOK], ALU.mult).then_inc(h_r, 1)

            def result(m):
                dve.wait_ge(resb_r, m[0])
                dve.wait_ge(pickb_r, m[0])
                for t in range(NT):
                    dve.wait_ge(down_mm, tile_count(m, t))
                    weighted_sum(res_b[:, t, :], ps[:, M0 + t, 0:D], pick_b[:, 0, t:t + 1],
                                 res_b[:, t, :]).then_inc(y_v, 1)
                    dve.wait_ge(y_v, tile_count(m, t))
                    last = weighted_sum(res_b[:, t, :], ps[:, M0 + t, D:2 * D], pick_b[:, 1, t:t + 1], res_b[:, t, :])
                last.then_inc(y_r, 1)

            def turn(x, y, m, prepare=lambda n: None):
                if y is not None:
                    own_picks(y)
                if m is not None:
                    mlp(m, 0, 1)
                if x is not None:
                    picking(x)
                if y is not None:
                    less_top(y, 0, 2)
                    less_top(y, 0, 3)
                if m is not None:
                    mlp(m, 1, 2)
                prepare(4)
                if x is not None:
                    softmax0_a(x)
                if m is not None:
                    mlp(m, 2, 3)
                if x is not None:
                    softmax0_b(x)
                if y is not None:
                    context(y, 0, 0)
                    context(y, 0, 1)
                if m is not None:
                    mlp(m, 3, 4)
                if y is not None:
                    split_ctx(y)
                prepare(0)
                prepare(1)
                if m is not None:
                    mlp(m, 4, 6)
                if x is not None:
                    am_out(x)
                prepare(2)
                prepare(3)
                if y is not None:
                    add_dense(y)
                prepare(5)
                if y is not None:
                    variance(2, y[0])
                    split_ci(y)
                if m is not None:
                    mlp(m, 6, 8)
                if x is not None:
                    fuse(x)
                    variance(0, x[0])
                if m is not None:
                    mlp(m, 8, 9)
                if y is not None:
                    less_top(y, 1, 0)
                if m is not None:
                    mlp(m, 9, MT)
                if x is not None:
                    norm_fused(x)
                if y is not None:
                    less_top(y, 1, 1)
                    less_top(y, 1, 2)
                    less_top(y, 1, 3)
                if x is not None:
                    variance(1, x[0])
                    split_x1(x)
                prepare(6)
                if x is not None:
                    factors(x)
                    unit_l(x, 0)
                    unit_l(x, 1)
                if y is not None:
                    context(y, 1, 0)
                    context(y, 1, 1)
                if x is not None:
                    rotary_cos(x, 0)
                if y is not None:
                    split_cctx(y)
                if x is not None:
                    unit_l(x, 2)
                    unit_l(x, 3)
                if y is not None:
                    add_cross(y)
                if x is not None:
                    rotary_sum(x, 0)
                    rotary_cos(x, 1)
                if y is not None:
                    variance(3, y[0])
                if x is not None:
                    unit_l(x, 4)
                    unit_l(x, 5)
                    rotary_sum(x, 1)
                prepare(7)
                if x is not None:
                    k_out(x)
                if m is not None:
                    result(m)
                if y is not None:
                    mlp_picks(y)
                    split_mi(y)
                if x is not None:
                    less_top(x, 0, 0)
                    less_top(x, 0, 1)

            dve.memset(vblk[:, :, :, :, :], 0.0)
            dve.memset(cvblk[:, :, :, :, :], 0.0)
            dve.memset(ones_row[one, :], 1.0)
            dve.memset(minus_half[:, :], -0.5).then_inc(zeroed, 1)
            dve.wait_ge(zeroed, 1)
            for e in range(2):
                dve.memset(vblk[64 * e:64 * e + 64, :, :, :, 2 * HD + e:2 * HD + e + 1], 1.0)
                last = dve.memset(cvblk[64 * e:64 * e + 64, :, :, :, 2 * CHD + e:2 * CHD + e + 1], 1.0)
            last.then_inc(filled, 1)
            dve.memset(pick_b[:, :, :], 0.0).then_inc(y_r, 1)
            dve.wait_ge(consts_in, 16 * 8)
            dve.tensor_copy(pos_f[:, :], pos_i[:, :]).then_inc(pos_done, 1)
            dve.wait_ge(pos_done, 1)
            dve.tensor_scalar(pos_neg[:, :], pos_f[:, :], 0.0, float(S), ALU.is_lt, ALU.mult).then_inc(pos_done, 1)
            dve.wait_ge(pos_done, 2)
            dve.tensor_tensor(pos_f[:, :], pos_f[:, :], pos_neg[:, :], ALU.add).then_inc(pos_done, 1)
            dve.wait_ge(pos_done, 3)
            dve.tensor_scalar(pos_f[:, :], pos_f[:, :], 0.0, float(S - 1), ALU.max, ALU.min).then_inc(pos_done, 1)
            dve.wait_ge(pos_done, 4)
            dve.tensor_scalar(onehot[:, :, :], pos_f[:, :].unsqueeze(1).to_broadcast([S, 2, S]),
                              consts[0:S, 7:8], None, ALU.is_equal).then_inc(pos_done, 1)
            split_chunk(0)
            turn(counts(0), None, None, setup)
            turn(counts(1), counts(0), None, lambda n: split_chunk(n) if n >= 4 else None)
            with dve.Fori(1, GROUPS - 1) as i:
                base = dve.snap((i - 1) * MT)
                turn((i + 2, i + 1), (i + 1, i), (i, i - 1, base))
            turn(None, counts(GROUPS - 1), (*counts(GROUPS - 2), (GROUPS - 2) * MT))
            turn(None, None, (*counts(GROUPS - 1), (GROUPS - 1) * MT))

        @block.gpsimd
        def _(pool):
            def split_xc(x):
                pool.wait_ge(xc_in, x[0] * 16)
                before(pool, kv_mm, x[1])
                pool.wait_ge(xc_hi_r, x[0])
                pool.tensor_tensor(xc_lo[:, :, :], xc[:, :, :], f32(xc_hi[:, :, :]), ALU.subtract).then_inc(xc_lo_r, 1)

            def ck_blocks(y):
                pool.wait_ge(kv_r, y[0])
                pool.wait_ge(s_mm[0][1], y[0])
                for m in range(4):
                    last = pool.tensor_tensor(kblk[:, m, :], ck_t[:, :], consts[:, 2 + m:3 + m].to_broadcast([P, TOK]),
                                              ALU.mult)
                last.then_inc(ckb_r, 1)

            def root(n, cur):
                pool.wait_ge(var_r[n], cur)
                pool.tensor_tensor(rms[:, n, :], var[:, n, :], minus_half[:, :], ALU.pow).then_inc(rms_r[n], 1)

            def rotary(x, t):
                q = qkv[:, t, 0:2 * D].rearrange("p (h e c) -> p h e c", h=2 * HEADS, e=2)
                r = rb[:, :].rearrange("p (h e c) -> p h e c", h=2 * HEADS, e=2)
                pool.wait_ge(qkv_r, unit_count(x, 2 * t + 2))
                if t == 0:
                    pool.wait_ge(trig_ready, 1)
                else:
                    pool.wait_ge(rope_r, tile_count(x, t - 1))
                for e in range(2):
                    sin = trig[:, 1, e * HD // 2:(e + 1) * HD // 2]
                    last = pool.tensor_tensor(r[:, :, e, :], q[:, :, 1 - e, :],
                                              sin.unsqueeze(1).to_broadcast([P, 2 * HEADS, HD // 2]), ALU.mult)
                last.then_inc(rope_s, 1)

            def mlp_input(y):
                pool.wait_ge(rms_r[3], y[0])
                pool.tensor_tensor(tok[:, :, :], res[:, :, :], rms[:, 3, :].unsqueeze(2).to_broadcast([P, NT, D]),
                                   ALU.mult).then_inc(mi_r, 1)

            def mlp(m, lo, hi):
                for n in range(lo, hi):
                    r = inner(n)
                    pool.wait_ge(h_hi_r, m[2] + (n + 1))
                    pool.tensor_tensor(h_lo[r, n, :], hb[r, n % HB, :], f32(h_hi[r, n, :]),
                                       ALU.subtract).then_inc(h_lo_r, 1)

            def turn(x, y, m):
                if x is not None:
                    split_xc(x)
                if m is not None:
                    mlp(m, 0, 3)
                if y is not None:
                    ck_blocks(y)
                if m is not None:
                    mlp(m, 3, 5)
                if y is not None:
                    root(2, y[0])
                if m is not None:
                    mlp(m, 5, 8)
                if x is not None:
                    root(0, x[0])
                if m is not None:
                    mlp(m, 8, MT)
                if x is not None:
                    root(1, x[0])
                    rotary(x, 0)
                    rotary(x, 1)
                if y is not None:
                    root(3, y[0])
                    mlp_input(y)

            pool.wait_ge(consts_in, 16 * 8)
            pool.wait_ge(filled, 1)
            turn(counts(0), None, None)
            turn(counts(1), counts(0), None)
            with pool.Fori(1, GROUPS - 1) as i:
                base = pool.snap((i - 1) * MT)
                turn((i + 2, i + 1), (i + 1, i), (i, i - 1, base))
            turn(None, counts(GROUPS - 1), (*counts(GROUPS - 2), (GROUPS - 2) * MT))
            turn(None, None, (*counts(GROUPS - 1), (GROUPS - 1) * MT))

        @block.tensor
        def _(pe):
            def product(o, lh, ll, rh, rl, start=False, stop=False):
                pe.matmul(o, lh, rh, start=start, stop=False, skip_group_check=True)
                pe.matmul(o, lh, rl, start=False, stop=False, skip_group_check=True)
                return pe.matmul(o, ll, rh, start=False, stop=stop, skip_group_check=True)

            def single(o, lhs, rhs):
                return pe.matmul(o, lhs, rhs, start=True, stop=True, skip_group_check=True)

            def transposes(bank, src):
                for t in range(NT):
                    for k in range(src.shape[2] // P):
                        last = pe.transpose(ps[:, bank, k * TOK + t * P:k * TOK + (t + 1) * P],
                                            src[:, t, k * P:(k + 1) * P], ident[:, :])
                return last

            def q0_product(x):
                pe.wait_ge(xc_hi_r, x[0])
                pe.wait_ge(xc_lo_r, x[0])
                before(pe, kv_r, x[1])
                for k in range(KD):
                    w = wcols("mem", k * C, C)
                    last = product(ps[:, X0, 0:TOK], w_hi[:, w], w_lo[:, w], xc_hi[:, k, :], xc_lo[:, k, :],
                                   k == 0, k == KD - 1)
                last.then_inc(q0_mm, 1)

            def scores0(x):
                pe.wait_ge(q0_r, x[0])
                before(pe, kb_r, x[1])
                for t in range(NT):
                    for b in range(2):
                        c = slice(t * P + b * S, t * P + (b + 1) * S)
                        last = single(ps[64 * b:64 * b + 64, X1, t * S:(t + 1) * S], q0[:, c], xc[:, KD, c])
                last.then_inc(sc0_mm, 1)

            def probs0_t(x):
                pe.wait_ge(p0_r, x[0])
                pe.transpose(ps[:, X0, 0:P], p0, ident[:, :]).then_inc(p0t_mm, 1)

            def attend0(x):
                pe.wait_ge(p0t_r, x[0])
                pe.wait_ge(ctok_in, x[0] * 16)
                for t in range(NT):
                    r = slice(64 * t, 64 * t + 64)
                    for b in range(2):
                        last = single(ps[:, X0 + t, b * S:(b + 1) * S], ctx_tok[r, b, :], p0_t[r, b * S:(b + 1) * S])
                last.then_inc(am_mm, 1)

            def context_gate(x):
                pe.wait_ge(gm_lo, 1)
                pe.wait_ge(bias_lo, 1)
                pe.wait_ge(am_hi_r, x[0])
                pe.wait_ge(am_lo_r, x[0])
                for t in range(NT):
                    w = wcols("mem_t", 0, 2 * D)
                    product(ps[:, X0 + t, :], am_hi[:, t, :], am_lo[:, t, :], w_hi[:, w], w_lo[:, w], True, False)
                    z = ps[:, X0 + t, D:2 * D]
                    for k in range(KD):
                        w = wcols("gate_x", k * D, D)
                        product(z, of_tile(xc_hi[:, k, :], t), of_tile(xc_lo[:, k, :], t), w_hi[:, w], w_lo[:, w])
                    pe.matmul(z, ones_r[one, :], b_hi, start=False, stop=False, skip_group_check=True)
                    last = pe.matmul(z, ones_r[one, :], b_lo, start=False, stop=True, skip_group_check=True)
                last.then_inc(mcz_mm, 1)

            def x1_t(x):
                pe.wait_ge(x1_r, x[0])
                transposes(X0, x_res).then_inc(tx1_mm, 1)

            def unit(x, u):
                t, n = UNITS[u]
                if u == 0:
                    pe.wait_ge(raw_lo, 3)
                    pe.wait_ge(x1_hi, x[0])
                    pe.wait_ge(x1_lo, x[0])
                if u >= 2:
                    pe.wait_ge(qkv_r, unit_count(x, u - 1))
                for k in range(KD):
                    w = wcols("qkv", k * 6 * D + n * 2 * D, 2 * D)
                    last = product(ps[:, (X1, X0)[u % 2], :], of_tile(ta_hi[:, k, :], t), of_tile(ta_lo[:, k, :], t),
                                   w_hi[:, w], w_lo[:, w], k == 0, k == KD - 1)
                last.then_inc(unit_mm, 1)

            def qk_t(x):
                pe.wait_ge(qkv_r, unit_count(x, len(UNITS)))
                pe.wait_ge(rope_r, tile_count(x, NT - 1))
                transposes(X0, qkv[:, :, 0:D]).then_inc(tq_mm, 1)
                transposes(X1, qkv[:, :, D:2 * D]).then_inc(tk_mm, 1)

            def ctx_kv(x):
                pe.wait_ge(qt_r, x[0])
                w = wcols("ckv", 0, C)
                product(ps[:, X0, 0:TOK], w_hi[:, w], w_lo[:, w], xc_hi[:, KD, :], xc_lo[:, KD, :], True, True)
                w = wcols("ckv", C, C)
                for t in range(NT):
                    last = product(ps[:, X0, TOK + t * P:TOK + (t + 1) * P], of_tile(xc_hi[:, KD, :], t),
                                   of_tile(xc_lo[:, KD, :], t), w_hi[:, w], w_lo[:, w], True, True)
                last.then_inc(kv_mm, 1)

            def mask(y, c):
                if c == 0:
                    pe.wait_ge(mask_set, 1)
                    before(pe, ctx_r[1], y[1] * NT)
                else:
                    before(pe, mi_lo, y[1])
                for j in (2 * c, 2 * c + 1):
                    pe.matmul(ps[:, j, :], ident_r[:, :], causal_r[:, :].unsqueeze(1).to_broadcast([P, 8, S]),
                              start=True, stop=False, skip_group_check=True)

            def scores(y, c):
                if c == 0:
                    pe.wait_ge(qt_r, y[0])
                    pe.wait_ge(kb_r, y[0])
                kb = kblk[:, :, :].rearrange("p (m e) c -> p m e c", e=2)
                for m in range(2):
                    for t in range(NT):
                        for j in (2 * c, 2 * c + 1):
                            for b in range(2):
                                r, tk = slice(32 * j, 32 * j + 32), slice(t * P + b * S, t * P + (b + 1) * S)
                                last = pe.matmul(ps[64 * b:64 * b + 64, j, (2 * m + t) * P:(2 * m + t + 1) * P],
                                                 q_t[r, m, tk], kb[r, m, :, tk],
                                                 start=False, stop=True, skip_group_check=True)
                last.then_inc(s_mm[0][c], 1)

            def cross_scores(y, c):
                if c == 0:
                    pe.wait_ge(cq_r, y[0])
                    pe.wait_ge(ckb_r, y[0])
                for t in range(NT):
                    for j in (2 * c, 2 * c + 1):
                        for b in range(2):
                            r, tk = slice(32 * j, 32 * j + 32), slice(t * P + b * S, t * P + (b + 1) * S)
                            last = single(ps[64 * b:64 * b + 64, j, t * 2 * P:(t + 1) * 2 * P],
                                          tok[r, 0, tk], kblk[r, :, tk])
                last.then_inc(s_mm[1][c], 1)

            def probs_t(y, k, j):
                pe.wait_ge(exp_r[k], bank_count(y, j))
                for n in range(4):
                    last = pe.transpose(ps[:, j, n * P:(n + 1) * P], sm[:, j, n * P:(n + 1) * P], ident[:, :])
                last.then_inc(pt_mm[k], 1)

            def values(y, k, t):
                if t == 0:
                    pe.wait_ge(vb_r if k == 0 else kv_r, y[0])
                    pe.wait_ge(pt_r[k], bank_count(y, 3))
                blocks, width = ((vblk, VB), (cvblk, CVB))[k]
                for h in range(PAIRS):
                    j, n = (h % 4, 2 * (h // 4) + t) if k == 0 else (h // 2, 2 * t + h % 2)
                    for b in range(2):
                        last = single(ps[64 * b:64 * b + 64, t, h * width:(h + 1) * width],
                                      sm[:, j, n * P + b * S:n * P + (b + 1) * S], blocks[:, t, b, h, :])
                last.then_inc(pv_mm[k], 1)

            def context_t(y):
                pe.wait_ge(ctx_r[0], tile_count(y, NT - 1))
                transposes(3, tok).then_inc(tctx_mm[0], 1)

            def dense(y, t):
                pe.wait_ge(raw_lo, 4)
                pe.wait_ge(ctx_hi[0], y[0])
                pe.wait_ge(ctx_lo[0], y[0])
                for k in range(KD):
                    w = wcols("dense", k * 2 * D, 2 * D)
                    last = product(ps[:, t, :], of_tile(ta_hi[:, k, :], t), of_tile(ta_lo[:, k, :], t),
                                   w_hi[:, w], w_lo[:, w], k == 0, k == KD - 1)
                last.then_inc(dense_mm, 1)

            def cross_input_t(y):
                pe.wait_ge(x2_r, y[0])
                transposes(2, res).then_inc(tci_mm, 1)

            def cross_q(y):
                pe.wait_ge(ci_hi, y[0])
                pe.wait_ge(ci_lo, y[0])
                for k in range(KD):
                    w = wcols("cq", k * C, C)
                    last = product(ps[:, 3, 0:TOK], w_hi[:, w], w_lo[:, w], tb_hi[:, k, :], tb_lo[:, k, :],
                                   k == 0, k == KD - 1)
                last.then_inc(cq_mm, 1)

            def cross_context_t(y):
                pe.wait_ge(ctx_r[1], tile_count(y, NT - 1))
                transposes(2, tok[:, :, 0:C]).then_inc(tctx_mm[1], 1)

            def cross_dense(y):
                pe.wait_ge(ctx_hi[1], y[0])
                pe.wait_ge(ctx_lo[1], y[0])
                w = wcols("cdense", 0, D)
                for t in range(NT):
                    last = product(ps[:, 3, t * D:(t + 1) * D], of_tile(tb_hi[:, 0, :], t), of_tile(tb_lo[:, 0, :], t),
                                   w_hi[:, w], w_lo[:, w], True, True)
                last.then_inc(cd_mm, 1)

            def mlp_input_t(y):
                pe.wait_ge(mi_r, y[0])
                transposes(2, tok).then_inc(tmi_mm, 1)

            def gate_up(m, lo, hi):
                if lo == 0:
                    pe.wait_ge(raw_lo, 6)
                    pe.wait_ge(mi_hi, m[0])
                    pe.wait_ge(mi_lo, m[0])
                for n in range(lo, hi):
                    width = P if n < 2 * FULL else 2 * LEFT
                    if n < 2:
                        pe.wait_ge(y_r, m[1] + 1)
                    else:
                        pe.wait_ge(h_r, m[2] + (n - 1))
                    for u in range(2):
                        for k in range(KD):
                            w = wcols("gu", k * GU + n * 2 * P + u * width, width)
                            last = product(ps[0:width, M0 + n % 2, u * TOK:(u + 1) * TOK], w_hi[:, w], w_lo[:, w],
                                           tc_hi[:, k, :], tc_lo[:, k, :], k == 0, k == KD - 1)
                    last.then_inc(gu_mm, 1)

            def down(m, t, lo, hi):
                if lo == 0 and t == 0:
                    pe.wait_ge(raw_lo, len(chunks))
                    pe.wait_ge(h_r, m[2] + MT)
                for n in range(lo, hi):
                    if t == 0:
                        pe.wait_ge(h_lo_r, m[2] + (n + 1))
                    if n < 2 * FULL:
                        r, e = slice(0, P), n // FULL
                        w, to = wcols("down", n * D, D), slice(e * D, (e + 1) * D)
                    else:
                        r, w, to = slice(0, 2 * LEFT), wcols("down_left", 0, 2 * D), slice(0, 2 * D)
                    last = product(ps[:, M0 + t, to], of_tile(h_hi[r, n, :], t), of_tile(h_lo[r, n, :], t),
                                   w_hi[r, w], w_lo[r, w], n == 0, n == MT - 1)
                if hi == MT:
                    last.then_inc(down_mm, 1)

            def turn(x, y, m):
                if m is not None:
                    gate_up(m, 0, 1)
                if y is not None:
                    mask(y, 1)
                    scores(y, 1)
                if m is not None:
                    gate_up(m, 1, 3)
                if x is not None:
                    q0_product(x)
                if y is not None:
                    probs_t(y, 0, 0)
                    probs_t(y, 0, 1)
                    probs_t(y, 0, 2)
                    probs_t(y, 0, 3)
                if x is not None:
                    scores0(x)
                if m is not None:
                    gate_up(m, 3, 4)
                if y is not None:
                    values(y, 0, 0)
                    values(y, 0, 1)
                if x is not None:
                    probs0_t(x)
                if m is not None:
                    gate_up(m, 4, 5)
                if y is not None:
                    context_t(y)
                if x is not None:
                    attend0(x)
                if m is not None:
                    gate_up(m, 5, 6)
                if y is not None:
                    dense(y, 0)
                    dense(y, 1)
                if m is not None:
                    gate_up(m, 6, 7)
                if y is not None:
                    cross_input_t(y)
                if m is not None:
                    gate_up(m, 7, 8)
                if x is not None:
                    context_gate(x)
                if y is not None:
                    cross_q(y)
                if m is not None:
                    gate_up(m, 8, 9)
                if y is not None:
                    cross_scores(y, 0)
                if m is not None:
                    gate_up(m, 9, MT)
                if y is not None:
                    cross_scores(y, 1)
                if m is not None:
                    down(m, 0, 0, 9)
                if y is not None:
                    probs_t(y, 1, 0)
                if x is not None:
                    x1_t(x)
                if y is not None:
                    probs_t(y, 1, 1)
                    probs_t(y, 1, 2)
                if m is not None:
                    down(m, 0, 9, MT)
                if x is not None:
                    unit(x, 0)
                if y is not None:
                    probs_t(y, 1, 3)
                if x is not None:
                    unit(x, 1)
                if y is not None:
                    values(y, 1, 0)
                    values(y, 1, 1)
                if x is not None:
                    unit(x, 2)
                if y is not None:
                    cross_context_t(y)
                if x is not None:
                    unit(x, 3)
                if m is not None:
                    down(m, 1, 0, 3)
                if y is not None:
                    cross_dense(y)
                if x is not None:
                    unit(x, 4)
                    unit(x, 5)
                if m is not None:
                    down(m, 1, 3, 9)
                if x is not None:
                    qk_t(x)
                if m is not None:
                    down(m, 1, 9, MT)
                if y is not None:
                    mlp_input_t(y)
                if x is not None:
                    mask(x, 0)
                    scores(x, 0)
                    ctx_kv(x)

            pe.wait_ge(consts_in, 16 * 8)
            pe.wait_ge(pos_done, 5)
            pe.matmul(ps[:, 6, 0:2 * HD], onehot[:, :, :], trig_tab[:, :], start=True, stop=True).then_inc(trig_mm, 1)
            pe.wait_ge(raw_in[0], 16)
            for k in range(KD):
                last = pe.matmul(ps[:, 7, 0:D], raw_mem[:, k * C:(k + 1) * C], raw_gate_m[:, k * D:(k + 1) * D],
                                 start=(k == 0), stop=(k == KD - 1))
            last.then_inc(gm_mm, 1)
            pe.wait_ge(raw_lo, 1)
            turn(counts(0), None, None)
            turn(counts(1), counts(0), None)
            with pe.Fori(1, GROUPS - 1) as i:
                base = pe.snap((i - 1) * MT)
                turn((i + 2, i + 1), (i + 1, i), (i, i - 1, base))
            turn(None, counts(GROUPS - 1), (*counts(GROUPS - 2), (GROUPS - 2) * MT))
            turn(None, None, (*counts(GROUPS - 1), (GROUPS - 1) * MT))


def kernel(**inputs):
    import numpy as np
    import concourse.bacc as bacc
    from concourse.bass_utils import run_bass_kernel_spmd as run

    v = {n: np.ascontiguousarray(x) for n, x in inputs.items()}

    def by_k(w):
        return w.reshape(-1, P, w.shape[1]).transpose(1, 0, 2).reshape(P, -1)

    x, cx = v["x"].reshape(GROUPS, TOK, D), v["ctx_1024"].reshape(GROUPS, TOK, C)
    x_t = x.transpose(0, 2, 1).reshape(GROUPS, KD, P, TOK).transpose(0, 2, 1, 3)
    xc = np.concatenate([x_t, cx.transpose(0, 2, 1)[:, :, None, :]], axis=2)
    x_tok = x.reshape(GROUPS, NT, P, D).transpose(0, 2, 1, 3)
    ctx_tok = cx.reshape(GROUPS, NT, 2, S, C).transpose(0, 1, 3, 2, 4).reshape(GROUPS, P, 2, C)
    types = v["mask_BxS_ik0"].reshape(-1)
    mask = np.stack([types, np.roll(types, -1)]).reshape(2, GROUPS, NT, P).transpose(1, 3, 0, 2)
    wm, wg = v["L0_xattn_W_mem"], v["L0_xattn_W_gate"].T
    w_first = np.concatenate([by_k(wm), by_k(wg[:D]), wm.T, v["L1_xattn_ckv_w"], by_k(v["L1_xattn_cq_w"]),
                              by_k(wg[D:])], axis=1)
    w_qkv = np.concatenate([v[f"L1_xattn_{e}_qkv"][:, n * D:(n + 1) * D] for n in range(3) for e in "vl"],
                           axis=1).reshape(KD, P, 6 * D)
    w_dense = np.concatenate([by_k(np.concatenate([v["L1_xattn_v_dense"], v["L1_xattn_l_dense"]], axis=1)),
                              v["L1_xattn_cdense_w"]], axis=1)
    gates, ups = ([v[f"L1_xattn_{e}_{n}"] for e in "vl"] for n in ("gate", "up"))
    cols, cut = [], FULL * P
    for e in range(2):
        for n in range(FULL):
            cols += [w[e][:, n * P:(n + 1) * P] for w in (gates, ups)]
    cols += [w[e][:, cut:] for w in (gates, ups) for e in range(2)]
    w_gu = np.concatenate(cols, axis=1).reshape(KD, P, GU)
    downs = [v["L1_xattn_v_down"], v["L1_xattn_l_down"]]
    w_down = by_k(np.concatenate([w[:cut] for w in downs], axis=0))
    w_down_left = np.zeros((2 * LEFT, 2 * D), np.float32)
    for e in range(2):
        w_down_left[e * LEFT:(e + 1) * LEFT, e * D:(e + 1) * D] = downs[e][cut:]
    ln = np.stack([v[f"L1_xattn_ln_{n}_w"].reshape(KD, P).T for n in ("in", "post_cross", "post_attn")], axis=1)
    p = np.arange(P)
    consts = np.zeros((P, 8), np.float32)
    for e in range(2):
        consts[:, e] = p // HD % 2 == e
    for m in range(4):
        consts[:, 2 + m] = p // CHD % 4 == m
    consts[:, 6] = p % S != S - 1
    consts[:, 7] = p
    causal = np.where(np.arange(S)[None, :] <= (p % S)[:, None], 0.0, MASKED).astype(np.float32)
    inv_freq = (1.0 / np.float32(10000.0) ** (np.arange(0, HD, 2, dtype=np.float32) / np.float32(HD))).astype(np.float32)
    angle = np.outer(np.arange(S, dtype=np.float32), inv_freq).astype(np.float32)
    cos, sin = np.cos(angle), np.sin(angle)
    trig_tab = np.concatenate([cos, cos, -sin, sin], axis=1).astype(np.float32)

    arrays = {
        "xc": xc, "x_tok": x_tok, "ctx_tok": ctx_tok, "mask": mask, "w_first": w_first, "w_qkv": w_qkv,
        "w_dense": w_dense, "w_gu": w_gu, "w_down": w_down, "w_down_left": w_down_left, "ln": ln,
        "ident": np.eye(P, dtype=np.float32), "consts": consts, "causal": causal, "trig_tab": trig_tab,
        "b_gate": v["L0_xattn_b_gate"].reshape(1, D), "norm0": v["L0_xattn_norm_w"], "pos": v["pos_1xS"].reshape(S),
    }
    arrays = {n: np.ascontiguousarray(x) for n, x in arrays.items()}
    nc = bacc.Bacc("TRN2", target_bir_lowering=False, num_devices=1)
    a = {n: nc.dram_tensor(f"in_{n}", x.shape, mybir.dt.from_np(x.dtype), kind="ExternalInput").ap()
         for n, x in arrays.items()}
    out = nc.dram_tensor("out_y", (GROUPS, P, NT, D), F32, kind="ExternalOutput").ap()
    build_program(nc, a, out)
    r = run(nc, [{f"in_{n}": x for n, x in arrays.items()}], core_ids=[0])
    y = r.results[0]["out_y"]
    return y.transpose(0, 2, 1, 3).reshape(B, S, D)
```
